# Optimizing a Trainium2 kernel written in Bass

```python
import numpy as np
import jax
import jax.numpy as jnp

def _softmax(x, axis=-1):
    return jax.nn.softmax(x, axis=axis)

def _gelu(x):
    return jax.nn.gelu(x, approximate=True)

def _silu(x):
    return jax.nn.silu(x)

def _sigmoid(x):
    return jax.nn.sigmoid(x)

def _layernorm(x, axis=-1, eps=1e-05):
    m = jnp.mean(x, axis=axis, keepdims=True)
    v = jnp.var(x, axis=axis, keepdims=True)
    return (x - m) / jnp.sqrt(v + eps)

def _scatter_add(tgt, idx, src, axis=0):
    return tgt.at[idx].add(src)

def _segment_sum(src, seg, n):
    return jax.ops.segment_sum(src, seg, n)
kernel_name = 'mk_cond_seq_d4_seqx_r2_0033f5'

def setup_inputs(seed: int=0):
    np.random.seed(seed)
    _w = jnp.asarray

    def _rec_inputs():
        import jax
        import jax.numpy as jnp
        _rk = jax.random.key(seed)
        x = 7.22e-05 + 1 * jax.random.normal(jax.random.fold_in(_rk, 1), (4, 1024, 512), jnp.float32)
        _lenS = 1024 - jax.random.randint(jax.random.fold_in(_rk, 7), (4,), 0, max(1, 1024 // 4) + 1, jnp.int32)
        _lenS2 = 1024 - jax.random.randint(jax.random.fold_in(_rk, 8), (4,), 0, max(1, 1024 // 4) + 1, jnp.int32)
        cond_2048 = 0.00386106 + 1.00199 * jax.random.normal(jax.random.fold_in(_rk, 11), (4, 1024), jnp.float32)
        itok_S_0_1023 = jax.random.randint(jax.random.fold_in(_rk, 14), (1024,), 0, 512, jnp.int32)
        _validS = jnp.arange(1024)[None, :] < _lenS[:, None]
        _validS2 = jnp.arange(1024)[None, :] < _lenS2[:, None]
        _causal = jnp.tril(jnp.ones((1024, 1024), dtype=bool))
        mask_BxS_ff1 = jnp.where(jnp.ones((4, 1024), dtype=bool), 1.0, 0.0).astype(jnp.float32)
        mask_BxS_ik0 = jnp.where(jnp.broadcast_to(_validS[:, :], (4, 1024)), 0, 1).astype(jnp.int32)
        return (x, cond_2048, itok_S_0_1023, mask_BxS_ff1, mask_BxS_ik0)
    x, cond_2048, itok_S_0_1023, mask_BxS_ff1, mask_BxS_ik0 = _rec_inputs()

    def _L0_cond_setup():
        import jax, jax.numpy as jnp
        import numpy as np
        B, T, D, H, TE = (8, 512, 512, 16, 1024)
        LN_EPS = 1e-05

        def layer_norm(x, w, b):
            m = jnp.mean(x, axis=-1, keepdims=True)
            v = jnp.var(x, axis=-1, keepdims=True)
            return (x - m) / jnp.sqrt(v + LN_EPS) * w + b
        key = jax.random.key(seed)
        ks = jax.random.split(key, 8)
        s = lambda k, sh: jax.random.normal(k, sh, jnp.float32) * 0.02
        return dict(x=jax.random.normal(ks[0], (B, T, D), jnp.float32), emb=jax.random.normal(ks[1], (B, TE), jnp.float32), src_mask=jnp.ones((B, T), jnp.float32), norm_w=jnp.ones((D,), jnp.float32), norm_b=jnp.zeros((D,), jnp.float32), q_w=s(ks[2], (D, D)), q_b=jnp.zeros((D,), jnp.float32), k_w=s(ks[3], (D, D)), k_b=jnp.zeros((D,), jnp.float32), v_w=s(ks[4], (D, D)), v_b=jnp.zeros((D,), jnp.float32), emb_w=s(ks[5], (TE, 2 * D)), emb_b=jnp.zeros((2 * D,), jnp.float32), sb_norm_w=jnp.ones((D,), jnp.float32), sb_norm_b=jnp.zeros((D,), jnp.float32), out_w=s(ks[6], (D, D)), out_b=jnp.zeros((D,), jnp.float32))
    _L0_cond_all = _L0_cond_setup()
    _L0_cond_in = {k: v for k, v in _L0_cond_all.items() if k in ('norm_w', 'norm_b', 'q_w', 'q_b', 'k_w', 'k_b', 'v_w', 'v_b', 'emb_w', 'emb_b', 'sb_norm_w', 'sb_norm_b', 'out_w', 'out_b')}
    del _L0_cond_all

    def _L1_cond_setup():
        import jax, jax.numpy as jnp
        import numpy as np
        H = 16
        LN_EPS = 1e-05

        def _layernorm(x, scale, bias):
            mu = jnp.mean(x, axis=-1, keepdims=True)
            var = jnp.var(x, axis=-1, keepdims=True)
            return (x - mu) * jax.lax.rsqrt(var + LN_EPS) * scale + bias
        key = jax.random.key(seed)
        ks = jax.random.split(key, 8)
        B, T, D, E = (4, 2048, 512, 1024)
        s = 0.02
        return {'x': jax.random.normal(ks[0], (B, T, D), jnp.float32), 'emb': jax.random.normal(ks[1], (B, E), jnp.float32), 'src_mask': jax.random.randint(ks[2], (B, T), 0, 2).astype(jnp.int32), 'norm_scale': jnp.ones((D,), jnp.float32), 'norm_bias': jnp.zeros((D,), jnp.float32), 'Wq': jax.random.normal(ks[3], (D, D), jnp.float32) * s, 'bq': jnp.zeros((D,), jnp.float32), 'Wk': jax.random.normal(ks[4], (D, D), jnp.float32) * s, 'bk': jnp.zeros((D,), jnp.float32), 'Wv': jax.random.normal(ks[5], (D, D), jnp.float32) * s, 'bv': jnp.zeros((D,), jnp.float32), 'film_emb_W': jax.random.normal(ks[6], (E, 2 * D), jnp.float32) * s, 'film_emb_b': jnp.zeros((2 * D,), jnp.float32), 'film_norm_scale': jnp.ones((D,), jnp.float32), 'film_norm_bias': jnp.zeros((D,), jnp.float32), 'film_out_W': jax.random.normal(ks[7], (D, D), jnp.float32) * s, 'film_out_b': jnp.zeros((D,), jnp.float32)}
    _L1_cond_all = _L1_cond_setup()
    _L1_cond_in = {k: v for k, v in _L1_cond_all.items() if k in ('norm_scale', 'norm_bias', 'Wq', 'bq', 'Wk', 'bk', 'Wv', 'bv', 'film_emb_W', 'film_emb_b', 'film_norm_scale', 'film_norm_bias', 'film_out_W', 'film_out_b')}
    del _L1_cond_all

    def _L2_cond_setup():
        import jax, jax.numpy as jnp
        import numpy as np
        D = 512
        DI = 1024
        N = 16
        DT_RANK = 64
        D_CONV = 4
        EPS = 1e-05

        def _layernorm(x, g, b):
            mu = jnp.mean(x, axis=-1, keepdims=True)
            var = jnp.mean((x - mu) ** 2, axis=-1, keepdims=True)
            return (x - mu) * jax.lax.rsqrt(var + EPS) * g + b

        def _mamba(xn, in_proj_w, conv_w, conv_b, x_proj_w, dt_proj_w, dt_proj_b, A_log, D_param, out_proj_w):
            b, sl, _ = xn.shape
            xz = jnp.einsum('bsd,ed->bse', xn, in_proj_w)
            x_in, z = jnp.split(xz, 2, axis=-1)
            xt = jnp.transpose(x_in, (0, 2, 1))
            u = jax.lax.conv_general_dilated(xt, conv_w[:, None, :], (1,), [(D_CONV - 1, 0)], feature_group_count=DI, dimension_numbers=('NCH', 'OIH', 'NCH')) + conv_b[None, :, None]
            u = jax.nn.silu(jnp.transpose(u, (0, 2, 1)))
            x_dbl = jnp.einsum('bsd,ed->bse', u, x_proj_w)
            dt_r, B, C = jnp.split(x_dbl, [DT_RANK, DT_RANK + N], axis=-1)
            dt = jax.nn.softplus(jnp.einsum('bsr,dr->bsd', dt_r, dt_proj_w) + dt_proj_b)
            A = -jnp.exp(A_log)

            def step(h, inp):
                dt_t, B_t, C_t, u_t = inp
                dA = jnp.exp(dt_t[:, :, None] * A)
                h = h * dA + (dt_t * u_t)[:, :, None] * B_t[:, None, :]
                y = jnp.einsum('bdn,bn->bd', h, C_t)
                return (h, y)
            seq = (jnp.transpose(dt, (1, 0, 2)), jnp.transpose(B, (1, 0, 2)), jnp.transpose(C, (1, 0, 2)), jnp.transpose(u, (1, 0, 2)))
            h0 = jnp.zeros((b, DI, N), xn.dtype)
            _, ys = jax.lax.scan(step, h0, seq)
            y = jnp.transpose(ys, (1, 0, 2)) + u * D_param
            y = y * jax.nn.silu(z)
            return jnp.einsum('bsd,ed->bse', y, out_proj_w)
        key = jax.random.key(seed)
        ks = jax.random.split(key, 16)
        s = lambda fan: 1.0 / np.sqrt(fan)
        inp = {'x': jax.random.normal(ks[0], (2, 1024, D), jnp.float32), 'c': jax.random.normal(ks[1], (2, 2 * D), jnp.float32), 'ln_g': jnp.ones((D,), jnp.float32), 'ln_b': jnp.zeros((D,), jnp.float32), 'ada_w': jax.random.normal(ks[2], (3 * D, 2 * D), jnp.float32) * s(2 * D), 'ada_b': jnp.zeros((3 * D,), jnp.float32), 'in_proj_w': jax.random.normal(ks[3], (2 * DI, D), jnp.float32) * s(D), 'conv_w': jax.random.normal(ks[4], (DI, D_CONV), jnp.float32) * s(D_CONV), 'conv_b': jnp.zeros((DI,), jnp.float32), 'x_proj_w': jax.random.normal(ks[5], (DT_RANK + 2 * N, DI), jnp.float32) * s(DI), 'dt_proj_w': jax.random.normal(ks[6], (DI, DT_RANK), jnp.float32) * s(DT_RANK), 'dt_proj_b': jax.random.uniform(ks[7], (DI,), jnp.float32, -4.0, -2.0), 'A_log': jnp.tile(jnp.log(jnp.arange(1, N + 1, dtype=jnp.float32)), (DI, 1)), 'D_param': jnp.ones((DI,), jnp.float32), 'out_proj_w': jax.random.normal(ks[8], (D, DI), jnp.float32) * s(DI)}
        return inp
    _L2_cond_all = _L2_cond_setup()
    _L2_cond_in = {k: v for k, v in _L2_cond_all.items() if k in ('ln_g', 'ln_b', 'ada_w', 'ada_b', 'in_proj_w', 'conv_w', 'conv_b', 'x_proj_w', 'dt_proj_w', 'dt_proj_b', 'A_log', 'D_param', 'out_proj_w')}
    del _L2_cond_all

    def _L3_cond_setup():
        import jax, jax.numpy as jnp
        import numpy as np
        B_SZ, S, D = (4, 512, 512)
        DI, DS, DTR, DC = (1024, 16, 64, 4)
        EPS = 1e-05

        def _layernorm(x, g, b):
            m = jnp.mean(x, axis=-1, keepdims=True)
            v = jnp.var(x, axis=-1, keepdims=True)
            return (x - m) * jax.lax.rsqrt(v + EPS) * g + b

        def _mamba(h, W_in, conv_w, conv_b, W_xp, W_dt, b_dt, A_log, D_param, W_out):
            bsz = h.shape[0]
            xz = h @ W_in
            xm, z = jnp.split(xz, 2, axis=-1)
            xc = jnp.transpose(xm, (0, 2, 1))
            xc = jax.lax.conv_general_dilated(xc, conv_w, (1,), [(DC - 1, 0)], feature_group_count=DI, dimension_numbers=('NCH', 'OIH', 'NCH'))
            xc = xc + conv_b[None, :, None]
            xm = jax.nn.silu(jnp.transpose(xc, (0, 2, 1)))
            xdbl = xm @ W_xp
            dtr, Bm, Cm = jnp.split(xdbl, [DTR, DTR + DS], axis=-1)
            dt = jax.nn.softplus(dtr @ W_dt + b_dt)
            A = -jnp.exp(A_log)

            def step(hst, inp):
                dt_t, B_t, C_t, x_t = inp
                dA = jnp.exp(dt_t[:, :, None] * A)
                hst = hst * dA + (dt_t * x_t)[:, :, None] * B_t[:, None, :]
                y = jnp.einsum('bds,bs->bd', hst, C_t)
                return (hst, y)
            inputs = (jnp.transpose(dt, (1, 0, 2)), jnp.transpose(Bm, (1, 0, 2)), jnp.transpose(Cm, (1, 0, 2)), jnp.transpose(xm, (1, 0, 2)))
            h0 = jnp.zeros((bsz, DI, DS), dt.dtype)
            _, ys = jax.lax.scan(step, h0, inputs)
            y = jnp.transpose(ys, (1, 0, 2)) + xm * D_param
            y = y * jax.nn.silu(z)
            return y @ W_out
        key = jax.random.key(seed)
        ks = jax.random.split(key, 12)

        def w(k, shape, scale=0.02):
            return jax.random.normal(k, shape, jnp.float32) * scale
        x = jax.random.normal(ks[0], (B_SZ, S, D), jnp.float32)
        c = jax.random.normal(ks[1], (B_SZ, 2 * D), jnp.float32)
        W_ada = w(ks[2], (2 * D, 3 * D))
        b_ada = jnp.zeros((3 * D,), jnp.float32)
        gamma = jnp.ones((D,), jnp.float32)
        beta = jnp.zeros((D,), jnp.float32)
        W_in = w(ks[3], (D, 2 * DI))
        conv_w = w(ks[4], (DI, 1, DC), 0.1)
        conv_b = jnp.zeros((DI,), jnp.float32)
        W_xp = w(ks[5], (DI, DTR + 2 * DS))
        W_dt = w(ks[6], (DTR, DI))
        b_dt = jnp.full((DI,), jnp.log(jnp.expm1(jnp.float32(0.01))), jnp.float32)
        A_log = jnp.log(jnp.broadcast_to(jnp.arange(1, DS + 1, dtype=jnp.float32), (DI, DS)))
        D_param = jnp.ones((DI,), jnp.float32)
        W_out = w(ks[7], (DI, D))
        perm = jax.random.permutation(ks[8], S)
        inv_perm = jnp.argsort(perm)
        return dict(x=x, c=c, W_ada=W_ada, b_ada=b_ada, gamma=gamma, beta=beta, W_in=W_in, conv_w=conv_w, conv_b=conv_b, W_xp=W_xp, W_dt=W_dt, b_dt=b_dt, A_log=A_log, D_param=D_param, W_out=W_out, perm=perm, inv_perm=inv_perm)
    _L3_cond_all = _L3_cond_setup()
    _L3_cond_in = {k: v for k, v in _L3_cond_all.items() if k in ('W_ada', 'b_ada', 'gamma', 'beta', 'W_in', 'conv_w', 'conv_b', 'W_xp', 'W_dt', 'b_dt', 'A_log', 'D_param', 'W_out')}
    del _L3_cond_all
    return {'x': x, 'cond_2048': cond_2048, 'itok_S_0_1023': itok_S_0_1023, 'mask_BxS_ff1': mask_BxS_ff1, 'mask_BxS_ik0': mask_BxS_ik0, 'L0_cond_norm_w': _L0_cond_in['norm_w'], 'L0_cond_norm_b': _L0_cond_in['norm_b'], 'L0_cond_q_w': _L0_cond_in['q_w'], 'L0_cond_q_b': _L0_cond_in['q_b'], 'L0_cond_k_w': _L0_cond_in['k_w'], 'L0_cond_k_b': _L0_cond_in['k_b'], 'L0_cond_v_w': _L0_cond_in['v_w'], 'L0_cond_v_b': _L0_cond_in['v_b'], 'L0_cond_emb_w': _L0_cond_in['emb_w'], 'L0_cond_emb_b': _L0_cond_in['emb_b'], 'L0_cond_sb_norm_w': _L0_cond_in['sb_norm_w'], 'L0_cond_sb_norm_b': _L0_cond_in['sb_norm_b'], 'L0_cond_out_w': _L0_cond_in['out_w'], 'L0_cond_out_b': _L0_cond_in['out_b'], 'L1_cond_norm_scale': _L1_cond_in['norm_scale'], 'L1_cond_norm_bias': _L1_cond_in['norm_bias'], 'L1_cond_Wq': _L1_cond_in['Wq'], 'L1_cond_bq': _L1_cond_in['bq'], 'L1_cond_Wk': _L1_cond_in['Wk'], 'L1_cond_bk': _L1_cond_in['bk'], 'L1_cond_Wv': _L1_cond_in['Wv'], 'L1_cond_bv': _L1_cond_in['bv'], 'L1_cond_film_emb_W': _L1_cond_in['film_emb_W'], 'L1_cond_film_emb_b': _L1_cond_in['film_emb_b'], 'L1_cond_film_norm_scale': _L1_cond_in['film_norm_scale'], 'L1_cond_film_norm_bias': _L1_cond_in['film_norm_bias'], 'L1_cond_film_out_W': _L1_cond_in['film_out_W'], 'L1_cond_film_out_b': _L1_cond_in['film_out_b'], 'L2_cond_ln_g': _L2_cond_in['ln_g'], 'L2_cond_ln_b': _L2_cond_in['ln_b'], 'L2_cond_ada_w': _L2_cond_in['ada_w'], 'L2_cond_ada_b': _L2_cond_in['ada_b'], 'L2_cond_in_proj_w': _L2_cond_in['in_proj_w'], 'L2_cond_conv_w': _L2_cond_in['conv_w'], 'L2_cond_conv_b': _L2_cond_in['conv_b'], 'L2_cond_x_proj_w': _L2_cond_in['x_proj_w'], 'L2_cond_dt_proj_w': _L2_cond_in['dt_proj_w'], 'L2_cond_dt_proj_b': _L2_cond_in['dt_proj_b'], 'L2_cond_A_log': _L2_cond_in['A_log'], 'L2_cond_D_param': _L2_cond_in['D_param'], 'L2_cond_out_proj_w': _L2_cond_in['out_proj_w'], 'L3_cond_W_ada': _L3_cond_in['W_ada'], 'L3_cond_b_ada': _L3_cond_in['b_ada'], 'L3_cond_gamma': _L3_cond_in['gamma'], 'L3_cond_beta': _L3_cond_in['beta'], 'L3_cond_W_in': _L3_cond_in['W_in'], 'L3_cond_conv_w': _L3_cond_in['conv_w'], 'L3_cond_conv_b': _L3_cond_in['conv_b'], 'L3_cond_W_xp': _L3_cond_in['W_xp'], 'L3_cond_W_dt': _L3_cond_in['W_dt'], 'L3_cond_b_dt': _L3_cond_in['b_dt'], 'L3_cond_A_log': _L3_cond_in['A_log'], 'L3_cond_D_param': _L3_cond_in['D_param'], 'L3_cond_W_out': _L3_cond_in['W_out']}

def reference(x, cond_2048, itok_S_0_1023, mask_BxS_ff1, mask_BxS_ik0, L0_cond_norm_w, L0_cond_norm_b, L0_cond_q_w, L0_cond_q_b, L0_cond_k_w, L0_cond_k_b, L0_cond_v_w, L0_cond_v_b, L0_cond_emb_w, L0_cond_emb_b, L0_cond_sb_norm_w, L0_cond_sb_norm_b, L0_cond_out_w, L0_cond_out_b, L1_cond_norm_scale, L1_cond_norm_bias, L1_cond_Wq, L1_cond_bq, L1_cond_Wk, L1_cond_bk, L1_cond_Wv, L1_cond_bv, L1_cond_film_emb_W, L1_cond_film_emb_b, L1_cond_film_norm_scale, L1_cond_film_norm_bias, L1_cond_film_out_W, L1_cond_film_out_b, L2_cond_ln_g, L2_cond_ln_b, L2_cond_ada_w, L2_cond_ada_b, L2_cond_in_proj_w, L2_cond_conv_w, L2_cond_conv_b, L2_cond_x_proj_w, L2_cond_dt_proj_w, L2_cond_dt_proj_b, L2_cond_A_log, L2_cond_D_param, L2_cond_out_proj_w, L3_cond_W_ada, L3_cond_b_ada, L3_cond_gamma, L3_cond_beta, L3_cond_W_in, L3_cond_conv_w, L3_cond_conv_b, L3_cond_W_xp, L3_cond_W_dt, L3_cond_b_dt, L3_cond_A_log, L3_cond_D_param, L3_cond_W_out):
    import jax
    import jax.numpy as jnp

    def _L0_cond_ref(x, emb, src_mask, norm_w, norm_b, q_w, q_b, k_w, k_b, v_w, v_b, emb_w, emb_b, sb_norm_w, sb_norm_b, out_w, out_b):
        import jax, jax.numpy as jnp
        import numpy as np
        B, T, D, H, TE = (8, 512, 512, 16, 1024)
        LN_EPS = 1e-05

        def layer_norm(x, w, b):
            m = jnp.mean(x, axis=-1, keepdims=True)
            v = jnp.var(x, axis=-1, keepdims=True)
            return (x - m) / jnp.sqrt(v + LN_EPS) * w + b
        Bx, Tx, Dx = x.shape
        xn = layer_norm(x, norm_w, norm_b)
        q = (xn @ q_w + q_b).reshape(Bx, Tx, H, -1)
        k = (xn @ k_w + k_b).reshape(Bx, Tx, H, -1)
        att = jnp.einsum('bnhl,bmhl->bnmh', q, k)
        mask = src_mask.reshape(Bx, 1, Tx, 1)
        att = att + (1.0 - mask) * -1000000.0
        att = jax.nn.softmax(att, axis=2)
        v = ((xn @ v_w + v_b) * src_mask[:, :, None]).reshape(Bx, Tx, H, -1)
        y = jnp.einsum('bnmh,bmhl->bnhl', att, v).reshape(Bx, Tx, Dx)
        e = jax.nn.silu(emb) @ emb_w + emb_b
        scale, shift = jnp.split(e[:, None, :], 2, axis=2)
        h = layer_norm(y, sb_norm_w, sb_norm_b) * (1.0 + scale) + shift
        h = jax.nn.silu(h) @ out_w + out_b
        return x + h

    def _L1_cond_ref(x, emb, src_mask, norm_scale, norm_bias, Wq, bq, Wk, bk, Wv, bv, film_emb_W, film_emb_b, film_norm_scale, film_norm_bias, film_out_W, film_out_b):
        import jax, jax.numpy as jnp
        import numpy as np
        H = 16
        LN_EPS = 1e-05

        def _layernorm(x, scale, bias):
            mu = jnp.mean(x, axis=-1, keepdims=True)
            var = jnp.var(x, axis=-1, keepdims=True)
            return (x - mu) * jax.lax.rsqrt(var + LN_EPS) * scale + bias
        B, T, D = x.shape
        dh = D // H
        xn = _layernorm(x, norm_scale, norm_bias)
        q = xn @ Wq + bq
        k = xn @ Wk + bk
        v = xn @ Wv + bv
        mask = (src_mask == 1)[:, :, None]
        k = jnp.where(mask, -jnp.inf, k)
        v = jnp.where(mask, 0.0, v)
        q = q.reshape(B, T, H, dh).transpose(0, 2, 1, 3)
        k = k.reshape(B, T, H, dh).transpose(0, 2, 1, 3)
        v = v.reshape(B, T, H, dh).transpose(0, 2, 1, 3)
        q = jax.nn.softmax(q, axis=-1)
        k = jax.nn.softmax(k, axis=2)
        attn = jnp.einsum('bhse,bhsd->bhed', k, v)
        y = jnp.einsum('bhtd,bhed->bhte', q, attn)
        y = y.transpose(0, 2, 1, 3).reshape(B, T, D)
        emb_out = jax.nn.silu(emb) @ film_emb_W + film_emb_b
        scale, shift = jnp.split(emb_out, 2, axis=-1)
        h = _layernorm(y, film_norm_scale, film_norm_bias) * (1.0 + scale[:, None, :]) + shift[:, None, :]
        h = jax.nn.silu(h) @ film_out_W + film_out_b
        return x + h

    def _L2_cond_ref(x, c, ln_g, ln_b, ada_w, ada_b, in_proj_w, conv_w, conv_b, x_proj_w, dt_proj_w, dt_proj_b, A_log, D_param, out_proj_w):
        import jax, jax.numpy as jnp
        import numpy as np
        D = 512
        DI = 1024
        N = 16
        DT_RANK = 64
        D_CONV = 4
        EPS = 1e-05

        def _layernorm(x, g, b):
            mu = jnp.mean(x, axis=-1, keepdims=True)
            var = jnp.mean((x - mu) ** 2, axis=-1, keepdims=True)
            return (x - mu) * jax.lax.rsqrt(var + EPS) * g + b

        def _mamba(xn, in_proj_w, conv_w, conv_b, x_proj_w, dt_proj_w, dt_proj_b, A_log, D_param, out_proj_w):
            b, sl, _ = xn.shape
            xz = jnp.einsum('bsd,ed->bse', xn, in_proj_w)
            x_in, z = jnp.split(xz, 2, axis=-1)
            xt = jnp.transpose(x_in, (0, 2, 1))
            u = jax.lax.conv_general_dilated(xt, conv_w[:, None, :], (1,), [(D_CONV - 1, 0)], feature_group_count=DI, dimension_numbers=('NCH', 'OIH', 'NCH')) + conv_b[None, :, None]
            u = jax.nn.silu(jnp.transpose(u, (0, 2, 1)))
            x_dbl = jnp.einsum('bsd,ed->bse', u, x_proj_w)
            dt_r, B, C = jnp.split(x_dbl, [DT_RANK, DT_RANK + N], axis=-1)
            dt = jax.nn.softplus(jnp.einsum('bsr,dr->bsd', dt_r, dt_proj_w) + dt_proj_b)
            A = -jnp.exp(A_log)

            def step(h, inp):
                dt_t, B_t, C_t, u_t = inp
                dA = jnp.exp(dt_t[:, :, None] * A)
                h = h * dA + (dt_t * u_t)[:, :, None] * B_t[:, None, :]
                y = jnp.einsum('bdn,bn->bd', h, C_t)
                return (h, y)
            seq = (jnp.transpose(dt, (1, 0, 2)), jnp.transpose(B, (1, 0, 2)), jnp.transpose(C, (1, 0, 2)), jnp.transpose(u, (1, 0, 2)))
            h0 = jnp.zeros((b, DI, N), xn.dtype)
            _, ys = jax.lax.scan(step, h0, seq)
            y = jnp.transpose(ys, (1, 0, 2)) + u * D_param
            y = y * jax.nn.silu(z)
            return jnp.einsum('bsd,ed->bse', y, out_proj_w)
        ada = jnp.einsum('bc,ec->be', jax.nn.silu(c), ada_w) + ada_b
        shift, scale, gate = jnp.split(ada, 3, axis=1)
        xn = _layernorm(x, ln_g, ln_b)
        xn = xn * (1.0 + scale[:, None, :]) + shift[:, None, :]
        x_ssm = _mamba(xn, in_proj_w, conv_w, conv_b, x_proj_w, dt_proj_w, dt_proj_b, A_log, D_param, out_proj_w)
        return x + gate[:, None, :] * x_ssm

    def _L3_cond_ref(x, c, W_ada, b_ada, gamma, beta, W_in, conv_w, conv_b, W_xp, W_dt, b_dt, A_log, D_param, W_out, perm, inv_perm):
        import jax, jax.numpy as jnp
        import numpy as np
        B_SZ, S, D = (4, 512, 512)
        DI, DS, DTR, DC = (1024, 16, 64, 4)
        EPS = 1e-05

        def _layernorm(x, g, b):
            m = jnp.mean(x, axis=-1, keepdims=True)
            v = jnp.var(x, axis=-1, keepdims=True)
            return (x - m) * jax.lax.rsqrt(v + EPS) * g + b

        def _mamba(h, W_in, conv_w, conv_b, W_xp, W_dt, b_dt, A_log, D_param, W_out):
            bsz = h.shape[0]
            xz = h @ W_in
            xm, z = jnp.split(xz, 2, axis=-1)
            xc = jnp.transpose(xm, (0, 2, 1))
            xc = jax.lax.conv_general_dilated(xc, conv_w, (1,), [(DC - 1, 0)], feature_group_count=DI, dimension_numbers=('NCH', 'OIH', 'NCH'))
            xc = xc + conv_b[None, :, None]
            xm = jax.nn.silu(jnp.transpose(xc, (0, 2, 1)))
            xdbl = xm @ W_xp
            dtr, Bm, Cm = jnp.split(xdbl, [DTR, DTR + DS], axis=-1)
            dt = jax.nn.softplus(dtr @ W_dt + b_dt)
            A = -jnp.exp(A_log)

            def step(hst, inp):
                dt_t, B_t, C_t, x_t = inp
                dA = jnp.exp(dt_t[:, :, None] * A)
                hst = hst * dA + (dt_t * x_t)[:, :, None] * B_t[:, None, :]
                y = jnp.einsum('bds,bs->bd', hst, C_t)
                return (hst, y)
            inputs = (jnp.transpose(dt, (1, 0, 2)), jnp.transpose(Bm, (1, 0, 2)), jnp.transpose(Cm, (1, 0, 2)), jnp.transpose(xm, (1, 0, 2)))
            h0 = jnp.zeros((bsz, DI, DS), dt.dtype)
            _, ys = jax.lax.scan(step, h0, inputs)
            y = jnp.transpose(ys, (1, 0, 2)) + xm * D_param
            y = y * jax.nn.silu(z)
            return y @ W_out
        mod = jax.nn.silu(c) @ W_ada + b_ada
        shift, scale, gate = jnp.split(mod, 3, axis=1)
        h = _layernorm(x, gamma, beta)
        h = h * (1.0 + scale[:, None, :]) + shift[:, None, :]
        h = h[:, perm]
        y = _mamba(h, W_in, conv_w, conv_b, W_xp, W_dt, b_dt, A_log, D_param, W_out)
        y = y[:, inv_perm]
        return x + gate[:, None, :] * y
    x = _L0_cond_ref(x, cond_2048, mask_BxS_ff1, L0_cond_norm_w, L0_cond_norm_b, L0_cond_q_w, L0_cond_q_b, L0_cond_k_w, L0_cond_k_b, L0_cond_v_w, L0_cond_v_b, L0_cond_emb_w, L0_cond_emb_b, L0_cond_sb_norm_w, L0_cond_sb_norm_b, L0_cond_out_w, L0_cond_out_b)
    x = _L1_cond_ref(x, cond_2048, mask_BxS_ik0, L1_cond_norm_scale, L1_cond_norm_bias, L1_cond_Wq, L1_cond_bq, L1_cond_Wk, L1_cond_bk, L1_cond_Wv, L1_cond_bv, L1_cond_film_emb_W, L1_cond_film_emb_b, L1_cond_film_norm_scale, L1_cond_film_norm_bias, L1_cond_film_out_W, L1_cond_film_out_b)
    x = _L2_cond_ref(x, cond_2048, L2_cond_ln_g, L2_cond_ln_b, L2_cond_ada_w, L2_cond_ada_b, L2_cond_in_proj_w, L2_cond_conv_w, L2_cond_conv_b, L2_cond_x_proj_w, L2_cond_dt_proj_w, L2_cond_dt_proj_b, L2_cond_A_log, L2_cond_D_param, L2_cond_out_proj_w)
    x = _L3_cond_ref(x, cond_2048, L3_cond_W_ada, L3_cond_b_ada, L3_cond_gamma, L3_cond_beta, L3_cond_W_in, L3_cond_conv_w, L3_cond_conv_b, L3_cond_W_xp, L3_cond_W_dt, L3_cond_b_dt, L3_cond_A_log, L3_cond_D_param, L3_cond_W_out, itok_S_0_1023, itok_S_0_1023)
    return x

_drawn_inputs = setup_inputs


def setup_inputs(seed=0):
    import zlib

    import numpy as np

    out = dict(_drawn_inputs(seed))
    spreads = {'L0_cond_norm_w': (1.0, 0.2),
     'L0_cond_norm_b': (0.0, 0.1),
     'L0_cond_q_b': (0.0, 0.1),
     'L0_cond_k_b': (0.0, 0.1),
     'L0_cond_v_b': (0.0, 0.1),
     'L0_cond_emb_b': (0.0, 0.1),
     'L0_cond_sb_norm_w': (1.0, 0.2),
     'L0_cond_sb_norm_b': (0.0, 0.1),
     'L0_cond_out_b': (0.0, 0.1),
     'L1_cond_norm_scale': (1.0, 0.2),
     'L1_cond_norm_bias': (0.0, 0.1),
     'L1_cond_bq': (0.0, 0.1),
     'L1_cond_bk': (0.0, 0.1),
     'L1_cond_bv': (0.0, 0.1),
     'L1_cond_film_emb_b': (0.0, 0.1),
     'L1_cond_film_norm_scale': (1.0, 0.2),
     'L1_cond_film_norm_bias': (0.0, 0.1),
     'L1_cond_film_out_b': (0.0, 0.1),
     'L2_cond_ln_g': (1.0, 0.2),
     'L2_cond_ln_b': (0.0, 0.1),
     'L2_cond_ada_b': (0.0, 0.1),
     'L2_cond_conv_b': (0.0, 0.1),
     'L2_cond_D_param': (1.0, 0.2),
     'L3_cond_b_ada': (0.0, 0.1),
     'L3_cond_gamma': (1.0, 0.2),
     'L3_cond_beta': (0.0, 0.1),
     'L3_cond_conv_b': (0.0, 0.1),
     'L3_cond_b_dt': (-4.600166320800781, 0.2),
     'L3_cond_D_param': (1.0, 0.2)}
    factors = {}
    for name, (base, spread) in spreads.items():
        noise = np.random.default_rng([zlib.crc32(name.encode()), seed]).standard_normal(out[name].shape)
        drawn = base * np.exp(spread * noise) if base else spread * noise
        out[name] = jnp.asarray(drawn.astype(out[name].dtype))
    for name, factor in factors.items():
        out[name] = (out[name] * factor).astype(out[name].dtype)
    return out
```

```python
from contextlib import ExitStack

import numpy as np
import concourse.bass as bass
from concourse import mybir

F32 = mybir.dt.float32
I32 = mybir.dt.int32
ALU = mybir.AluOpType
ACT = mybir.ActivationFunctionType
AX = mybir.AxisListType

P = 128
B, T, D = 4, 1024, 512
E = 1024
H, DH = 16, 32
DI, NS, R, KC = 1024, 16, 64, 4
KT = D // P
TT = T // P
HALF = 512
IB = DI // P
ET = E // P
EPS = 1e-5
HUGE = 3.0e38

COLS = [("q_b", 4), ("k_b", 4), ("bk", 4),
        ("norm_w0", 4), ("norm_b0", 4), ("sb_w", 4), ("sb_b", 4), ("emb_b0", 8),
        ("norm_w1", 4), ("norm_b1", 4), ("film_w", 4), ("film_b", 4), ("emb_b1", 8),
        ("ln_g2", 4), ("ln_b2", 4), ("ada_b2", 8), ("ln_g3", 4), ("ln_b3", 4), ("ada_b3", 8),
        ("conv_b2", 8), ("dt_b2", 8), ("D2", 8), ("conv_w2", 32), ("A_log2", 128),
        ("conv_b3", 8), ("dt_b3", 8), ("D3", 8), ("conv_w3", 32), ("A_log3", 128)]
COL_AT, _n = {}, 0
for _name, _w in COLS:
    COL_AT[_name] = _n
    _n += _w
NCOL = _n
ROWS = ["v_b", "out_b0", "bq", "bv", "out_b1", "gate_b2", "gate_b3"]
TABS = 6


class Count:

    def __init__(self, handle, base):
        self.handle, self.base = handle, base

    def at(self, n):
        return n + self.base

    def stage_added(self, n):
        self.base += n


class Core:

    def __init__(self, nc, ctx):
        self.nc = nc
        sem = lambda name: ctx.enter_context(nc.semaphore(name))
        many = lambda name, n, base: [Count(sem(f"{name}{k}"), base) for k in range(n)]
        self.bank_full = many("bank_full", 8, 1)
        self.bank_free = many("bank_free", 8, 1)
        self.stage_stored = many("stage_stored", 8, 16)
        self.stage_full = many("stage_full", 8, 0)
        self.residual_in = many("residual_in", 8, 0)
        self.input_in = many("input_in", 2, 0)
        self.input_free = many("input_free", 2, 1)
        self.consts_in = Count(sem("consts_in"), 0)
        self.vector_step = Count(sem("vector_step"), 0)
        self.scalar_step = Count(sem("scalar_step"), 0)
        self.pool_step = Count(sem("pool_step"), 0)
        self.turned_out = many("turned_out", 2, 16)
        self.u_out = Count(sem("u_out"), 16)
        self.scanned = Count(sem("scanned"), 16)
        self.scaled = Count(sem("scaled"), 16)
        self.unit_turned = Count(sem("unit_turned"), 16)
        self.gated = Count(sem("gated"), 2)
        self.g_stored = many("g_stored", 2, 16)
        self.replica_in = many("replica_in", NS, 0)
        self.passed = Count(sem("passed"), 0)
        self.named = {}
        self._sem = sem

    def apart(self, engine):
        engine.sem_inc(self.passed.handle, 1)

    def count(self, name):
        if name not in self.named:
            self.named[name] = Count(self._sem(name), 0)
        return self.named[name]


class Chain:

    def __init__(self, engine, count, offset=0):
        self.engine, self.count, self.n, self.offset = engine, count, 0, offset

    def __call__(self, instruction):
        self.n += 1
        instruction.then_inc(self.count.handle, 1)
        self.engine.wait_ge(self.count.handle, self.count.at(self.n + self.offset))


def allocator(nc, ctx, stage):
    def sb(name, shape, dt=F32):
        return ctx.enter_context(nc.sbuf_tensor(f"{stage}_{name}", shape, dt))

    def psum(name, shape):
        return ctx.enter_context(nc.psum_tensor(f"{stage}_{name}", shape, F32))

    return sb, psum


def give_credits(core, ident, zero_eps):
    nc = core.nc
    ready = core.count("ident_ready")
    with nc.Block() as block:
        @block.vector
        def _(dve):
            for c in core.bank_full + core.bank_free + core.input_free:
                dve.sem_inc(c.handle, 1)
            for c in core.stage_stored:
                dve.sem_inc(c.handle, 16)
            for c in [core.u_out, core.scanned, core.scaled, core.unit_turned, core.gated] + core.g_stored + core.turned_out:
                dve.sem_inc(c.handle, c.base)
            nc.vector.memset(zero_eps[:, 0:1], EPS)
            nc.vector.memset(zero_eps[:, 1:2], 0.0)
            nc.vector.memset(zero_eps[:, 2:3], 1.0)

        @block.gpsimd
        def _(pool):
            nc.gpsimd.memset(ident[:], 0.0).then_inc(ready.handle, 1)
            pool.wait_ge(ready.handle, 1)
            nc.gpsimd.affine_select(out=ident[:], in_=ident[:], compare_op=ALU.not_equal, fill=1.0,
                                    base=0, pattern=[[-1, P]], channel_multiplier=1)


def modulation(core, io, scr, cols):
    nc = core.nc
    with ExitStack() as ctx:
        sb, psum = allocator(nc, ctx, "mod")
        W = [sb(f"W{k}", [P, ET, 3 * D]) for k in range(2)]
        condT = sb("condT", [P, ET, B])
        silu_cT = sb("silu_cT", [P, ET, B])
        gate_bias = sb("gate_bias", [B, 2, D])
        gates = sb("gates", [B, 2, D])
        tab = sb("tab", [P, TABS, B, 8])
        e = sb("e", [P, 4, 8, B])
        part = sb("part", [P, 4, KT, B])
        mask0 = sb("mask0", [P, B, TT])
        mask1 = sb("mask1", [P, B, TT], I32)
        keep = sb("keep", [P, 2, B, TT])
        A = sb("A", [P, 2, IB, NS + 1])
        ps = [psum(f"ps{k}", [P, 8 * B]) for k in range(2)]
        pg = psum("pg", [B, D])
        w_in, w_free = core.input_in, core.input_free
        silu_done, mm_done = core.count("silu_done"), core.count("mod_mm_done")
        dve_done, act_done = core.count("mod_dve_done"), core.count("mod_act_done")
        widths = [2 * D, 2 * D, 3 * D, 3 * D]
        w_src = [io["emb_w0"], io["emb_w1"], io["ada_w2"], io["ada_w3"]]
        block = ctx.enter_context(nc.Block())
        col = lambda name, k, n=1: cols[:, COL_AT[name] + k:COL_AT[name] + k + n]

        @block.sync
        def _(sp):
            ci = core.consts_in.handle
            sp.dma_start(cols[:], io["cols"]).then_inc(ci, 16)
            sp.dma_start(condT[:], io["condT"].rearrange("(k p) b -> p k b", p=P)).then_inc(ci, 16)
            sp.dma_start(gate_bias[:], io["rows"][5:7, :].rearrange("(o r) d -> o r d", o=1)
                         .broadcast_to([B, 2, D])).then_inc(ci, 16)
            sp.dma_start(mask0[:], io["mask0_cols"]).then_inc(ci, 16)
            sp.dma_start(mask1[:], io["mask1_cols"]).then_inc(ci, 16)
            for l in range(4):
                if l >= 2:
                    sp.wait_ge(w_free[l % 2].handle, w_free[l % 2].at(1))
                sp.dma_start(W[l % 2][:, :, 0:widths[l]],
                             w_src[l].rearrange("(k p) f -> p k f", p=P)).then_inc(w_in[l % 2].handle, 16)
            out = core.count("tables_out")
            sp.wait_ge(dve_done.handle, dve_done.at(1))
            sp.wait_ge(act_done.handle, act_done.at(1))
            for t in range(TABS):
                sp.dma_start(scr["tab"][t].rearrange("b p e -> p b e"), tab[:, t]).then_inc(out.handle, 16)
            sp.dma_start(scr["gate"].rearrange("l b d -> b l d"), gates[:]).then_inc(out.handle, 16)
            for l in range(2):
                sp.dma_start(scr["keep"][l].rearrange("b p e -> p b e"), keep[:, l]).then_inc(out.handle, 16)
                sp.dma_start(scr["A"][l].rearrange("i p e -> p i e"), A[:, l]).then_inc(out.handle, 16)
            sp.wait_ge(out.handle, out.at(16 * (TABS + 5)))

        @block.scalar
        def _(act):
            act.wait_ge(core.consts_in.handle, core.consts_in.at(80))
            nc.scalar.activation(silu_cT[:], condT[:], ACT.Silu).then_inc(silu_done.handle, 1)
            for l in range(2):
                last = nc.scalar.activation(A[:, l, :, 0:NS],
                                            col(f"A_log{l + 2}", 0, 128).rearrange("p (i n) -> p i n", n=NS), ACT.Exp)
            last.then_inc(core.scalar_step.handle, 1)
            act.wait_ge(core.scalar_step.handle, core.scalar_step.at(1))
            for l in range(2):
                nc.scalar.mul(A[:, l, :, 0:NS], A[:, l, :, 0:NS], -1.0)
                last = nc.scalar.copy(A[:, l, :, NS], col(f"D{l + 2}", 0, 8))
            last.then_inc(act_done.handle, 1)

        @block.tensor
        def _(pe):
            pe.wait_ge(silu_done.handle, silu_done.at(1))
            for l in range(4):
                pe.wait_ge(w_in[l % 2].handle, w_in[l % 2].at(16 * (l // 2 + 1)))
                if l >= 1:
                    pe.wait_ge(core.count("mod_read").handle, core.count("mod_read").at(l))
                for f in range(8):
                    for k in range(ET):
                        last = nc.tensor.matmul(ps[l % 2][:, f * B:(f + 1) * B], W[l % 2][:, k, f * P:(f + 1) * P],
                                                silu_cT[:, k, :], start=(k == 0), stop=(k == ET - 1))
                if l >= 2:
                    for k in range(ET):
                        last = nc.tensor.matmul(pg[:], silu_cT[:, k, :], W[l % 2][:, k, 2 * D:3 * D],
                                                start=(k == 0), stop=(k == ET - 1))
                last.then_inc(mm_done.handle, 1)

        @block.vector
        def _(dve):
            read = core.count("mod_read")
            step = Chain(dve, core.vector_step)
            dve.wait_ge(core.consts_in.handle, core.consts_in.at(80))
            nc.vector.tensor_copy(keep[:, 0], mask0[:])
            nc.vector.tensor_scalar(keep[:, 1], mask1[:], 1.0, None, ALU.not_equal)
            for t, w, b in ((0, "norm_w0", "norm_b0"), (2, "norm_w1", "norm_b1")):
                for bb in range(B):
                    nc.vector.tensor_copy(tab[:, t, bb, 0:4], col(w, 0, 4))
                    nc.vector.tensor_copy(tab[:, t, bb, 4:8], col(b, 0, 4))
            for l in range(4):
                t, w, b, bias = ((1, "sb_w", "sb_b", "emb_b0"), (3, "film_w", "film_b", "emb_b1"),
                                 (4, "ln_g2", "ln_b2", "ada_b2"), (5, "ln_g3", "ln_b3", "ada_b3"))[l]
                scale0, shift0 = (0, 4) if l < 2 else (4, 0)
                dve.wait_ge(mm_done.handle, mm_done.at(l + 1))
                for f in range(8):
                    last = nc.vector.tensor_scalar(e[:, l, f], ps[l % 2][:, f * B:(f + 1) * B], col(bias, f), None, ALU.add)
                if l >= 2:
                    last = nc.vector.tensor_tensor(gates[:, l - 2], pg[:], gate_bias[:, l - 2], ALU.add)
                last.then_inc(read.handle, 1)
                dve.wait_ge(read.handle, read.at(l + 1))
                if l < 2:
                    dve.sem_inc(w_free[l % 2].handle, 1)
                for k in range(KT):
                    nc.vector.tensor_scalar(tab[:, t, :, k], e[:, l, scale0 + k], 1.0, col(w, k), ALU.add, ALU.mult)
                    last = nc.vector.tensor_scalar(part[:, l, k], e[:, l, scale0 + k], 1.0, col(b, k), ALU.add, ALU.mult)
                step(last)
                for k in range(KT):
                    last = nc.vector.tensor_tensor(tab[:, t, :, 4 + k], part[:, l, k], e[:, l, shift0 + k], ALU.add)
            last.then_inc(dve_done.handle, 1)

    core.consts_in.stage_added(80)
    for k in range(2):
        w_in[k].stage_added(32)
        w_free[k].stage_added(1)
    core.vector_step.stage_added(4)
    core.scalar_step.stage_added(1)


def normalize(core, name, ident, eps, src, tab, func, dst, gather=None):
    nc = core.nc
    with ExitStack() as ctx:
        sb, psum = allocator(nc, ctx, name)
        x = [sb(f"x{k}", [P, TT, D]) for k in range(2)]
        tb = [sb(f"tb{k}", [P, 8]) for k in range(2)]
        xh = sb("xh", [P, TT, D])
        xT = [sb(f"xT{k}", [P, KT, T]) for k in range(2)]
        st = sb("st", [P, TT, 6])
        mv = sb("mv", [P, TT, 2])
        lv = sb("lv", [P, TT])
        rstd = sb("rstd", [P, TT])
        banks = [psum(f"bank{k}", [P, HALF]) for k in range(8)]
        stats_done, rstd_done = core.count("stats_done"), core.count("rstd_done")
        xhat_done, turned_out = core.count("xhat_done"), core.turned_out
        evacuated = core.count("turned_in_sbuf")
        xs_in, xs_free = core.input_in, core.input_free
        full, free = core.bank_full, core.bank_free
        if gather is not None:
            idx = sb("idx", [P, TT], I32)
            idx_b = sb("idx_b", [P, B, TT], I32)
            idx_done = core.count("idx_done")
        block = ctx.enter_context(nc.Block())
        n_in = 32 if gather is None else 16
        rows_in = None if gather is None else [core.count(f"{name}_rows_in{k}") for k in range(2)]

        def load_rows(eng, it, j, u):
            eng.wait_ge(xs_free[j].handle, xs_free[j].at(u))
            eng.dma_start(tb[j][:], tab[it]).then_inc(xs_in[j].handle, 16)
            eng.dma_start(x[j][:], src[it].rearrange("(k p) d -> p k d", p=P)).then_inc(xs_in[j].handle, 16)

        if gather is None:
            @block.sync
            def _(sp):
                with sp.Fori(0, B // 2) as i:
                    for j in range(2):
                        load_rows(sp, i * 2 + j, j, i)
        else:
            @block.sync
            def _(sp):
                sp.dma_start(idx[:], gather).then_inc(core.consts_in.handle, 16)
                for it in range(B):
                    j = it % 2
                    sp.wait_ge(xs_free[j].handle, xs_free[j].at(it // 2))
                    sp.dma_start(tb[j][:], tab[it]).then_inc(xs_in[j].handle, 16)

            @block.gpsimd
            def _(pool):
                pool.wait_ge(idx_done.handle, idx_done.at(1))
                for it in range(B):
                    j = it % 2
                    pool.wait_ge(xs_free[j].handle, xs_free[j].at(it // 2))
                    for k in range(TT):
                        pool.indirect_dma_start(x[j][:, k, :], None, src.rearrange("b t d -> (b t) d"),
                                                bass.IndirectOffsetOnAxis(ap=idx_b[:, it, k:k + 1], axis=0)
                                                ).then_inc(rows_in[j].handle, 16)

        @block.vector
        def _(dve):
            if gather is not None:
                dve.wait_ge(core.consts_in.handle, core.consts_in.at(16))
                for it in range(B):
                    last = nc.vector.tensor_scalar(idx_b[:, it, :], idx[:], float(it * T), None, ALU.add)
                last.then_inc(idx_done.handle, 1)
            with dve.Fori(0, B // 2) as i:
                for j in range(2):
                    it = i * 2 + j
                    dve.wait_ge(xs_in[j].handle, xs_in[j].at(i * n_in + n_in))
                    if gather is not None:
                        dve.wait_ge(rows_in[j].handle, rows_in[j].at(i * (16 * TT) + 16 * TT))
                    for k in range(TT):
                        last = nc.vector.bn_stats(st[:, k, :], x[j][:, k, :])
                    last.then_inc(core.vector_step.handle, 1)
                    dve.wait_ge(core.vector_step.handle, core.vector_step.at(it + 1))
                    core.apart(dve)
                    for k in range(TT):
                        last = nc.vector.bn_aggr(mv[:, k, :], st[:, k, :])
                    last.then_inc(stats_done.handle, 1)
                    dve.wait_ge(rstd_done.handle, rstd_done.at(it + 1))
                    for k in range(TT):
                        if k == 0:
                            for o in range(8):
                                dve.wait_ge(full[o].handle, full[o].at(it))
                        ins = nc.vector.tensor_scalar(xh[:, k, :], x[j][:, k, :], mv[:, k, 0:1], rstd[:, k:k + 1],
                                                      ALU.subtract, ALU.mult)
                        if k % 4 == 3:
                            ins.then_inc(xhat_done.handle, 1)
                    dve.wait_ge(xhat_done.handle, xhat_done.at(it * 2 + 2))
                    dve.wait_ge(evacuated.handle, evacuated.at(it * 8 + 8))
                    dve.sem_inc(xs_free[j].handle, 1)

        @block.scalar
        def _(act):
            with act.Fori(0, B // 2) as i:
                for j in range(2):
                    it = i * 2 + j
                    act.wait_ge(stats_done.handle, stats_done.at(it + 1))
                    nc.scalar.activation(lv[:], mv[:, :, 1], ACT.Ln, bias=eps[:, 0:1]).then_inc(core.scalar_step.handle, 1)
                    act.wait_ge(core.scalar_step.handle, core.scalar_step.at(it + 1))
                    nc.scalar.activation(rstd[:], lv[:], ACT.Exp, scale=-0.5).then_inc(rstd_done.handle, 1)
                    act.wait_ge(turned_out[j].handle, turned_out[j].at(i * 16))
                    for h in range(2):
                        for kt in range(KT):
                            o = h * KT + kt
                            act.wait_ge(full[o].handle, full[o].at(it + 1))
                            nc.scalar.activation(xT[j][:, kt, h * HALF:(h + 1) * HALF], banks[o][:], func,
                                                 scale=tb[j][:, kt:kt + 1], bias=tb[j][:, 4 + kt:5 + kt]
                                                 ).then_inc(evacuated.handle, 1)
                            act.wait_ge(evacuated.handle, evacuated.at(it * 8 + (o + 1)))
                            act.sem_inc(free[o].handle, 1)
                    act.dma_start(dst[it], xT[j][:]).then_inc(turned_out[j].handle, 16)
            for j in range(2):
                act.wait_ge(turned_out[j].handle, turned_out[j].at(8 * B))

        @block.tensor
        def _(pe):
            with pe.Fori(0, B // 2) as i:
                for j in range(2):
                    it = i * 2 + j
                    for h in range(2):
                        pe.wait_ge(xhat_done.handle, xhat_done.at(it * 2 + (h + 1)))
                        for kt in range(KT):
                            o = h * KT + kt
                            pe.wait_ge(free[o].handle, free[o].at(it))
                            for q in range(4):
                                last = nc.tensor.transpose(banks[o][:, q * P:(q + 1) * P],
                                                           xh[:, h * 4 + q, kt * P:(kt + 1) * P], ident[:])
                            last.then_inc(full[o].handle, 1)

    for k in range(2):
        xs_in[k].stage_added(n_in * B // 2)
        xs_free[k].stage_added(B // 2)
    for o in range(8):
        full[o].stage_added(B)
        free[o].stage_added(B)
    core.vector_step.stage_added(B)
    core.scalar_step.stage_added(B)
    stats_done.stage_added(B)
    rstd_done.stage_added(B)
    xhat_done.stage_added(2 * B)
    evacuated.stage_added(8 * B)
    for j in range(2):
        turned_out[j].stage_added(8 * B)
    if gather is not None:
        core.consts_in.stage_added(16)
        idx_done.stage_added(1)


def project(core, name, io, cols, src, jobs):
    nc = core.nc
    with ExitStack() as ctx:
        sb, psum = allocator(nc, ctx, name)
        xT = [sb(f"xT{k}", [P, KT, T]) for k in range(2)]
        W = [sb(f"W{n}", [P, KT, job["n"]]) for n, job in enumerate(jobs)]
        row = [sb(f"row{n}", [P, D]) if job.get("row") is not None else None for n, job in enumerate(jobs)]
        kp = [sb(f"keep{k}", [P, TT]) for k in range(2)]
        keep = next((job["keep"] for job in jobs if job.get("keep") is not None), None)
        has_res = any(job.get("residual") is not None for job in jobs)
        res = [sb(f"res{k}", [P, D]) for k in range(8)] if has_res else None
        stage = [sb(f"stage{k}", [P, HALF]) for k in range(8)]
        banks = [psum(f"bank{k}", [P, HALF]) for k in range(8)]
        outs = []
        for n, job in enumerate(jobs):
            if job["kind"] == "T":
                outs += [(n, m, h) for m in range(job["n"] // P) for h in range(2)]
            else:
                outs += [(n, f, t) for t in range(TT) for f in range(job["n"] // D)]
        uses = len(outs) // 8
        full, free = core.bank_full, core.bank_free
        staged, stored = core.stage_full, core.stage_stored
        steps = sum(1 for n, _, _ in outs if jobs[n].get("keep") is not None or jobs[n].get("residual") is not None)
        n_const = 16 * (len(jobs) + sum(r is not None for r in row))
        n_in = 16 if keep is None else 32
        block = ctx.enter_context(nc.Block())

        def on_scalar(n):
            return jobs[n]["kind"] == "T" or jobs[n].get("silu")

        @block.tensor
        def _(pe):
            pe.wait_ge(core.consts_in.handle, core.consts_in.at(n_const))
            with pe.Fori(0, B // 2) as i:
                for j in range(2):
                    pe.wait_ge(core.input_in[j].handle, core.input_in[j].at(i * n_in + n_in))
                    for o, (n, a, b) in enumerate(outs):
                        k8 = o % 8
                        pe.wait_ge(free[k8].handle, free[k8].at((i * 2 + j) * uses + o // 8))
                        for kt in range(KT):
                            if jobs[n]["kind"] == "T":
                                lhs, rhs = W[n][:, kt, a * P:(a + 1) * P], xT[j][:, kt, b * HALF:(b + 1) * HALF]
                            else:
                                lhs, rhs = xT[j][:, kt, b * P:(b + 1) * P], W[n][:, kt, a * D:(a + 1) * D]
                            last = nc.tensor.matmul(banks[k8][:], lhs, rhs, start=(kt == 0), stop=(kt == KT - 1))
                        last.then_inc(full[k8].handle, 1)
                        if o == len(outs) - 1:
                            pe.wait_ge(full[k8].handle, full[k8].at((i * 2 + j) * uses + uses))
                    if keep is not None:
                        kv = [o for o, (n, _, _) in enumerate(outs) if jobs[n].get("keep") is not None][-1]
                        pe.wait_ge(staged[kv % 8].handle, staged[kv % 8].at((i * 2 + j) * uses + (kv // 8 + 1)))
                    pe.sem_inc(core.input_free[j].handle, 1)

        @block.scalar
        def _(act):
            with act.Fori(0, B // 2) as i:
                for j in range(2):
                    for o, (n, a, b) in enumerate(outs):
                        if not on_scalar(n):
                            continue
                        k8, u = o % 8, (i * 2 + j) * uses + o // 8
                        act.wait_ge(full[k8].handle, full[k8].at(u + 1))
                        act.wait_ge(stored[k8].handle, stored[k8].at(u * 16))
                        job = jobs[n]
                        if job.get("silu"):
                            ins = nc.scalar.activation(stage[k8][:], banks[k8][:], ACT.Silu)
                        elif job.get("col") is not None:
                            at = COL_AT[job["col"]] + a
                            ins = nc.scalar.activation(stage[k8][:], banks[k8][:], ACT.Identity, bias=cols[:, at:at + 1])
                        else:
                            ins = nc.scalar.copy(stage[k8][:], banks[k8][:])
                        ins.then_inc(staged[k8].handle, 1)
                        act.wait_ge(staged[k8].handle, staged[k8].at(u + 1))
                        act.sem_inc(free[k8].handle, 1)

        @block.vector
        def _(dve):
            if n_const:
                dve.wait_ge(core.consts_in.handle, core.consts_in.at(n_const))
            with dve.Fori(0, B // 2) as i:
                for j in range(2):
                    done = 0
                    if keep is not None:
                        dve.wait_ge(core.input_in[j].handle, core.input_in[j].at(i * n_in + n_in))
                    for o, (n, a, b) in enumerate(outs):
                        if on_scalar(n):
                            continue
                        k8, u = o % 8, (i * 2 + j) * uses + o // 8
                        job = jobs[n]
                        dve.wait_ge(full[k8].handle, full[k8].at(u + 1))
                        dve.wait_ge(stored[k8].handle, stored[k8].at(u * 16))
                        ins = nc.vector.tensor_tensor(stage[k8][:], banks[k8][:], row[n][:], ALU.add)
                        if job.get("keep") is not None or job.get("residual") is not None:
                            done += 1
                            ins.then_inc(core.vector_step.handle, 1)
                            dve.wait_ge(core.vector_step.handle, core.vector_step.at((i * 2 + j) * steps + done))
                            if job.get("keep") is not None:
                                ins = nc.vector.tensor_scalar(stage[k8][:], stage[k8][:], kp[j][:, b:b + 1], None, ALU.mult)
                            else:
                                dve.wait_ge(core.residual_in[k8].handle, core.residual_in[k8].at(u * 16 + 16))
                                ins = nc.vector.tensor_tensor(stage[k8][:], stage[k8][:], res[k8][:], ALU.add)
                        ins.then_inc(staged[k8].handle, 1)
                        dve.wait_ge(staged[k8].handle, staged[k8].at(u + 1))
                        dve.sem_inc(free[k8].handle, 1)

        @block.sync
        def _(sp):
            def load(it):
                j = it % 2
                sp.wait_ge(core.input_free[j].handle, core.input_free[j].at(it // 2))
                sp.dma_start(xT[j][:], src[it]).then_inc(core.input_in[j].handle, 16)
                if keep is not None:
                    sp.dma_start(kp[j][:], keep[it]).then_inc(core.input_in[j].handle, 16)

            for n, job in enumerate(jobs):
                sp.dma_start(W[n][:], job["w"].rearrange("(k p) f -> p k f", p=P)).then_inc(core.consts_in.handle, 16)
                if row[n] is not None:
                    sp.dma_start(row[n][:], io["rows"][job["row"]:job["row"] + 1, :].broadcast_to([P, D])
                                 ).then_inc(core.consts_in.handle, 16)
            load(0)
            load(1)
            for it in range(B):
                if has_res:
                    for k in range(8):
                        sp.wait_ge(free[k].handle, free[k].at(it * uses))
                        sp.dma_start(res[k][:], jobs[0]["residual"][it, k * P:(k + 1) * P, :]
                                     ).then_inc(core.residual_in[k].handle, 16)
                for o, (n, a, b) in enumerate(outs):
                    k8, u = o % 8, it * uses + o // 8
                    job = jobs[n]
                    if job["kind"] == "T":
                        dst = job["dst"][it, :, a, b * HALF:(b + 1) * HALF]
                    else:
                        dst = job["dst"][it, b * P:(b + 1) * P, a * D:(a + 1) * D]
                    sp.wait_ge(staged[k8].handle, staged[k8].at(u + 1))
                    sp.dma_start(dst, stage[k8][:]).then_inc(stored[k8].handle, 16)
                if it + 2 < B:
                    load(it + 2)
            for k in range(8):
                sp.wait_ge(stored[k].handle, stored[k].at(16 * B * uses))

    core.consts_in.stage_added(n_const)
    for k in range(2):
        core.input_in[k].stage_added(n_in * B // 2)
        core.input_free[k].stage_added(B // 2)
    for k in range(8):
        full[k].stage_added(B * uses)
        free[k].stage_added(B * uses)
        staged[k].stage_added(B * uses)
        stored[k].stage_added(16 * B * uses)
        if has_res:
            core.residual_in[k].stage_added(16 * B)
    core.vector_step.stage_added(B * steps)


def attention(core, ident, io, scr):
    nc = core.nc
    VW = DH + 1
    with ExitStack() as ctx:
        sb, psum = allocator(nc, ctx, "att")
        kT = sb("kT", [P, KT, T])
        v = sb("v", [P, TT, D])
        va = sb("va", [P, TT * H, VW])
        mrow = sb("mrow", [P, T])
        mneg = sb("mneg", [P, T])
        q = [sb(f"q{k}", [P, KT, P]) for k in range(2)]
        sm = [sb(f"sm{k}", [P, T]) for k in range(2)]
        nmax = [sb(f"nmax{k}", [P, 1]) for k in range(2)]
        pr = [sb(f"pr{k}", [P, T]) for k in range(2)]
        pT = [sb(f"pT{k}", [P, T]) for k in range(2)]
        rden = sb("rden", [P, 2, 8])
        y = [sb(f"y{k}", [P, H, DH]) for k in range(2)]
        S = [psum(f"S{k}", [P, T]) for k in range(2)]
        TP = psum("TP", [P, T])
        Y = [psum(f"Y{k}", [P, 8 * VW]) for k in range(2)]
        kv_in, kv_free = core.count("kv_in"), core.input_free[0]
        q_in, q_free = core.input_in, core.count("q_free")
        va_ready, mneg_ready = core.count("va_ready"), core.count("mneg_ready")
        scored, shifted = core.count("scored"), core.count("shifted")
        exped, turned = core.count("exped"), core.count("turned")
        copied, weighed = core.count("copied"), core.count("weighed")
        y_ready, y_taken = core.count("y_ready"), core.count("y_taken")
        y_stored = core.stage_stored
        U = 2 * H
        block = ctx.enter_context(nc.Block())
        PAIRS = TT // 2

        @block.sync
        def _(sp):
            with sp.Fori(0, B) as b:
                sp.wait_ge(kv_free.handle, kv_free.at(b))
                sp.dma_start(kT[:], scr["kT"][b]).then_inc(kv_in.handle, 16)
                sp.dma_start(v[:], scr["v"][b].rearrange("(k p) d -> p k d", p=P)).then_inc(kv_in.handle, 16)
                sp.dma_start(mrow[:], io["mask0"][bass.ds(b, 1), :].broadcast_to([P, T])).then_inc(kv_in.handle, 16)
                with sp.Fori(0, PAIRS) as i:
                    for j in range(2):
                        n = (b * PAIRS + i) * 2 + j
                        sp.wait_ge(q_free.handle, q_free.at(b * PAIRS + i + 1))
                        sp.dma_start(q[j][:], scr["qT"][b, :, :, bass.ds((i * 2 + j) * P, P)]
                                     ).then_inc(q_in[j].handle, 16)

        @block.gpsimd
        def _(pool):
            pool.sem_inc(q_free.handle, 1)
            nc.gpsimd.memset(va[:, :, DH:VW], 1.0)
            with pool.Fori(0, B) as b:
                pool.wait_ge(kv_in.handle, kv_in.at(b * 48 + 48))
                core.apart(pool)
                nc.gpsimd.tensor_copy(va[:, :, 0:DH], v[:].rearrange("p k (h e) -> p (k h) e", e=DH)
                                      ).then_inc(va_ready.handle, 1)
                nc.gpsimd.tensor_scalar(mneg[:], mrow[:], 1.0, 1.0e6, ALU.subtract, ALU.mult
                                        ).then_inc(mneg_ready.handle, 1)
                pool.wait_ge(y_taken.handle, y_taken.at((b + 1) * TT))
                pool.sem_inc(kv_free.handle, 1)

        @block.tensor
        def _(pe):
            with pe.Fori(0, B) as b:
                pe.wait_ge(va_ready.handle, va_ready.at(b + 1))
                core.apart(pe)
                with pe.Fori(0, PAIRS) as i:
                    pair = b * PAIRS + i
                    base = pair * U

                    def scores(u):
                        j, h = u // H, u % H
                        if h == 0:
                            pe.wait_ge(q_in[j].handle, q_in[j].at(pair * 16 + 16))
                        if u >= 2:
                            pe.wait_ge(shifted.handle, shifted.at(base + (u - 1)))
                        rows = slice(32 * (h % 4), 32 * (h % 4) + 32)
                        for c in range(2):
                            last = nc.tensor.matmul(S[u % 2][:, c * HALF:(c + 1) * HALF], q[j][rows, h // 4, :],
                                                    kT[rows, h // 4, c * HALF:(c + 1) * HALF], start=True, stop=True)
                        last.then_inc(scored.handle, 1)

                    def turn(u):
                        pe.wait_ge(exped.handle, exped.at(base + (u + 1)))
                        if u >= 1:
                            pe.wait_ge(copied.handle, copied.at(base + u))
                        for m in range(TT):
                            last = nc.tensor.transpose(TP[:, m * P:(m + 1) * P], pr[u % 2][:, m * P:(m + 1) * P], ident[:])
                        last.then_inc(turned.handle, 1)

                    def weigh(u):
                        j, h = u // H, u % H
                        pe.wait_ge(copied.handle, copied.at(base + (u + 1)))
                        if h % 8 == 0 and u >= H:
                            pe.wait_ge(y_ready.handle, y_ready.at((pair * 2 + (j - 1)) * 2 + (h // 8 + 1)))
                        for m in range(TT):
                            last = nc.tensor.matmul(Y[h // 8][:, (h % 8) * VW:(h % 8 + 1) * VW],
                                                    pT[u % 2][:, m * P:(m + 1) * P], va[:, m * H + h, :],
                                                    start=(m == 0), stop=(m == TT - 1))
                        last.then_inc(weighed.handle, 1)

                    scores(0)
                    for u in range(U):
                        if u + 1 < U:
                            scores(u + 1)
                        turn(u)
                        if u >= 1:
                            weigh(u - 1)
                    weigh(U - 1)
                    pe.wait_ge(y_ready.handle, y_ready.at(pair * 4 + 4))
                    pe.sem_inc(q_free.handle, 1)

        @block.vector
        def _(dve):
            with dve.Fori(0, B) as b:
                dve.wait_ge(mneg_ready.handle, mneg_ready.at(b + 1))
                core.apart(dve)
                with dve.Fori(0, PAIRS) as i:
                    pair = b * PAIRS + i
                    base = pair * U

                    def take(j, half):
                        dve.wait_ge(weighed.handle, weighed.at(base + (j * H + 8 * half + 8)))
                        Yv = Y[half][:].rearrange("p (h e) -> p h e", e=VW)
                        nc.vector.reciprocal(rden[:, half, :], Yv[:, :, DH]).then_inc(core.vector_step.handle, 1)
                        dve.wait_ge(core.vector_step.handle, core.vector_step.at((pair * 2 + j) * 2 + (half + 1)))
                        if half == 0:
                            dve.wait_ge(y_stored[j].handle, y_stored[j].at(pair * 16))
                        nc.vector.tensor_tensor(y[j][:, 8 * half:8 * half + 8, :], Yv[:, :, 0:DH],
                                                rden[:, half, :].unsqueeze(2).broadcast_to([P, 8, DH]), ALU.mult
                                                ).then_inc(y_ready.handle, 1)

                    for u in range(U):
                        dve.wait_ge(scored.handle, scored.at(base + (u + 1)))
                        if u >= 2:
                            dve.wait_ge(exped.handle, exped.at(base + (u - 1)))
                        core.apart(dve)
                        nc.vector.tensor_tensor_reduce(sm[u % 2][:], S[u % 2][:], mneg[:], -1.0, HUGE,
                                                       ALU.add, ALU.min, nmax[u % 2][:]).then_inc(shifted.handle, 1)
                        if u >= 10 and (u - 10) % 8 == 0:
                            g = (u - 10) // 8
                            take(g // 2, g % 2)
                    take(1, 1)

        @block.scalar
        def _(act):
            with act.Fori(0, B * PAIRS) as pair:
                base = pair * U
                for u in range(U):
                    act.wait_ge(shifted.handle, shifted.at(base + (u + 1)))
                    if u >= 2:
                        act.wait_ge(turned.handle, turned.at(base + (u - 1)))
                    nc.scalar.activation(pr[u % 2][:], sm[u % 2][:], ACT.Exp, bias=nmax[u % 2][:, 0:1], scale=-1.0
                                         ).then_inc(exped.handle, 1)
                    act.wait_ge(turned.handle, turned.at(base + (u + 1)))
                    if u >= 2:
                        act.wait_ge(weighed.handle, weighed.at(base + (u - 1)))
                    nc.scalar.copy(pT[u % 2][:], TP[:]).then_inc(copied.handle, 1)
                    if u in (H + 4, U - 1):
                        j = 0 if u == H + 4 else 1
                        act.wait_ge(y_ready.handle, y_ready.at(pair * 4 + (j * 2 + 2)))
                        act.dma_start(scr["y"].rearrange("b t d -> (b t) d")[bass.ds((pair * 2 + j) * P, P), :],
                                      y[j][:].rearrange("p h e -> p (h e)")).then_inc(y_stored[j].handle, 16)
                        act.sem_inc(y_taken.handle, 1)
            for j in range(2):
                act.wait_ge(y_stored[j].handle, y_stored[j].at(16 * B * PAIRS))

    n = B * TT * H
    for c in (scored, shifted, exped, turned, copied, weighed):
        c.stage_added(n)
    for j in range(2):
        q_in[j].stage_added(16 * B * PAIRS)
        y_stored[j].stage_added(16 * B * PAIRS)
    kv_free.stage_added(B)
    kv_in.stage_added(48 * B)
    core.vector_step.stage_added(2 * B * TT)


def linear_attention(core, ident, io, scr):
    nc = core.nc
    with ExitStack() as ctx:
        sb, psum = allocator(nc, ctx, "lin")
        kT = sb("kT", [P, KT, T])
        q = sb("q", [P, TT, D])
        v = sb("v", [P, TT, D])
        mi = sb("mi", [P, T], I32)
        mneg = sb("mneg", [P, T])
        ks = sb("ks", [P, KT, T])
        nmax = sb("nmax", [P, KT])
        ksum = sb("ksum", [P, KT])
        kr = sb("kr", [P, KT])
        kn = sb("kn", [P, TT, D])
        qmax = sb("qmax", [P, TT * H])
        qsum = sb("qsum", [P, TT * H])
        qr = sb("qr", [P, TT * H])
        qT = sb("qT", [P, KT, T])
        at = sb("at", [P, KT, P])
        y = sb("y", [P, TT, D])
        banks = [psum(f"bank{k}", [P, HALF]) for k in range(8)]
        kv_in = core.count("kv_in")
        chain_v, chain_a = core.vector_step, core.scalar_step
        lin = {n: core.count("lin_" + n) for n in ("k_shift", "k_exp", "k_norm", "q_shift", "q_exp", "q_norm",
                                                   "k_turn", "k_copy", "q_turn", "q_copy", "at", "at_copy",
                                                   "y", "y_copy", "stored")}
        w = lambda eng, n, value: eng.wait_ge(lin[n].handle, value)
        block = ctx.enter_context(nc.Block())

        @block.sync
        def _(sp):
            with sp.Fori(0, B) as b:
                sp.wait_ge(core.input_free[0].handle, core.input_free[0].at(b))
                sp.dma_start(kT[:], scr["kT"][b]).then_inc(kv_in.handle, 16)
                sp.dma_start(mi[:], io["mask1"][bass.ds(b, 1), :].broadcast_to([P, T])).then_inc(kv_in.handle, 16)
                sp.dma_start(q[:], scr["q"][b].rearrange("(k p) d -> p k d", p=P)).then_inc(kv_in.handle, 16)
                sp.dma_start(v[:], scr["v"][b].rearrange("(k p) d -> p k d", p=P)).then_inc(kv_in.handle, 16)
                w(sp, "y_copy", b * TT + TT)
                sp.dma_start(scr["y"][b].rearrange("(k p) d -> p k d", p=P), y[:]).then_inc(lin["stored"].handle, 16)
                w(sp, "stored", b * 16 + 16)
                sp.sem_inc(core.input_free[0].handle, 1)

        @block.vector
        def _(dve):
            nc.vector.memset(at[:], 0.0)
            with dve.Fori(0, B) as b:
                dve.wait_ge(kv_in.handle, kv_in.at(b * 64 + 64))
                nc.vector.tensor_scalar(mneg[:], mi[:], 1.0, -HUGE, ALU.is_equal, ALU.mult).then_inc(chain_v.handle, 1)
                dve.wait_ge(chain_v.handle, chain_v.at(b * 4 + 1))
                core.apart(dve)
                for kt in range(KT):
                    nc.vector.tensor_tensor_reduce(ks[:, kt], kT[:, kt], mneg[:], -1.0, HUGE, ALU.add, ALU.min,
                                                   nmax[:, kt:kt + 1]).then_inc(lin["k_shift"].handle, 1)
                qv = q[:].rearrange("p k (h e) -> p (k h) e", e=DH)
                wide = lambda x: x[:].unsqueeze(2).broadcast_to([P, TT * H, DH])
                nc.vector.tensor_reduce(qmax[:], qv, AX.X, ALU.max).then_inc(chain_v.handle, 1)
                dve.wait_ge(chain_v.handle, chain_v.at(b * 4 + 2))
                nc.vector.tensor_tensor(qv, qv, wide(qmax), ALU.subtract).then_inc(lin["q_shift"].handle, 1)
                w(dve, "k_exp", b * KT + KT)
                nc.vector.reciprocal(kr[:], ksum[:]).then_inc(chain_v.handle, 1)
                dve.wait_ge(chain_v.handle, chain_v.at(b * 4 + 3))
                for kt in range(KT):
                    last = nc.vector.tensor_scalar(ks[:, kt], ks[:, kt], kr[:, kt:kt + 1], None, ALU.mult)
                last.then_inc(lin["k_norm"].handle, 1)
                w(dve, "q_exp", b + 1)
                nc.vector.tensor_reduce(qsum[:], qv, AX.X, ALU.add).then_inc(chain_v.handle, 1)
                dve.wait_ge(chain_v.handle, chain_v.at(b * 4 + 4))
                nc.vector.reciprocal(qr[:], qsum[:]).then_inc(lin["q_norm"].handle, 1)
                w(dve, "q_norm", b * 2 + 1)
                nc.vector.tensor_tensor(qv, qv, wide(qr), ALU.mult).then_inc(lin["q_norm"].handle, 1)
                w(dve, "at", b + 1)
                for g in range(4):
                    r = slice(32 * g, 32 * g + 32)
                    last = nc.vector.tensor_copy(at[r, :, r], banks[0][:].rearrange("p (k e) -> p k e", e=P)[r, :, r])
                last.then_inc(lin["at_copy"].handle, 1)

        @block.scalar
        def _(act):
            with act.Fori(0, B) as b:
                for kt in range(KT):
                    w(act, "k_shift", b * KT + (kt + 1))
                    nc.scalar.activation(ks[:, kt], ks[:, kt], ACT.Exp, bias=nmax[:, kt:kt + 1], scale=-1.0,
                                         accum_out=ksum[:, kt:kt + 1]).then_inc(lin["k_exp"].handle, 1)
                w(act, "q_shift", b + 1)
                nc.scalar.activation(q[:], q[:], ACT.Exp).then_inc(lin["q_exp"].handle, 1)
                for t in range(TT):
                    w(act, "k_turn", b * TT + (t + 1))
                    nc.scalar.copy(kn[:, t], banks[t][:]).then_inc(lin["k_copy"].handle, 1)
                for t in range(TT):
                    w(act, "q_turn", b * TT + (t + 1))
                    nc.scalar.copy(qT[:, t % 4, (t // 4) * HALF:(t // 4 + 1) * HALF], banks[t][:]).then_inc(lin["q_copy"].handle, 1)
                for t in range(TT):
                    w(act, "y", b * TT + (t + 1))
                    nc.scalar.copy(y[:, t], banks[t][:]).then_inc(lin["y_copy"].handle, 1)

        @block.tensor
        def _(pe):
            with pe.Fori(0, B) as b:
                w(pe, "k_norm", b + 1)
                for t in range(TT):
                    for kt in range(KT):
                        last = nc.tensor.transpose(banks[t][:, kt * P:(kt + 1) * P], ks[:, kt, t * P:(t + 1) * P], ident[:])
                    last.then_inc(lin["k_turn"].handle, 1)
                w(pe, "q_norm", b * 2 + 2)
                w(pe, "k_copy", b * TT + TT)
                for o in range(8):
                    h, kt = o // 4, o % 4
                    for z in range(4):
                        last = nc.tensor.transpose(banks[o][:, z * P:(z + 1) * P], q[:, h * 4 + z, kt * P:(kt + 1) * P], ident[:])
                    last.then_inc(lin["q_turn"].handle, 1)
                w(pe, "q_copy", b * TT + TT)
                for kt in range(KT):
                    for t in range(TT):
                        last = nc.tensor.matmul(banks[0][:, kt * P:(kt + 1) * P], v[:, t, kt * P:(kt + 1) * P],
                                                kn[:, t, kt * P:(kt + 1) * P], start=(t == 0), stop=(t == TT - 1))
                last.then_inc(lin["at"].handle, 1)
                w(pe, "at_copy", b + 1)
                for t in range(TT):
                    for kt in range(KT):
                        last = nc.tensor.matmul(banks[t][:, kt * P:(kt + 1) * P], qT[:, kt, t * P:(t + 1) * P],
                                                at[:, kt], start=True, stop=True)
                    last.then_inc(lin["y"].handle, 1)

    kv_in.stage_added(64 * B)
    core.input_free[0].stage_added(B)
    chain_v.stage_added(4 * B)


def ssm_inputs(core, cols, eps, io, scr, layer):
    nc = core.nc
    with ExitStack() as ctx:
        sb, psum = allocator(nc, ctx, f"ssmin{layer}")
        xp = [sb(f"xp{k}", [P, KC - 1 + T]) for k in range(2)]
        acc = [sb(f"acc{k}", [P, T]) for k in range(2)]
        u = sb("u", [P, IB, T])
        Wx = sb("Wx", [P, IB, R + 2 * NS])
        Wdt = sb("Wdt", [R, DI])
        xd = sb("xd", [R + 2 * NS, T])
        ea = [sb(f"ea{k}", [P, T]) for k in range(2)]
        dt = [sb(f"dt{k}", [P, T]) for k in range(2)]
        zs = [sb(f"zs{k}", [P, T]) for k in range(2)]
        X = psum("X", [R + 2 * NS, T])
        DTP = [psum(f"DTP{k}", [P, T]) for k in range(2)]
        c = {n: core.count("ssm_" + n) for n in ("x_in0", "x_in1", "conv", "u", "u_out", "proj", "proj_copy", "bc_out",
                                                 "dtp", "z", "relu", "log", "dt", "dt_out0", "dt_out1", "step")}
        w = lambda eng, n, value: eng.wait_ge(c[n].handle, c[n].at(value))
        col = lambda name, k: cols[:, COL_AT[name + str(layer)] + k:COL_AT[name + str(layer)] + k + 1]
        block = ctx.enter_context(nc.Block())

        @block.sync
        def _(sp):
            sp.dma_start(Wx[:], io[f"x_w{layer}"].rearrange("(k p) f -> p k f", p=P)).then_inc(core.consts_in.handle, 16)
            sp.dma_start(Wdt[:], io[f"dt_w{layer}"]).then_inc(core.consts_in.handle, 16)
            with sp.Fori(0, B) as b:
                for m in range(IB):
                    if m >= 2:
                        w(sp, "conv", b * IB + (m - 1))
                    else:
                        sp.wait_ge(core.input_free[m].handle, core.input_free[m].at(b))
                    sp.dma_start(xp[m % 2][:, KC - 1:], scr["xi"][b, :, m, :]).then_inc(c[f"x_in{m % 2}"].handle, 16)

        @block.vector
        def _(dve):
            for k in range(2):
                last = nc.vector.memset(xp[k][:, 0:KC - 1], 0.0)
            last.then_inc(core.vector_step.handle, 1)
            dve.wait_ge(core.vector_step.handle, core.vector_step.at(1))
            with dve.Fori(0, B) as b:
                for m in range(IB):
                    w(dve, f"x_in{m % 2}", b * 64 + (m // 2 + 1) * 16)
                    if m >= 2:
                        w(dve, "u", b * IB + (m - 1))
                    a, at = acc[m % 2], COL_AT[f"conv_w{layer}"] + KC * m
                    nc.vector.tensor_scalar(a[:], xp[m % 2][:, 0:T], cols[:, at:at + 1], None, ALU.mult
                                            ).then_inc(c["step"].handle, 1)
                    for k in range(1, KC):
                        w(dve, "step", b * (3 * IB) + (m * 3 + k))
                        ins = nc.vector.scalar_tensor_tensor(out=a[:], in0=xp[m % 2][:, k:k + T],
                                                             scalar=cols[:, at + k:at + k + 1], in1=a[:],
                                                             op0=ALU.mult, op1=ALU.add)
                        ins.then_inc(c["step" if k < KC - 1 else "conv"].handle, 1)
                w(dve, "conv", b * IB + IB)
                for k in range(2):
                    dve.sem_inc(core.input_free[k].handle, 1)
                for m in range(IB):
                    w(dve, "z", b * IB + (m + 1))
                    dve.wait_ge(core.stage_stored[m % 2].handle, core.stage_stored[m % 2].at(b * 64 + (m // 2) * 16))
                    nc.vector.tensor_scalar(dt[m % 2][:], zs[m % 2][:], 0.0, None, ALU.max).then_inc(c["relu"].handle, 1)
                    w(dve, "relu", b * IB + (m + 1))
                    w(dve, "log", b * IB + (m + 1))
                    nc.vector.tensor_tensor(dt[m % 2][:], dt[m % 2][:], ea[m % 2][:], ALU.add).then_inc(c["dt"].handle, 1)

        @block.scalar
        def _(act):
            step = core.scalar_step
            with act.Fori(0, B) as b:
                for m in range(IB):
                    w(act, "conv", b * IB + (m + 1))
                    if m == 0:
                        act.wait_ge(core.u_out.handle, core.u_out.at(b * (16 * IB)))
                    nc.scalar.activation(u[:, m], acc[m % 2][:], ACT.Silu, bias=col("conv_b", m)).then_inc(c["u"].handle, 1)
                    w(act, "u", b * IB + (m + 1))
                    act.dma_start(scr["u"][b, m], u[:, m]).then_inc(core.u_out.handle, 16)
                w(act, "proj", b + 1)
                act.wait_ge(core.u_out.handle, core.u_out.at(b * (16 * IB)))
                nc.scalar.copy(xd[:], X[:]).then_inc(c["proj_copy"].handle, 1)
                w(act, "proj_copy", b + 1)
                act.dma_start(scr["bc"][b], xd[R:, :]).then_inc(c["bc_out"].handle, 16)
                for m in range(IB):
                    w(act, "dtp", b * IB + (m + 1))
                    nc.scalar.activation(zs[m % 2][:], DTP[m % 2][:], ACT.Identity, bias=col("dt_b", m)).then_inc(c["z"].handle, 1)
                    w(act, "z", b * IB + (m + 1))
                    nc.scalar.activation(ea[m % 2][:], zs[m % 2][:], ACT.Abs).then_inc(step.handle, 1)
                    act.wait_ge(step.handle, step.at(b * (2 * IB) + (2 * m + 1)))
                    nc.scalar.activation(ea[m % 2][:], ea[m % 2][:], ACT.Exp, scale=-1.0).then_inc(step.handle, 1)
                    act.wait_ge(step.handle, step.at(b * (2 * IB) + (2 * m + 2)))
                    nc.scalar.activation(ea[m % 2][:], ea[m % 2][:], ACT.Ln, bias=eps[:, 2:3]).then_inc(c["log"].handle, 1)
                    w(act, "dt", b * IB + (m + 1))
                    act.dma_start(scr["dt"][b, m], dt[m % 2][:]).then_inc(core.stage_stored[m % 2].handle, 16)
                w(act, "bc_out", b * 16 + 16)
            act.wait_ge(core.u_out.handle, core.u_out.at(16 * IB * B))
            for k in range(2):
                act.wait_ge(core.stage_stored[k].handle, core.stage_stored[k].at(64 * B))

        @block.tensor
        def _(pe):
            pe.wait_ge(core.consts_in.handle, core.consts_in.at(32))
            with pe.Fori(0, B) as b:
                for m in range(IB):
                    w(pe, "u", b * IB + (m + 1))
                    for h in range(2):
                        last = nc.tensor.matmul(X[:, h * HALF:(h + 1) * HALF], Wx[:, m, :], u[:, m, h * HALF:(h + 1) * HALF],
                                                start=(m == 0), stop=(m == IB - 1))
                last.then_inc(c["proj"].handle, 1)
                w(pe, "proj_copy", b + 1)
                for m in range(IB):
                    if m >= 2:
                        w(pe, "z", b * IB + (m - 1))
                    for h in range(2):
                        last = nc.tensor.matmul(DTP[m % 2][:, h * HALF:(h + 1) * HALF], Wdt[:, m * P:(m + 1) * P],
                                                xd[0:R, h * HALF:(h + 1) * HALF], start=True, stop=True)
                    last.then_inc(c["dtp"].handle, 1)

    core.consts_in.stage_added(32)
    core.vector_step.stage_added(1)
    core.scalar_step.stage_added(2 * IB * B)
    core.u_out.stage_added(16 * IB * B)
    for k in range(2):
        core.input_free[k].stage_added(B)
        core.stage_stored[k].stage_added(64 * B)
        c[f"x_in{k}"].stage_added(64 * B)
    for n, per in (("conv", IB), ("u", IB), ("proj", 1), ("proj_copy", 1), ("bc_out", 16), ("dtp", IB), ("z", IB), ("relu", IB),
                   ("log", IB), ("dt", IB), ("step", 3 * IB)):
        c[n].stage_added(per * B)


def scan(core, ident, scr, layer):
    nc = core.nc
    with ExitStack() as ctx:
        sb, psum = allocator(nc, ctx, f"scan{layer}")
        Brep = sb("Brep", [P, NS, T])
        Crep = sb("Crep", [P, NS, T])
        two = lambda n, shape: [sb(f"{n}{k}", shape) for k in range(2)]
        dt, u, A, z = two("dt", [P, T]), two("u", [P, T]), two("A", [P, NS + 1]), two("z", [P, TT, P])
        dtu, uD, g = two("dtu", [P, T]), two("uD", [P, T]), two("g", [P, TT, P])
        drive, hC = two("drive", [P, T]), two("hC", [P, T])
        dAh = [psum(f"dAh{k}", [P, T]) for k in range(2)]
        yT = [psum(f"yT{k}", [P, TT, P]) for k in range(2)]
        scanned, scaled, turned, gated = core.scanned, core.scaled, core.unit_turned, core.gated
        decayed, driven, uD_ready = core.count("decayed"), core.count("driven"), core.count("uD_ready")
        y_full, dtu_ready = core.count("scan_y_full"), core.count("dtu_ready")
        in_, in_free = core.input_in, core.input_free
        def g_dst(pair, j):
            return scr["g"].rearrange("b m p k d -> (b m) p k d")[pair * 2 + j]

        PAIRS = IB // 2
        block = ctx.enter_context(nc.Block())

        @block.sync
        def _(sp):
            def load(b, m, j, use):
                sp.wait_ge(in_free[j].handle, in_free[j].at(use))
                core.apart(sp)
                for dst, src in ((dt[j][:], scr["dt"][b, m]), (u[j][:], scr["u"][b, m]),
                                 (A[j][:], scr["A"][layer - 2][m]),
                                 (z[j][:], scr["z"][b, :, bass.ds(m * P, P)].rearrange("(k p) d -> p k d", p=P))):
                    sp.dma_start(dst, src).then_inc(in_[j].handle, 16)

            with sp.Fori(0, B) as b:
                for j in range(2):
                    load(b, j, j, b * PAIRS)
                for n in range(NS):
                    sp.wait_ge(scaled.handle, scaled.at(b * (IB * NS) + (n + 1 - NS)))
                    sp.dma_start(Brep[:, n, :], scr["bc"][b, n:n + 1, :].broadcast_to([P, T])).then_inc(core.replica_in[n].handle, 16)
                    sp.dma_start(Crep[:, n, :], scr["bc"][b, NS + n:NS + n + 1, :].broadcast_to([P, T])
                                 ).then_inc(core.replica_in[n].handle, 16)
                with sp.Fori(1, PAIRS) as i:
                    for j in range(2):
                        load(b, i * 2 + j, j, b * PAIRS + i)

        @block.scalar
        def _(act):
            with act.Fori(0, B * PAIRS) as pair:
                for j in range(2):
                    act.wait_ge(in_[j].handle, in_[j].at(pair * 64 + 64))
                    act.wait_ge(y_full.handle, y_full.at(pair * 2 + (j - 1))) if j else None
                    nc.scalar.activation(uD[j][:], u[j][:], ACT.Copy, scale=A[j][:, NS:NS + 1]).then_inc(uD_ready.handle, 1)
                    for n in range(NS):
                        k = (pair * 2 + j) * NS + n
                        act.wait_ge(scaled.handle, scaled.at(k - 1))
                        nc.scalar.activation(dAh[n % 2][:], dt[j][:], ACT.Exp, scale=A[j][:, n:n + 1]
                                             ).then_inc(decayed.handle, 1)
                        if j == 1 and n == 6:
                            act.wait_ge(gated.handle, gated.at(pair * 2 + 1))
                            act.dma_start(g_dst(pair, 0), g[0][:]).then_inc(core.g_stored[0].handle, 16)
                act.wait_ge(gated.handle, gated.at(pair * 2 + 2))
                act.dma_start(g_dst(pair, 1), g[1][:]).then_inc(core.g_stored[1].handle, 16)
            for j in range(2):
                act.wait_ge(core.g_stored[j].handle, core.g_stored[j].at(16 * B * PAIRS))

        @block.gpsimd
        def _(pool):
            with pool.Fori(0, B) as b:
                core.apart(pool)
                with pool.Fori(0, PAIRS) as i:
                    pair = b * PAIRS + i
                    for j in range(2):
                        pool.wait_ge(in_[j].handle, in_[j].at(pair * 64 + 64))
                        nc.gpsimd.tensor_tensor(dtu[j][:], dt[j][:], u[j][:], ALU.mult).then_inc(dtu_ready.handle, 1)
                        pool.wait_ge(dtu_ready.handle, dtu_ready.at(pair * 2 + (j + 1)))
                        for n in range(NS):
                            k = (pair * 2 + j) * NS + n
                            pool.wait_ge(core.replica_in[n].handle, core.replica_in[n].at(b * 32 + 32))
                            pool.wait_ge(scanned.handle, scanned.at(k - 1))
                            nc.gpsimd.tensor_tensor(drive[n % 2][:], dtu[j][:], Brep[:, n, :], ALU.mult
                                                    ).then_inc(driven.handle, 1)

        @block.vector
        def _(dve):
            with dve.Fori(0, B) as b:
                core.apart(dve)
                with dve.Fori(0, PAIRS) as i:
                    pair = b * PAIRS + i

                    def gate(j):
                        dve.wait_ge(y_full.handle, y_full.at(pair * 2 + (j + 1)))
                        dve.wait_ge(core.g_stored[j].handle, core.g_stored[j].at(pair * 16))
                        nc.vector.tensor_tensor(g[j][:], yT[j][:], z[j][:], ALU.mult).then_inc(gated.handle, 1)
                        dve.wait_ge(gated.handle, gated.at(pair * 2 + (j + 1)))
                        dve.sem_inc(in_free[j].handle, 1)

                    for j in range(2):
                        dve.wait_ge(in_[j].handle, in_[j].at(pair * 64 + 64))
                        for n in range(NS):
                            k = (pair * 2 + j) * NS + n
                            dve.wait_ge(core.replica_in[n].handle, core.replica_in[n].at(b * 32 + 32))
                            dve.wait_ge(decayed.handle, decayed.at(k + 1))
                            dve.wait_ge(driven.handle, driven.at(k + 1))
                            nc.vector.tensor_tensor_scan(dAh[n % 2][:], dAh[n % 2][:], drive[n % 2][:], 0.0,
                                                         ALU.mult, ALU.add).then_inc(scanned.handle, 1)
                            dve.wait_ge(scanned.handle, scanned.at(k + 1))
                            dve.wait_ge(turned.handle, turned.at(k - 1))
                            nc.vector.tensor_tensor(hC[n % 2][:], dAh[n % 2][:], Crep[:, n, :], ALU.mult
                                                    ).then_inc(scaled.handle, 1)
                            if j == 1 and n == 2:
                                gate(0)
                    gate(1)

        @block.tensor
        def _(pe):
            with pe.Fori(0, B * PAIRS) as pair:
                for j in range(2):
                    pe.wait_ge(gated.handle, gated.at(pair * 2 + (j - 1)))
                    for n in range(NS + 1):
                        if n < NS:
                            pe.wait_ge(scaled.handle, scaled.at((pair * 2 + j) * NS + (n + 1)))
                        else:
                            pe.wait_ge(uD_ready.handle, uD_ready.at(pair * 2 + (j + 1)))
                        src = hC[n % 2] if n < NS else uD[j]
                        for t in range(TT):
                            last = nc.tensor.matmul(yT[j][:, t, :], src[:, t * P:(t + 1) * P], ident[:],
                                                    start=(n == 0 and t % 4 == 0), stop=(n == NS), is_transpose=True,
                                                    skip_group_check=True)
                        last.then_inc((turned if n < NS else y_full).handle, 1)

    units = B * IB * NS
    for cc in (scanned, scaled, turned, decayed, driven):
        cc.stage_added(units)
    for cc in (gated, uD_ready, y_full, dtu_ready):
        cc.stage_added(B * IB)
    for j in range(2):
        in_[j].stage_added(64 * B * PAIRS)
        in_free[j].stage_added(B * PAIRS)
        core.g_stored[j].stage_added(16 * B * PAIRS)
    for n in range(NS):
        core.replica_in[n].stage_added(32 * B)


def ssm_output(core, ident, io, scr, layer, residual, dst):
    nc = core.nc
    with ExitStack() as ctx:
        sb, psum = allocator(nc, ctx, f"ssmout{layer}")
        Wo = sb("Wo", [P, IB, D])
        gt = sb("gt", [P, D])
        two = lambda n, shape: [sb(f"{n}{k}", shape) for k in range(2)]
        g, gT, x, out = two("g", [P, IB, P]), two("gT", [P, IB, P]), two("x", [P, D]), two("out", [P, D])
        TP = [psum(f"TP{k}", [P, IB, P]) for k in range(2)]
        O = [psum(f"O{k}", [P, D]) for k in range(2)]
        c = {n: core.count("out_" + n) for n in ("gate_in", "turn", "copy", "mm", "step", "done")}
        w = lambda eng, n, value: eng.wait_ge(c[n].handle, c[n].at(value))
        n_in = 16 if residual is None else 32
        PAIRS = TT // 2
        block = ctx.enter_context(nc.Block())

        @block.sync
        def _(sp):
            sp.dma_start(Wo[:], io[f"out_w{layer}"].rearrange("(k p) f -> p k f", p=P)).then_inc(core.consts_in.handle, 16)
            with sp.Fori(0, B) as b:
                for j in range(2):
                    sp.wait_ge(core.input_free[j].handle, core.input_free[j].at(b * PAIRS))
                    core.apart(sp)
                sp.dma_start(gt[:], scr["gate"][layer - 2, bass.ds(b, 1), :].broadcast_to([P, D])).then_inc(c["gate_in"].handle, 16)
                with sp.Fori(0, PAIRS) as i:
                    for j in range(2):
                        sp.wait_ge(core.input_free[j].handle, core.input_free[j].at(b * PAIRS + i))
                        core.apart(sp)
                        sp.dma_start(g[j][:], scr["g"][b, :, :, i * 2 + j, :].rearrange("m p d -> p m d")
                                     ).then_inc(core.input_in[j].handle, 16)
                        if residual is not None:
                            sp.dma_start(x[j][:], residual[b, bass.ds((i * 2 + j) * P, P), :]).then_inc(core.input_in[j].handle, 16)

        @block.tensor
        def _(pe):
            pe.wait_ge(core.consts_in.handle, core.consts_in.at(16))
            with pe.Fori(0, B * PAIRS) as pair:
                for j in range(2):
                    pe.wait_ge(core.input_in[j].handle, core.input_in[j].at(pair * n_in + n_in))
                    pe.wait_ge(core.bank_free[j].handle, core.bank_free[j].at(pair))
                    for m in range(IB):
                        last = nc.tensor.transpose(TP[j][:, m, :], g[j][:, m, :], ident[:])
                    last.then_inc(c["turn"].handle, 1)
                for j in range(2):
                    w(pe, "copy", pair * 2 + (j + 1))
                    pe.wait_ge(core.input_free[j].handle, core.input_free[j].at(pair))
                    for m in range(IB):
                        last = nc.tensor.matmul(O[j][:], gT[j][:, m, :], Wo[:, m, :], start=(m == 0), stop=(m == IB - 1))
                    last.then_inc(c["mm"].handle, 1)

        @block.scalar
        def _(act):
            with act.Fori(0, B * PAIRS) as pair:
                for j in range(2):
                    w(act, "turn", pair * 2 + (j + 1))
                    act.wait_ge(core.input_free[j].handle, core.input_free[j].at(pair))
                    nc.scalar.copy(gT[j][:], TP[j][:]).then_inc(c["copy"].handle, 1)
                    w(act, "copy", pair * 2 + (j + 1))
                    act.sem_inc(core.bank_free[j].handle, 1)
                for j in range(2):
                    w(act, "done", pair * 2 + (j + 1))
                    act.dma_start(dst.rearrange("b t d -> (b t) d")[bass.ds((pair * 2 + j) * P, P), :], out[j][:]
                                  ).then_inc(core.stage_stored[j].handle, 16)
            for j in range(2):
                act.wait_ge(core.stage_stored[j].handle, core.stage_stored[j].at(16 * B * PAIRS))

        @block.vector
        def _(dve):
            with dve.Fori(0, B) as b:
                w(dve, "gate_in", b * 16 + 16)
                core.apart(dve)
                with dve.Fori(0, PAIRS) as i:
                    pair = b * PAIRS + i
                    for j in range(2):
                        w(dve, "mm", pair * 2 + (j + 1))
                        dve.wait_ge(core.stage_stored[j].handle, core.stage_stored[j].at(pair * 16))
                        ins = nc.vector.tensor_tensor(out[j][:], O[j][:], gt[:], ALU.mult)
                        if residual is not None:
                            ins.then_inc(c["step"].handle, 1)
                            w(dve, "step", pair * 2 + (j + 1))
                            ins = nc.vector.tensor_tensor(out[j][:], out[j][:], x[j][:], ALU.add)
                        ins.then_inc(c["done"].handle, 1)
                        w(dve, "done", pair * 2 + (j + 1))
                        dve.sem_inc(core.input_free[j].handle, 1)

    core.consts_in.stage_added(16)
    for j in range(2):
        core.input_in[j].stage_added(n_in * B * PAIRS)
        core.input_free[j].stage_added(B * PAIRS)
        core.bank_free[j].stage_added(B * PAIRS)
        core.bank_full[j].stage_added(0)
        core.stage_stored[j].stage_added(16 * B * PAIRS)
    c["gate_in"].stage_added(16 * B)
    for n in ("turn", "copy", "mm", "done"):
        c[n].stage_added(2 * B * PAIRS)
    if residual is not None:
        c["step"].stage_added(2 * B * PAIRS)


def gather_add(core, io, src, residual, dst):
    nc = core.nc
    with ExitStack() as ctx:
        sb, psum = allocator(nc, ctx, "gather")
        idx = sb("idx", [P, TT], I32)
        idx_b = sb("idx_b", [P, B, TT], I32)
        two = lambda n, shape: [sb(f"{n}{k}", shape) for k in range(2)]
        y, x = two("y", [P, TT, D]), two("x", [P, TT, D])
        idx_done, added = core.count("idx_done"), core.count("gather_added")
        rows_in = [core.count(f"gather_rows_in{k}") for k in range(2)]
        block = ctx.enter_context(nc.Block())

        @block.sync
        def _(sp):
            sp.dma_start(idx[:], io["perm"]).then_inc(core.consts_in.handle, 16)
            for b in range(B):
                sp.wait_ge(core.input_free[b % 2].handle, core.input_free[b % 2].at(b // 2))
                sp.dma_start(x[b % 2][:], residual[b].rearrange("(k p) d -> p k d", p=P)
                             ).then_inc(core.residual_in[b % 2].handle, 16)

        @block.gpsimd
        def _(pool):
            pool.wait_ge(idx_done.handle, idx_done.at(1))
            for b in range(B):
                pool.wait_ge(core.input_free[b % 2].handle, core.input_free[b % 2].at(b // 2))
                for k in range(TT):
                    pool.indirect_dma_start(y[b % 2][:, k, :], None, src.rearrange("b t d -> (b t) d"),
                                            bass.IndirectOffsetOnAxis(ap=idx_b[:, b, k:k + 1], axis=0)
                                            ).then_inc(rows_in[b % 2].handle, 16)

        @block.vector
        def _(dve):
            dve.wait_ge(core.consts_in.handle, core.consts_in.at(16))
            for b in range(B):
                last = nc.vector.tensor_scalar(idx_b[:, b, :], idx[:], float(b * T), None, ALU.add)
            last.then_inc(idx_done.handle, 1)
            for b in range(B):
                dve.wait_ge(rows_in[b % 2].handle, rows_in[b % 2].at((b // 2 + 1) * 16 * TT))
                dve.wait_ge(core.residual_in[b % 2].handle, core.residual_in[b % 2].at((b // 2 + 1) * 16))
                nc.vector.tensor_tensor(x[b % 2][:], x[b % 2][:], y[b % 2][:], ALU.add).then_inc(added.handle, 1)

        @block.scalar
        def _(act):
            for b in range(B):
                act.wait_ge(added.handle, added.at(b + 1))
                act.dma_start(dst[b].rearrange("(k p) d -> p k d", p=P), x[b % 2][:]
                              ).then_inc(core.stage_stored[b % 2].handle, 16)
                act.wait_ge(core.stage_stored[b % 2].handle, core.stage_stored[b % 2].at((b // 2 + 1) * 16))
                act.sem_inc(core.input_free[b % 2].handle, 1)


LAYERS = 4


def program(nc, io, out, kind="Internal"):
    scr = {}
    for name, shape in (("tab", [TABS, B, P, 8]), ("gate", [2, B, D]), ("keep", [2, B, P, TT]), ("A", [2, IB, P, NS + 1]),
                        ("xT", [B, P, KT, T]), ("qT", [B, P, KT, T]), ("kT", [B, P, KT, T]), ("q", [B, T, D]),
                        ("v", [B, T, D]), ("y", [B, T, D]), ("x1", [B, T, D]), ("x2", [B, T, D]), ("x3", [B, T, D]),
                        ("xi", [B, P, IB, T]), ("z", [B, T, DI]), ("u", [B, IB, P, T]), ("dt", [B, IB, P, T]),
                        ("bc", [B, 2 * NS, T]), ("g", [B, IB, P, TT, P])):
        scr[name] = nc.dram_tensor(f"scratch_{name}", shape, F32, kind=kind).ap()
    with ExitStack() as ctx:
        core = Core(nc, ctx)
        ident = ctx.enter_context(nc.sbuf_tensor("ident", [P, P], F32))
        eps = ctx.enter_context(nc.sbuf_tensor("eps", [P, 4], F32))
        cols = ctx.enter_context(nc.sbuf_tensor("column_tables", [P, NCOL], F32))
        give_credits(core, ident, eps)
        modulation(core, io, scr, cols)
        tab = scr["tab"]

        normalize(core, "n0", ident, eps, io["x"], tab[0], ACT.Identity, scr["xT"])
        project(core, "p0", io, cols, scr["xT"], [
            dict(kind="T", w=io["q_w"], n=D, col="q_b", dst=scr["qT"]),
            dict(kind="T", w=io["k_w"], n=D, col="k_b", dst=scr["kT"]),
            dict(kind="N", w=io["v_w"], n=D, row=0, keep=scr["keep"][0], dst=scr["v"])])
        attention(core, ident, io, scr)
        normalize(core, "n1", ident, eps, scr["y"], tab[1], ACT.Silu, scr["xT"])
        project(core, "p1", io, cols, scr["xT"], [
            dict(kind="N", w=io["out_w"], n=D, row=1, residual=io["x"], dst=scr["x1"])])

        normalize(core, "n2", ident, eps, scr["x1"], tab[2], ACT.Identity, scr["xT"])
        project(core, "p2", io, cols, scr["xT"], [
            dict(kind="T", w=io["Wk"], n=D, col="bk", dst=scr["kT"]),
            dict(kind="N", w=io["Wq"], n=D, row=2, dst=scr["q"]),
            dict(kind="N", w=io["Wv"], n=D, row=3, keep=scr["keep"][1], dst=scr["v"])])
        linear_attention(core, ident, io, scr)
        normalize(core, "n3", ident, eps, scr["y"], tab[3], ACT.Silu, scr["xT"])
        project(core, "p3", io, cols, scr["xT"], [
            dict(kind="N", w=io["film_out_W"], n=D, row=4, residual=scr["x1"], dst=scr["x2"])])

        for layer, x_in in ((2, scr["x2"]), (3, scr["x3"])):
            normalize(core, f"n{layer + 2}", ident, eps, x_in, tab[layer + 2], ACT.Identity, scr["xT"],
                      gather=io["perm"] if layer == 3 else None)
            project(core, f"p{layer + 2}", io, cols, scr["xT"], [
                dict(kind="T", w=io[f"in_wx{layer}"], n=DI, dst=scr["xi"]),
                dict(kind="N", w=io[f"in_wz{layer}"], n=DI, silu=True, dst=scr["z"])])
            ssm_inputs(core, cols, eps, io, scr, layer)
            scan(core, ident, scr, layer)
            if layer == 2:
                ssm_output(core, ident, io, scr, layer, scr["x2"], scr["x3"])
            else:
                ssm_output(core, ident, io, scr, layer, None, scr["y"])
        gather_add(core, io, scr["y"], scr["x3"], out)


def kernel(**inputs):
    import concourse.bacc as bacc
    from concourse.bass_utils import run_bass_kernel_spmd as run

    a = {k: np.asarray(v) for k, v in inputs.items()}
    l0 = {k[8:]: v for k, v in a.items() if k.startswith("L0_cond_")}
    l1 = {k[8:]: v for k, v in a.items() if k.startswith("L1_cond_")}
    l2 = {k[8:]: v for k, v in a.items() if k.startswith("L2_cond_")}
    l3 = {k[8:]: v for k, v in a.items() if k.startswith("L3_cond_")}

    def columns(v):
        return v.reshape(-1, P).T

    def tile_columns(v):
        return v.reshape(-1, P, v.shape[-1]).transpose(1, 0, 2).reshape(P, -1)

    col = dict(q_b=l0["q_b"], k_b=l0["k_b"], bk=l1["bk"], norm_w0=l0["norm_w"], norm_b0=l0["norm_b"],
               sb_w=l0["sb_norm_w"], sb_b=l0["sb_norm_b"], emb_b0=l0["emb_b"],
               norm_w1=l1["norm_scale"], norm_b1=l1["norm_bias"], film_w=l1["film_norm_scale"],
               film_b=l1["film_norm_bias"], emb_b1=l1["film_emb_b"],
               ln_g2=l2["ln_g"], ln_b2=l2["ln_b"], ada_b2=l2["ada_b"][:2 * D],
               ln_g3=l3["gamma"], ln_b3=l3["beta"], ada_b3=l3["b_ada"][:2 * D],
               conv_b2=l2["conv_b"], dt_b2=l2["dt_proj_b"], D2=l2["D_param"],
               conv_b3=l3["conv_b"], dt_b3=l3["b_dt"], D3=l3["D_param"])
    col = {k: columns(v) for k, v in col.items()}
    col.update(conv_w2=tile_columns(l2["conv_w"]), A_log2=tile_columns(l2["A_log"]),
               conv_w3=tile_columns(l3["conv_w"].reshape(DI, KC)), A_log3=tile_columns(l3["A_log"]))
    arrays = {
        "x": a["x"],
        "cols": np.concatenate([col[n] for n, _ in COLS], axis=1),
        "rows": np.stack([l0["v_b"], l0["out_b"], l1["bq"], l1["bv"], l1["film_out_b"],
                          l2["ada_b"][2 * D:], l3["b_ada"][2 * D:]]),
        "condT": a["cond_2048"].T,
        "mask0": a["mask_BxS_ff1"], "mask1": a["mask_BxS_ik0"],
        "mask0_cols": a["mask_BxS_ff1"].reshape(B, TT, P).transpose(2, 0, 1),
        "mask1_cols": a["mask_BxS_ik0"].reshape(B, TT, P).transpose(2, 0, 1),
        "perm": a["itok_S_0_1023"].reshape(TT, P).T,
        "emb_w0": l0["emb_w"], "emb_w1": l1["film_emb_W"], "ada_w2": l2["ada_w"].T, "ada_w3": l3["W_ada"],
        "q_w": l0["q_w"], "k_w": l0["k_w"], "v_w": l0["v_w"], "out_w": l0["out_w"],
        "Wq": l1["Wq"], "Wk": l1["Wk"], "Wv": l1["Wv"], "film_out_W": l1["film_out_W"],
        "in_wx2": l2["in_proj_w"][:DI].T, "in_wz2": l2["in_proj_w"][DI:].T,
        "in_wx3": l3["W_in"][:, :DI], "in_wz3": l3["W_in"][:, DI:],
        "x_w2": l2["x_proj_w"].T, "x_w3": l3["W_xp"], "dt_w2": l2["dt_proj_w"].T, "dt_w3": l3["W_dt"],
        "out_w2": l2["out_proj_w"].T, "out_w3": l3["W_out"],
    }
    arrays = {k: np.ascontiguousarray(v) for k, v in arrays.items()}
    nc = bacc.Bacc("TRN2", target_bir_lowering=False, num_devices=1)
    io = {k: nc.dram_tensor(k, v.shape, mybir.dt.from_np(v.dtype), kind="ExternalInput").ap() for k, v in arrays.items()}
    out = nc.dram_tensor("out", (B, T, D), F32, kind="ExternalOutput").ap()
    program(nc, io, out)
    return run(nc, [arrays], core_ids=[0]).results[0]["out"]
```

```python
from contextlib import ExitStack

import numpy as np
import concourse.bass as bass
from concourse import mybir

F32 = mybir.dt.float32
F32R = mybir.dt.float32r
I32 = mybir.dt.int32
ALU = mybir.AluOpType
ACT = mybir.ActivationFunctionType
AX = mybir.AxisListType

P = 128
B, T, D = 4, 1024, 512
E = 1024
H, DH = 16, 32
DI, NS, R, KC = 1024, 16, 64, 4
KT = D // P
TT = T // P
HALF = 512
IB = DI // P
ET = E // P
EPS = 1e-5
HUGE = 3.0e38

COLS = [("q_b", 4), ("k_b", 4), ("bk", 4),
        ("norm_w0", 4), ("norm_b0", 4), ("sb_w", 4), ("sb_b", 4), ("emb_b0", 8),
        ("norm_w1", 4), ("norm_b1", 4), ("film_w", 4), ("film_b", 4), ("emb_b1", 8),
        ("ln_g2", 4), ("ln_b2", 4), ("ada_b2", 8), ("ln_g3", 4), ("ln_b3", 4), ("ada_b3", 8),
        ("conv_b2", 8), ("dt_b2", 8), ("D2", 8), ("conv_w2", 32), ("A_log2", 128),
        ("conv_b3", 8), ("dt_b3", 8), ("D3", 8), ("conv_w3", 32), ("A_log3", 128)]
COL_AT, _n = {}, 0
for _name, _w in COLS:
    COL_AT[_name] = _n
    _n += _w
NCOL = _n
ROWS = ["v_b", "out_b0", "bq", "bv", "out_b1", "gate_b2", "gate_b3"]
TABS = 6


class Count:

    def __init__(self, handle, base):
        self.handle, self.base = handle, base

    def at(self, n):
        return n + self.base

    def stage_added(self, n):
        self.base += n


class Core:

    def __init__(self, nc, ctx):
        self.nc = nc
        sem = lambda name: ctx.enter_context(nc.semaphore(name))
        many = lambda name, n, base: [Count(sem(f"{name}{k}"), base) for k in range(n)]
        self.bank_full = many("bank_full", 8, 1)
        self.bank_free = many("bank_free", 8, 1)
        self.stage_stored = many("stage_stored", 8, 16)
        self.stage_full = many("stage_full", 8, 0)
        self.residual_in = many("residual_in", 8, 0)
        self.input_in = many("input_in", 2, 0)
        self.input_free = many("input_free", 2, 1)
        self.consts_in = Count(sem("consts_in"), 0)
        self.vector_step = Count(sem("vector_step"), 0)
        self.scalar_step = Count(sem("scalar_step"), 0)
        self.pool_step = Count(sem("pool_step"), 0)
        self.turned_out = many("turned_out", 2, 16)
        self.bc_taken = Count(sem("bc_taken"), 1)
        self.scanned = Count(sem("scanned"), 16)
        self.scaled = Count(sem("scaled"), 16)
        self.unit_turned = Count(sem("unit_turned"), 16)
        self.gated = Count(sem("gated"), 2)
        self.g_stored = many("g_stored", 2, 16)
        self.replica_in = many("replica_in", NS, 0)
        self.scored = Count(sem("scored"), 2 * H)
        self.weighed = Count(sem("weighed"), H)
        self.shifted = Count(sem("shifted"), 1)
        self.passed = Count(sem("passed"), 0)
        self.named = {}
        self._sem = sem

    def apart(self, engine):
        engine.sem_inc(self.passed.handle, 1)

    def count(self, name):
        if name not in self.named:
            self.named[name] = Count(self._sem(name), 0)
        return self.named[name]


class Chain:

    def __init__(self, engine, count, offset=0):
        self.engine, self.count, self.n, self.offset = engine, count, 0, offset

    def __call__(self, instruction):
        self.n += 1
        instruction.then_inc(self.count.handle, 1)
        self.engine.wait_ge(self.count.handle, self.count.at(self.n + self.offset))


def allocator(nc, ctx, stage):
    def sb(name, shape, dt=F32):
        return ctx.enter_context(nc.sbuf_tensor(f"{stage}_{name}", shape, dt))

    def psum(name, shape):
        return ctx.enter_context(nc.psum_tensor(f"{stage}_{name}", shape, F32))

    return sb, psum


def give_credits(core, ident, zero_eps):
    nc = core.nc
    ready = core.count("ident_ready")
    with nc.Block() as block:
        @block.vector
        def _(dve):
            for c in core.bank_full + core.bank_free + core.input_free:
                dve.sem_inc(c.handle, 1)
            for c in core.stage_stored:
                dve.sem_inc(c.handle, 16)
            for c in [core.bc_taken, core.scanned, core.scaled, core.unit_turned, core.gated,
                      core.scored, core.weighed, core.shifted] + core.g_stored + core.turned_out:
                dve.sem_inc(c.handle, c.base)
            nc.vector.memset(zero_eps[:, 0:1], EPS)
            nc.vector.memset(zero_eps[:, 1:2], 0.0)
            nc.vector.memset(zero_eps[:, 2:3], 1.0)

        @block.gpsimd
        def _(pool):
            nc.gpsimd.memset(ident[:], 0.0).then_inc(ready.handle, 1)
            pool.wait_ge(ready.handle, 1)
            nc.gpsimd.affine_select(out=ident[:], in_=ident[:], compare_op=ALU.not_equal, fill=1.0,
                                    base=0, pattern=[[-1, P]], channel_multiplier=1)


def modulation(core, io, scr, cols):
    nc = core.nc
    with ExitStack() as ctx:
        sb, psum = allocator(nc, ctx, "mod")
        W = [sb(f"W{k}", [P, ET, 3 * D]) for k in range(2)]
        condT = sb("condT", [P, ET, B])
        silu_cT = sb("silu_cT", [P, ET, B])
        gate_bias = sb("gate_bias", [B, 2, D])
        gates = sb("gates", [B, 2, D])
        tab = sb("tab", [P, TABS, B, 8])
        e = sb("e", [P, 4, 8, B])
        part = sb("part", [P, 4, KT, B])
        mask0 = sb("mask0", [P, B, TT])
        mask1 = sb("mask1", [P, B, TT], I32)
        keep = sb("keep", [P, 2, B, TT])
        A = sb("A", [P, 2, IB, NS + 1])
        ps = [psum(f"ps{k}", [P, 8 * B]) for k in range(2)]
        pg = psum("pg", [B, D])
        w_in, w_free = core.input_in, core.input_free
        silu_done, mm_done = core.count("silu_done"), core.count("mod_mm_done")
        dve_done, act_done = core.count("mod_dve_done"), core.count("mod_act_done")
        widths = [2 * D, 2 * D, 3 * D, 3 * D]
        w_src = [io["emb_w0"], io["emb_w1"], io["ada_w2"], io["ada_w3"]]
        block = ctx.enter_context(nc.Block())
        col = lambda name, k, n=1: cols[:, COL_AT[name] + k:COL_AT[name] + k + n]

        @block.sync
        def _(sp):
            ci = core.consts_in.handle
            sp.dma_start(cols[:], io["cols"]).then_inc(ci, 16)
            sp.dma_start(condT[:], io["condT"].rearrange("(k p) b -> p k b", p=P)).then_inc(ci, 16)
            sp.dma_start(gate_bias[:], io["rows"][5:7, :].rearrange("(o r) d -> o r d", o=1)
                         .broadcast_to([B, 2, D])).then_inc(ci, 16)
            sp.dma_start(mask0[:], io["mask0_cols"]).then_inc(ci, 16)
            sp.dma_start(mask1[:], io["mask1_cols"]).then_inc(ci, 16)
            for l in range(4):
                if l >= 2:
                    sp.wait_ge(w_free[l % 2].handle, w_free[l % 2].at(1))
                sp.dma_start(W[l % 2][:, :, 0:widths[l]],
                             w_src[l].rearrange("(k p) f -> p k f", p=P)).then_inc(w_in[l % 2].handle, 16)
            out = core.count("tables_out")
            sp.wait_ge(dve_done.handle, dve_done.at(1))
            sp.wait_ge(act_done.handle, act_done.at(1))
            for t in range(TABS):
                sp.dma_start(scr["tab"][t].rearrange("b p e -> p b e"), tab[:, t]).then_inc(out.handle, 16)
            sp.dma_start(scr["gate"].rearrange("l b d -> b l d"), gates[:]).then_inc(out.handle, 16)
            for l in range(2):
                sp.dma_start(scr["keep"][l].rearrange("b p e -> p b e"), keep[:, l]).then_inc(out.handle, 16)
                sp.dma_start(scr["A"][l].rearrange("i p e -> p i e"), A[:, l]).then_inc(out.handle, 16)
            sp.wait_ge(out.handle, out.at(16 * (TABS + 5)))

        @block.scalar
        def _(act):
            act.wait_ge(core.consts_in.handle, core.consts_in.at(80))
            nc.scalar.activation(silu_cT[:], condT[:], ACT.Silu).then_inc(silu_done.handle, 1)
            for l in range(2):
                last = nc.scalar.activation(A[:, l, :, 0:NS],
                                            col(f"A_log{l + 2}", 0, 128).rearrange("p (i n) -> p i n", n=NS), ACT.Exp)
            last.then_inc(core.scalar_step.handle, 1)
            act.wait_ge(core.scalar_step.handle, core.scalar_step.at(1))
            for l in range(2):
                nc.scalar.mul(A[:, l, :, 0:NS], A[:, l, :, 0:NS], -1.0)
                last = nc.scalar.copy(A[:, l, :, NS], col(f"D{l + 2}", 0, 8))
            last.then_inc(act_done.handle, 1)

        @block.tensor
        def _(pe):
            pe.wait_ge(silu_done.handle, silu_done.at(1))
            for l in range(4):
                pe.wait_ge(w_in[l % 2].handle, w_in[l % 2].at(16 * (l // 2 + 1)))
                if l >= 1:
                    pe.wait_ge(core.count("mod_read").handle, core.count("mod_read").at(l))
                for f in range(8):
                    for k in range(ET):
                        last = nc.tensor.matmul(ps[l % 2][:, f * B:(f + 1) * B], W[l % 2][:, k, f * P:(f + 1) * P],
                                                silu_cT[:, k, :], start=(k == 0), stop=(k == ET - 1))
                if l >= 2:
                    for k in range(ET):
                        last = nc.tensor.matmul(pg[:], silu_cT[:, k, :], W[l % 2][:, k, 2 * D:3 * D],
                                                start=(k == 0), stop=(k == ET - 1))
                last.then_inc(mm_done.handle, 1)

        @block.vector
        def _(dve):
            read = core.count("mod_read")
            step = Chain(dve, core.vector_step)
            dve.wait_ge(core.consts_in.handle, core.consts_in.at(80))
            nc.vector.tensor_copy(keep[:, 0], mask0[:])
            nc.vector.tensor_scalar(keep[:, 1], mask1[:], 1.0, None, ALU.not_equal)
            for t, w, b in ((0, "norm_w0", "norm_b0"), (2, "norm_w1", "norm_b1")):
                for bb in range(B):
                    nc.vector.tensor_copy(tab[:, t, bb, 0:4], col(w, 0, 4))
                    nc.vector.tensor_copy(tab[:, t, bb, 4:8], col(b, 0, 4))
            for l in range(4):
                t, w, b, bias = ((1, "sb_w", "sb_b", "emb_b0"), (3, "film_w", "film_b", "emb_b1"),
                                 (4, "ln_g2", "ln_b2", "ada_b2"), (5, "ln_g3", "ln_b3", "ada_b3"))[l]
                scale0, shift0 = (0, 4) if l < 2 else (4, 0)
                dve.wait_ge(mm_done.handle, mm_done.at(l + 1))
                for f in range(8):
                    last = nc.vector.tensor_scalar(e[:, l, f], ps[l % 2][:, f * B:(f + 1) * B], col(bias, f), None, ALU.add)
                if l >= 2:
                    last = nc.vector.tensor_tensor(gates[:, l - 2], pg[:], gate_bias[:, l - 2], ALU.add)
                last.then_inc(read.handle, 1)
                dve.wait_ge(read.handle, read.at(l + 1))
                if l < 2:
                    dve.sem_inc(w_free[l % 2].handle, 1)
                for k in range(KT):
                    nc.vector.tensor_scalar(tab[:, t, :, k], e[:, l, scale0 + k], 1.0, col(w, k), ALU.add, ALU.mult)
                    last = nc.vector.tensor_scalar(part[:, l, k], e[:, l, scale0 + k], 1.0, col(b, k), ALU.add, ALU.mult)
                step(last)
                for k in range(KT):
                    last = nc.vector.tensor_tensor(tab[:, t, :, 4 + k], part[:, l, k], e[:, l, shift0 + k], ALU.add)
            last.then_inc(dve_done.handle, 1)

    core.consts_in.stage_added(80)
    for k in range(2):
        w_in[k].stage_added(32)
        w_free[k].stage_added(1)
    core.vector_step.stage_added(4)
    core.scalar_step.stage_added(1)


def normalize(core, name, ident, eps, src, tab, func, dst, gather=None):
    nc = core.nc
    with ExitStack() as ctx:
        sb, psum = allocator(nc, ctx, name)
        x = [sb(f"x{k}", [P, TT, D]) for k in range(2)]
        tb = [sb(f"tb{k}", [P, 8]) for k in range(2)]
        xh = sb("xh", [P, TT, D])
        xT = [sb(f"xT{k}", [P, KT, T]) for k in range(2)]
        st = sb("st", [P, TT, 6])
        mv = sb("mv", [P, TT, 2])
        lv = sb("lv", [P, TT])
        rstd = sb("rstd", [P, TT])
        banks = [psum(f"bank{k}", [P, HALF]) for k in range(8)]
        stats_done, rstd_done = core.count("stats_done"), core.count("rstd_done")
        xhat_done, turned_out = core.count("xhat_done"), core.turned_out
        evacuated = core.count("turned_in_sbuf")
        xs_in, xs_free = core.input_in, core.input_free
        full, free = core.bank_full, core.bank_free
        if gather is not None:
            idx = sb("idx", [P, TT], I32)
            idx_b = sb("idx_b", [P, B, TT], I32)
            idx_done = core.count("idx_done")
        block = ctx.enter_context(nc.Block())
        n_in = 32 if gather is None else 16
        rows_in = None if gather is None else [core.count(f"{name}_rows_in{k}") for k in range(2)]

        def load_rows(eng, it, j, u):
            eng.wait_ge(xs_free[j].handle, xs_free[j].at(u))
            eng.dma_start(tb[j][:], tab[it]).then_inc(xs_in[j].handle, 16)
            eng.dma_start(x[j][:], src[it].rearrange("(k p) d -> p k d", p=P)).then_inc(xs_in[j].handle, 16)

        if gather is None:
            @block.sync
            def _(sp):
                with sp.Fori(0, B // 2) as i:
                    for j in range(2):
                        load_rows(sp, i * 2 + j, j, i)
        else:
            @block.sync
            def _(sp):
                sp.dma_start(idx[:], gather).then_inc(core.consts_in.handle, 16)
                for it in range(B):
                    j = it % 2
                    sp.wait_ge(xs_free[j].handle, xs_free[j].at(it // 2))
                    sp.dma_start(tb[j][:], tab[it]).then_inc(xs_in[j].handle, 16)

            @block.gpsimd
            def _(pool):
                pool.wait_ge(idx_done.handle, idx_done.at(1))
                for it in range(B):
                    j = it % 2
                    pool.wait_ge(xs_free[j].handle, xs_free[j].at(it // 2))
                    for k in range(TT):
                        pool.indirect_dma_start(x[j][:, k, :], None, src.rearrange("b t d -> (b t) d"),
                                                bass.IndirectOffsetOnAxis(ap=idx_b[:, it, k:k + 1], axis=0)
                                                ).then_inc(rows_in[j].handle, 16)

        @block.vector
        def _(dve):
            if gather is not None:
                dve.wait_ge(core.consts_in.handle, core.consts_in.at(16))
                for it in range(B):
                    last = nc.vector.tensor_scalar(idx_b[:, it, :], idx[:], float(it * T), None, ALU.add)
                last.then_inc(idx_done.handle, 1)
            with dve.Fori(0, B // 2) as i:
                for j in range(2):
                    it = i * 2 + j
                    dve.wait_ge(xs_in[j].handle, xs_in[j].at(i * n_in + n_in))
                    if gather is not None:
                        dve.wait_ge(rows_in[j].handle, rows_in[j].at(i * (16 * TT) + 16 * TT))
                    for k in range(TT):
                        last = nc.vector.bn_stats(st[:, k, :], x[j][:, k, :])
                    last.then_inc(core.vector_step.handle, 1)
                    dve.wait_ge(core.vector_step.handle, core.vector_step.at(it + 1))
                    core.apart(dve)
                    for k in range(TT):
                        last = nc.vector.bn_aggr(mv[:, k, :], st[:, k, :])
                    last.then_inc(stats_done.handle, 1)
                    dve.wait_ge(rstd_done.handle, rstd_done.at(it + 1))
                    for k in range(TT):
                        if k == 0:
                            for o in range(8):
                                dve.wait_ge(full[o].handle, full[o].at(it))
                        ins = nc.vector.tensor_scalar(xh[:, k, :], x[j][:, k, :], mv[:, k, 0:1], rstd[:, k:k + 1],
                                                      ALU.subtract, ALU.mult)
                        if k % 4 == 3:
                            ins.then_inc(xhat_done.handle, 1)
                    dve.wait_ge(xhat_done.handle, xhat_done.at(it * 2 + 2))
                    dve.wait_ge(evacuated.handle, evacuated.at(it * 8 + 8))
                    dve.sem_inc(xs_free[j].handle, 1)

        @block.scalar
        def _(act):
            with act.Fori(0, B // 2) as i:
                for j in range(2):
                    it = i * 2 + j
                    act.wait_ge(stats_done.handle, stats_done.at(it + 1))
                    nc.scalar.activation(lv[:], mv[:, :, 1], ACT.Ln, bias=eps[:, 0:1]).then_inc(core.scalar_step.handle, 1)
                    act.wait_ge(core.scalar_step.handle, core.scalar_step.at(it + 1))
                    nc.scalar.activation(rstd[:], lv[:], ACT.Exp, scale=-0.5).then_inc(rstd_done.handle, 1)
                    act.wait_ge(turned_out[j].handle, turned_out[j].at(i * 16))
                    for h in range(2):
                        for kt in range(KT):
                            o = h * KT + kt
                            act.wait_ge(full[o].handle, full[o].at(it + 1))
                            nc.scalar.activation(xT[j][:, kt, h * HALF:(h + 1) * HALF], banks[o][:], func,
                                                 scale=tb[j][:, kt:kt + 1], bias=tb[j][:, 4 + kt:5 + kt]
                                                 ).then_inc(evacuated.handle, 1)
                            act.wait_ge(evacuated.handle, evacuated.at(it * 8 + (o + 1)))
                            act.sem_inc(free[o].handle, 1)
                    act.dma_start(dst[it], xT[j][:]).then_inc(turned_out[j].handle, 16)
            for j in range(2):
                act.wait_ge(turned_out[j].handle, turned_out[j].at(8 * B))

        @block.tensor
        def _(pe):
            with pe.Fori(0, B // 2) as i:
                for j in range(2):
                    it = i * 2 + j
                    for h in range(2):
                        pe.wait_ge(xhat_done.handle, xhat_done.at(it * 2 + (h + 1)))
                        for kt in range(KT):
                            o = h * KT + kt
                            pe.wait_ge(free[o].handle, free[o].at(it))
                            for q in range(4):
                                last = nc.tensor.transpose(banks[o][:, q * P:(q + 1) * P],
                                                           xh[:, h * 4 + q, kt * P:(kt + 1) * P], ident[:])
                            last.then_inc(full[o].handle, 1)

    for k in range(2):
        xs_in[k].stage_added(n_in * B // 2)
        xs_free[k].stage_added(B // 2)
    for o in range(8):
        full[o].stage_added(B)
        free[o].stage_added(B)
    core.vector_step.stage_added(B)
    core.scalar_step.stage_added(B)
    stats_done.stage_added(B)
    rstd_done.stage_added(B)
    xhat_done.stage_added(2 * B)
    evacuated.stage_added(8 * B)
    for j in range(2):
        turned_out[j].stage_added(8 * B)
    if gather is not None:
        core.consts_in.stage_added(16)
        idx_done.stage_added(1)


def project(core, name, io, cols, src, jobs):
    nc = core.nc
    with ExitStack() as ctx:
        sb, psum = allocator(nc, ctx, name)
        xT = [sb(f"xT{k}", [P, KT, T]) for k in range(2)]
        W = [sb(f"W{n}", [P, KT, job["n"]]) for n, job in enumerate(jobs)]
        row = [sb(f"row{n}", [P, D]) if job.get("row") is not None else None for n, job in enumerate(jobs)]
        kp = [sb(f"keep{k}", [P, TT]) for k in range(2)]
        keep = next((job["keep"] for job in jobs if job.get("keep") is not None), None)
        has_res = any(job.get("residual") is not None for job in jobs)
        res = [sb(f"res{k}", [P, D]) for k in range(8)] if has_res else None
        split = jobs[0].get("split", False)
        stage = None if split else [sb(f"stage{k}", [P, HALF]) for k in range(8)]
        parts = [sb(f"parts{k}", [P, 2 * HALF]) for k in range(8)] if split else None
        whole = sb("whole", [P, HALF]) if split else None
        hi_done = core.count("hi_done")

        def part_of(k8, n, s):
            if jobs[n]["kind"] == "T":
                return parts[k8][:, s * HALF:(s + 1) * HALF]
            return parts[k8][:].rearrange("p (h s e) -> p h s e", s=2, e=DH)[:, :, s]

        banks = [psum(f"bank{k}", [P, HALF]) for k in range(8)]
        outs = []
        for n, job in enumerate(jobs):
            if job["kind"] == "T":
                outs += [(n, m, h) for m in range(job["n"] // P) for h in range(2)]
            else:
                outs += [(n, f, t) for t in range(TT) for f in range(job["n"] // D)]
        uses = len(outs) // 8
        full, free = core.bank_full, core.bank_free
        staged, stored = core.stage_full, core.stage_stored
        chained = lambda n: jobs[n].get("keep") is not None or jobs[n].get("residual") is not None
        steps = sum((3 if split else 1) for n, _, _ in outs if chained(n))
        n_T = sum(1 for n, _, _ in outs if jobs[n]["kind"] == "T")
        n_const = 16 * (len(jobs) + sum(r is not None for r in row))
        n_in = 16 if keep is None else 32
        block = ctx.enter_context(nc.Block())

        def on_scalar(n):
            return jobs[n]["kind"] == "T"

        @block.tensor
        def _(pe):
            pe.wait_ge(core.consts_in.handle, core.consts_in.at(n_const))
            with pe.Fori(0, B // 2) as i:
                for j in range(2):
                    pe.wait_ge(core.input_in[j].handle, core.input_in[j].at(i * n_in + n_in))
                    for o, (n, a, b) in enumerate(outs):
                        k8 = o % 8
                        pe.wait_ge(free[k8].handle, free[k8].at((i * 2 + j) * uses + o // 8))
                        for kt in range(KT):
                            if jobs[n]["kind"] == "T":
                                lhs, rhs = W[n][:, kt, a * P:(a + 1) * P], xT[j][:, kt, b * HALF:(b + 1) * HALF]
                            else:
                                lhs, rhs = xT[j][:, kt, b * P:(b + 1) * P], W[n][:, kt, a * D:(a + 1) * D]
                            last = nc.tensor.matmul(banks[k8][:], lhs, rhs, start=(kt == 0), stop=(kt == KT - 1))
                        last.then_inc(full[k8].handle, 1)
                        if o == len(outs) - 1:
                            pe.wait_ge(full[k8].handle, full[k8].at((i * 2 + j) * uses + uses))
                    if keep is not None:
                        kv = [o for o, (n, _, _) in enumerate(outs) if jobs[n].get("keep") is not None][-1]
                        pe.wait_ge(staged[kv % 8].handle, staged[kv % 8].at((i * 2 + j) * uses + (kv // 8 + 1)))
                    pe.sem_inc(core.input_free[j].handle, 1)

        @block.scalar
        def _(act):
            with act.Fori(0, B // 2) as i:
                for j in range(2):
                    for o, (n, a, b) in enumerate(outs):
                        if not on_scalar(n):
                            continue
                        k8, u = o % 8, (i * 2 + j) * uses + o // 8
                        act.wait_ge(full[k8].handle, full[k8].at(u + 1))
                        act.wait_ge(stored[k8].handle, stored[k8].at(u * 16))
                        at = COL_AT[jobs[n]["col"]] + a
                        result = part_of(k8, n, 0).bitcast(F32R) if split else stage[k8][:]
                        ins = nc.scalar.activation(result, banks[k8][:], ACT.Identity, bias=cols[:, at:at + 1])
                        if split:
                            ins.then_inc(hi_done.handle, 1)
                            continue
                        ins.then_inc(staged[k8].handle, 1)
                        act.wait_ge(staged[k8].handle, staged[k8].at(u + 1))
                        act.sem_inc(free[k8].handle, 1)

        @block.vector
        def _(dve):
            if n_const:
                dve.wait_ge(core.consts_in.handle, core.consts_in.at(n_const))
            with dve.Fori(0, B // 2) as i:
                for j in range(2):
                    done = turned = 0
                    if keep is not None:
                        dve.wait_ge(core.input_in[j].handle, core.input_in[j].at(i * n_in + n_in))
                    for o, (n, a, b) in enumerate(outs):
                        k8, u = o % 8, (i * 2 + j) * uses + o // 8
                        job = jobs[n]
                        if on_scalar(n):
                            if split:
                                turned += 1
                                at = COL_AT[job["col"]] + a
                                dve.wait_ge(hi_done.handle, hi_done.at((i * 2 + j) * n_T + turned))
                                nc.vector.scalar_tensor_tensor(part_of(k8, n, 1).bitcast(F32R), banks[k8][:], cols[:, at:at + 1],
                                                               part_of(k8, n, 0), ALU.add, ALU.subtract
                                                               ).then_inc(staged[k8].handle, 1)
                                dve.wait_ge(staged[k8].handle, staged[k8].at(u + 1))
                                dve.sem_inc(free[k8].handle, 1)
                            continue
                        dve.wait_ge(full[k8].handle, full[k8].at(u + 1))
                        dve.wait_ge(stored[k8].handle, stored[k8].at(u * 16))
                        value = whole if split else stage[k8]
                        ins = nc.vector.tensor_tensor(value[:], banks[k8][:], row[n][:], ALU.add)
                        if job.get("keep") is not None or job.get("residual") is not None:
                            done += 1
                            ins.then_inc(core.vector_step.handle, 1)
                            dve.wait_ge(core.vector_step.handle, core.vector_step.at((i * 2 + j) * steps + done))
                            if job.get("keep") is not None:
                                ins = nc.vector.tensor_scalar(value[:], value[:], kp[j][:, b:b + 1], None, ALU.mult)
                            else:
                                dve.wait_ge(core.residual_in[k8].handle, core.residual_in[k8].at(u * 16 + 16))
                                ins = nc.vector.tensor_tensor(stage[k8][:], stage[k8][:], res[k8][:], ALU.add)
                        if split:
                            step = lambda n_: core.vector_step.at((i * 2 + j) * steps + n_)
                            ins.then_inc(core.vector_step.handle, 1)
                            dve.wait_ge(core.vector_step.handle, step(done + 1))
                            by_head = whole[:].rearrange("p (h e) -> p h e", e=DH)
                            nc.vector.tensor_copy(part_of(k8, n, 0).bitcast(F32R), by_head).then_inc(core.vector_step.handle, 1)
                            dve.wait_ge(core.vector_step.handle, step(done + 2))
                            ins = nc.vector.tensor_tensor(part_of(k8, n, 1).bitcast(F32R), by_head, part_of(k8, n, 0), ALU.subtract)
                            done += 2
                        ins.then_inc(staged[k8].handle, 1)
                        dve.wait_ge(staged[k8].handle, staged[k8].at(u + 1))
                        dve.sem_inc(free[k8].handle, 1)

        @block.sync
        def _(sp):
            def load(it):
                j = it % 2
                sp.wait_ge(core.input_free[j].handle, core.input_free[j].at(it // 2))
                sp.dma_start(xT[j][:], src[it]).then_inc(core.input_in[j].handle, 16)
                if keep is not None:
                    sp.dma_start(kp[j][:], keep[it]).then_inc(core.input_in[j].handle, 16)

            for n, job in enumerate(jobs):
                sp.dma_start(W[n][:], job["w"].rearrange("(k p) f -> p k f", p=P)).then_inc(core.consts_in.handle, 16)
                if row[n] is not None:
                    sp.dma_start(row[n][:], io["rows"][job["row"]:job["row"] + 1, :].broadcast_to([P, D])
                                 ).then_inc(core.consts_in.handle, 16)
            load(0)
            load(1)
            for it in range(B):
                if has_res:
                    for k in range(8):
                        sp.wait_ge(free[k].handle, free[k].at(it * uses))
                        sp.dma_start(res[k][:], jobs[0]["residual"][it, k * P:(k + 1) * P, :]
                                     ).then_inc(core.residual_in[k].handle, 16)
                for o, (n, a, b) in enumerate(outs):
                    k8, u = o % 8, it * uses + o // 8
                    job = jobs[n]
                    sp.wait_ge(staged[k8].handle, staged[k8].at(u + 1))
                    if job["kind"] == "T" and split:
                        tile = parts[k8][:].rearrange("p (s t) -> p s t", s=2)
                        dst = job["dst"][it, :, a * P:(a + 1) * P, b * HALF:(b + 1) * HALF].rearrange("s p t -> p s t")
                    elif job["kind"] == "T":
                        tile, dst = stage[k8][:], job["dst"][it, :, a, b * HALF:(b + 1) * HALF]
                    else:
                        tile = parts[k8][:] if split else stage[k8][:]
                        width = tile.shape[1]
                        dst = job["dst"][it, b * P:(b + 1) * P, a * width:(a + 1) * width]
                    sp.dma_start(dst, tile).then_inc(stored[k8].handle, 16)
                if it + 2 < B:
                    load(it + 2)
            for k in range(8):
                sp.wait_ge(stored[k].handle, stored[k].at(16 * B * uses))

    core.consts_in.stage_added(n_const)
    for k in range(2):
        core.input_in[k].stage_added(n_in * B // 2)
        core.input_free[k].stage_added(B // 2)
    for k in range(8):
        full[k].stage_added(B * uses)
        free[k].stage_added(B * uses)
        staged[k].stage_added(B * uses)
        stored[k].stage_added(16 * B * uses)
        if has_res:
            core.residual_in[k].stage_added(16 * B)
    core.vector_step.stage_added(B * steps)
    if split:
        hi_done.stage_added(B * n_T)


def attention(core, ident, io, scr):
    nc = core.nc
    with ExitStack() as ctx:
        sb, psum = allocator(nc, ctx, "att")
        k = sb("k", [P, H, T])
        v = sb("v", [P, TT, H, 2 * DH])
        mrow = sb("mrow", [P, T])
        mneg = sb("mneg", [P, T])
        fold = sb("fold", [2 * DH, DH])
        q = [sb(f"q{j}", [P, H, P]) for j in range(2)]
        sm = [sb(f"sm{j}", [P, T]) for j in range(2)]
        nmax = [sb(f"nmax{j}", [P, 1]) for j in range(2)]
        pr = [sb(f"pr{j}", [P, T]) for j in range(2)]
        psums = sb("psums", [P, 2 * H])
        pT = [[sb(f"pT{part}{j}", [P, T]) for j in range(2)] for part in ("hi", "lo")]
        rden = sb("rden", [P, 4])
        yts = sb("yts", [2 * DH, 4, P])
        y = [sb(f"y{j}", [P, H, DH]) for j in range(2)]
        S = [psum(f"S{j}", [P, T]) for j in range(2)]
        TP = psum("TP", [P, T])
        YT = psum("YT", [2 * DH, 4, P])
        Y = psum("Y", [P, 4, DH])
        C = H // 4
        k_in, v_in = ([core.count(f"{n}_chunk_in{c}") for c in range(C)] for n in "kv")
        mask_in, mneg_ready, fold_ready = core.count("mask_in"), core.count("mneg_ready"), core.count("fold_ready")
        q_in = core.input_in
        scored, shifted, weighed = core.scored, core.shifted, core.weighed
        exped, turned = core.count("exped"), core.count("turned")
        hi_copied, lo_taken = core.count("hi_copied"), core.count("lo_taken")
        y_ready, yt_copied, y_turned = core.count("y_ready"), core.count("yt_copied"), core.count("y_turned")
        y_stored = core.stage_stored
        G = 8
        U = 2 * H
        PAIRS = TT // 2
        BU = TT * H
        block = ctx.enter_context(nc.Block())

        @block.sync
        def _(sp):
            def load_k(b, c):
                sp.wait_ge(scored.handle, scored.at(b * BU + (4 * c + 4 - H)))
                for g, part in enumerate((0, 1, 0, 1)):
                    sp.dma_start(k[DH * g:DH * g + DH, 4 * c:4 * c + 4, :],
                                 scr["k_split"][b, part].rearrange("(h e) t -> e h t", e=DH)[:, 4 * c:4 * c + 4, :]
                                 ).then_inc(k_in[c].handle, 16)

            def load_v(b, c):
                sp.wait_ge(weighed.handle, weighed.at(b * BU + (4 * c + 4 - H)))
                sp.dma_start(v[:, :, 4 * c:4 * c + 4, :],
                             scr["v_split"][b].rearrange("(k p) (h e) -> p k h e", p=P, e=2 * DH)[:, :, 4 * c:4 * c + 4, :]
                             ).then_inc(v_in[c].handle, 16)

            def load_q(b, i, j):
                sp.wait_ge(scored.handle, scored.at((b * PAIRS + i) * U + (H * (j + 1) - U)))
                for g, part in enumerate((0, 0, 1, 1)):
                    sp.dma_start(q[j][DH * g:DH * g + DH, :, :],
                                 scr["q_split"][b, part, :, bass.ds((i * 2 + j) * P, P)]
                                 .rearrange("(h e) t -> e h t", e=DH)).then_inc(q_in[j].handle, 16)

            with sp.Fori(0, B) as b:
                sp.wait_ge(mneg_ready.handle, mneg_ready.at(b))
                sp.dma_start(mrow[:], io["mask0"][bass.ds(b, 1), :].broadcast_to([P, T])).then_inc(mask_in.handle, 16)
                load_k(b, 0)
                load_k(b, 1)
                load_v(b, 0)
                load_k(b, 2)
                load_v(b, 1)
                load_k(b, 3)
                load_v(b, 2)
                for j in range(2):
                    load_q(b, 0, j)
                load_v(b, 3)
                core.apart(sp)
                with sp.Fori(1, PAIRS) as i:
                    for j in range(2):
                        load_q(b, i, j)

        @block.gpsimd
        def _(pool):
            with pool.Fori(0, B) as b:
                pool.wait_ge(mask_in.handle, mask_in.at(b * 16 + 16))
                pool.wait_ge(shifted.handle, shifted.at(b * BU))
                core.apart(pool)
                nc.gpsimd.tensor_scalar(mneg[:], mrow[:], 1.0, 1.0e6, ALU.subtract, ALU.mult
                                        ).then_inc(mneg_ready.handle, 1)

        @block.tensor
        def _(pe):
            pe.wait_ge(fold_ready.handle, fold_ready.at(1))
            with pe.Fori(0, B) as b:
                core.apart(pe)
                with pe.Fori(0, PAIRS) as i:
                    pair = b * PAIRS + i
                    base = pair * U

                    def scores(u):
                        j, h = u // H, u % H
                        if h == 0:
                            pe.wait_ge(q_in[j].handle, q_in[j].at(pair * 64 + 64))
                        if u < H and h % 4 == 0:
                            pe.wait_ge(k_in[h // 4].handle, k_in[h // 4].at(b * 64 + 64))
                        if u >= 2:
                            pe.wait_ge(shifted.handle, shifted.at(base + (u - 1)))
                        for c in range(2):
                            last = nc.tensor.matmul(S[u % 2][:, c * HALF:(c + 1) * HALF], q[j][:, h, :].bitcast(F32R),
                                                    k[:, h, c * HALF:(c + 1) * HALF].bitcast(F32R), start=True, stop=True)
                        last.then_inc(scored.handle, 1)

                    def turn(u):
                        pe.wait_ge(exped.handle, exped.at(base + (u + 1)))
                        for half in range(2):
                            if u >= 1:
                                pe.wait_ge(lo_taken.handle, lo_taken.at(base * 2 + (2 * u - 1 + half)))
                            for m in range(4 * half, 4 * half + 4):
                                last = nc.tensor.transpose(TP[:, m * P:(m + 1) * P], pr[u % 2][:, m * P:(m + 1) * P], ident[:])
                            last.then_inc(turned.handle, 1)

                    def weigh(u):
                        g, h = u // 4, u % H
                        pe.wait_ge(lo_taken.handle, lo_taken.at(base * 2 + (2 * u + 2)))
                        if u < H and h % 4 == 0:
                            pe.wait_ge(v_in[h // 4].handle, v_in[h // 4].at(b * 16 + 16))
                        if u % 4 == 0 and g >= 1:
                            pe.wait_ge(yt_copied.handle, yt_copied.at(pair * G + g))
                        for m in range(TT):
                            for part in range(2):
                                last = nc.tensor.matmul(YT[:, h % 4, :], v[:, m, h, :].bitcast(F32R),
                                                        pT[part][u % 2][:, m * P:(m + 1) * P].bitcast(F32R),
                                                        start=(m == 0 and part == 0), stop=(m == TT - 1 and part == 1))
                        last.then_inc(weighed.handle, 1)

                    def turn_back(g):
                        pe.wait_ge(yt_copied.handle, yt_copied.at(pair * G + (g + 1)))
                        if g >= 1:
                            pe.wait_ge(y_ready.handle, y_ready.at(pair * G + g))
                        core.apart(pe)
                        for n in range(4):
                            last = nc.tensor.matmul(Y[:, n, :], yts[:, n, :], fold[:], start=True, stop=True)
                        last.then_inc(y_turned.handle, 1)

                    scores(0)
                    scores(1)
                    for u in range(U):
                        if u + 2 < U:
                            scores(u + 2)
                        turn(u)
                        if u >= 1:
                            weigh(u - 1)
                        if u >= 6 and u % 4 == 2:
                            turn_back((u - 6) // 4)
                    weigh(U - 1)
                    turn_back(G - 1)
                    pe.wait_ge(y_ready.handle, y_ready.at(pair * G + G))

        @block.vector
        def _(dve):
            nc.vector.tensor_tensor(fold[:], ident[0:2 * DH, 0:DH], ident[0:2 * DH, DH:2 * DH], ALU.add
                                    ).then_inc(fold_ready.handle, 1)
            with dve.Fori(0, B) as b:
                dve.wait_ge(mneg_ready.handle, mneg_ready.at(b + 1))
                core.apart(dve)
                with dve.Fori(0, PAIRS) as i:
                    pair = b * PAIRS + i
                    base = pair * U

                    def shift(u):
                        dve.wait_ge(scored.handle, scored.at(base + (u + 1)))
                        if u >= 2:
                            dve.wait_ge(exped.handle, exped.at(base + (u - 1)))
                        core.apart(dve)
                        nc.vector.tensor_tensor_reduce(sm[u % 2][:], S[u % 2][:], mneg[:], -1.0, HUGE,
                                                       ALU.add, ALU.min, nmax[u % 2][:]).then_inc(shifted.handle, 1)

                    def take_lo(u):
                        for half in range(2):
                            cols_ = slice(half * HALF, (half + 1) * HALF)
                            dve.wait_ge(hi_copied.handle, hi_copied.at(base * 2 + (2 * u + half + 1)))
                            nc.vector.tensor_tensor(pT[1][u % 2][:, cols_].bitcast(F32R), TP[:, cols_],
                                                    pT[0][u % 2][:, cols_], ALU.subtract).then_inc(lo_taken.handle, 1)

                    def copy_yt(g):
                        dve.wait_ge(weighed.handle, weighed.at(base + (4 * g + 4)))
                        if g >= 1:
                            dve.wait_ge(y_turned.handle, y_turned.at(pair * G + g))
                        nc.vector.tensor_copy(yts[:], YT[:]).then_inc(yt_copied.handle, 1)

                    def take(g):
                        j, h = g // 4, (g % 4) * 4
                        dve.wait_ge(y_turned.handle, y_turned.at(pair * G + (g + 1)))
                        nc.vector.reciprocal(rden[:], psums[:, 4 * g:4 * g + 4]).then_inc(core.vector_step.handle, 1)
                        dve.wait_ge(core.vector_step.handle, core.vector_step.at(pair * G + (g + 1)))
                        if h == 0:
                            dve.wait_ge(y_stored[j].handle, y_stored[j].at(pair * 16))
                        nc.vector.tensor_tensor(y[j][:, h:h + 4, :], Y[:],
                                                rden[:].unsqueeze(2).broadcast_to([P, 4, DH]), ALU.mult
                                                ).then_inc(y_ready.handle, 1)

                    shift(0)
                    shift(1)
                    for u in range(U):
                        if u >= 1:
                            take_lo(u - 1)
                        if u >= 5 and u % 4 == 1:
                            copy_yt((u - 5) // 4)
                        if u + 2 < U:
                            shift(u + 2)
                        if u >= 8 and u % 4 == 0:
                            take((u - 8) // 4)
                    take_lo(U - 1)
                    for g in range(G - 2, G):
                        if g == G - 1:
                            copy_yt(g)
                        take(g)

        @block.scalar
        def _(act):
            with act.Fori(0, B * PAIRS) as pair:
                base = pair * U

                def copy_hi(u):
                    if u >= 2:
                        act.wait_ge(weighed.handle, weighed.at(base + (u - 1)))
                    for half in range(2):
                        cols_ = slice(half * HALF, (half + 1) * HALF)
                        act.wait_ge(turned.handle, turned.at(base * 2 + (2 * u + half + 1)))
                        nc.scalar.copy(pT[0][u % 2][:, cols_].bitcast(F32R), TP[:, cols_]).then_inc(hi_copied.handle, 1)

                for u in range(U):
                    act.wait_ge(shifted.handle, shifted.at(base + (u + 1)))
                    if u >= 2:
                        act.wait_ge(turned.handle, turned.at(base * 2 + (2 * u - 2)))
                    nc.scalar.activation(pr[u % 2][:], sm[u % 2][:], ACT.Exp, bias=nmax[u % 2][:, 0:1], scale=-1.0,
                                         accum_out=psums[:, u:u + 1]).then_inc(exped.handle, 1)
                    if u >= 1:
                        copy_hi(u - 1)
                    if u == U - 1:
                        copy_hi(u)
                    if u in (H + 8, U - 1):
                        j = 0 if u == H + 8 else 1
                        act.wait_ge(y_ready.handle, y_ready.at(pair * G + (j * 4 + 4)))
                        act.dma_start(scr["y"].rearrange("b t d -> (b t) d")[bass.ds((pair * 2 + j) * P, P), :],
                                      y[j][:].rearrange("p h e -> p (h e)")).then_inc(y_stored[j].handle, 16)
            for j in range(2):
                act.wait_ge(y_stored[j].handle, y_stored[j].at(16 * B * PAIRS))

    n = B * TT * H
    for c in (scored, shifted, exped, weighed):
        c.stage_added(n)
    for j in range(2):
        q_in[j].stage_added(64 * B * PAIRS)
        y_stored[j].stage_added(16 * B * PAIRS)
    core.vector_step.stage_added(4 * B * TT)


def linear_attention(core, ident, io, scr):
    nc = core.nc
    with ExitStack() as ctx:
        sb, psum = allocator(nc, ctx, "lin")
        kT = sb("kT", [P, KT, T])
        q = sb("q", [P, TT, D])
        v = sb("v", [P, TT, D])
        mi = sb("mi", [P, T], I32)
        mneg = sb("mneg", [P, T])
        ks = sb("ks", [P, KT, T])
        nmax = sb("nmax", [P, KT])
        ksum = sb("ksum", [P, KT])
        kr = sb("kr", [P, KT])
        kn = sb("kn", [P, TT, D])
        qmax = sb("qmax", [P, TT * H])
        qsum = sb("qsum", [P, TT * H])
        qr = sb("qr", [P, TT * H])
        qT = sb("qT", [P, KT, T])
        at = sb("at", [P, KT, P])
        y = sb("y", [P, TT, D])
        banks = [psum(f"bank{k}", [P, HALF]) for k in range(8)]
        kv_in = core.count("kv_in")
        chain_v, chain_a = core.vector_step, core.scalar_step
        lin = {n: core.count("lin_" + n) for n in ("k_shift", "k_exp", "k_norm", "q_shift", "q_exp", "q_norm",
                                                   "k_turn", "k_copy", "q_turn", "q_copy", "at", "at_copy",
                                                   "y", "y_copy", "stored")}
        w = lambda eng, n, value: eng.wait_ge(lin[n].handle, value)
        block = ctx.enter_context(nc.Block())

        @block.sync
        def _(sp):
            with sp.Fori(0, B) as b:
                sp.wait_ge(core.input_free[0].handle, core.input_free[0].at(b))
                sp.dma_start(kT[:], scr["kT"][b]).then_inc(kv_in.handle, 16)
                sp.dma_start(mi[:], io["mask1"][bass.ds(b, 1), :].broadcast_to([P, T])).then_inc(kv_in.handle, 16)
                sp.dma_start(q[:], scr["q"][b].rearrange("(k p) d -> p k d", p=P)).then_inc(kv_in.handle, 16)
                sp.dma_start(v[:], scr["v"][b].rearrange("(k p) d -> p k d", p=P)).then_inc(kv_in.handle, 16)
                w(sp, "y_copy", b * TT + TT)
                sp.dma_start(scr["y"][b].rearrange("(k p) d -> p k d", p=P), y[:]).then_inc(lin["stored"].handle, 16)
                w(sp, "stored", b * 16 + 16)
                sp.sem_inc(core.input_free[0].handle, 1)

        @block.vector
        def _(dve):
            nc.vector.memset(at[:], 0.0)
            with dve.Fori(0, B) as b:
                dve.wait_ge(kv_in.handle, kv_in.at(b * 64 + 64))
                nc.vector.tensor_scalar(mneg[:], mi[:], 1.0, -HUGE, ALU.is_equal, ALU.mult).then_inc(chain_v.handle, 1)
                dve.wait_ge(chain_v.handle, chain_v.at(b * 4 + 1))
                core.apart(dve)
                for kt in range(KT):
                    nc.vector.tensor_tensor_reduce(ks[:, kt], kT[:, kt], mneg[:], -1.0, HUGE, ALU.add, ALU.min,
                                                   nmax[:, kt:kt + 1]).then_inc(lin["k_shift"].handle, 1)
                qv = q[:].rearrange("p k (h e) -> p (k h) e", e=DH)
                wide = lambda x: x[:].unsqueeze(2).broadcast_to([P, TT * H, DH])
                nc.vector.tensor_reduce(qmax[:], qv, AX.X, ALU.max).then_inc(chain_v.handle, 1)
                dve.wait_ge(chain_v.handle, chain_v.at(b * 4 + 2))
                nc.vector.tensor_tensor(qv, qv, wide(qmax), ALU.subtract).then_inc(lin["q_shift"].handle, 1)
                w(dve, "k_exp", b * KT + KT)
                nc.vector.reciprocal(kr[:], ksum[:]).then_inc(chain_v.handle, 1)
                dve.wait_ge(chain_v.handle, chain_v.at(b * 4 + 3))
                for kt in range(KT):
                    last = nc.vector.tensor_scalar(ks[:, kt], ks[:, kt], kr[:, kt:kt + 1], None, ALU.mult)
                last.then_inc(lin["k_norm"].handle, 1)
                w(dve, "q_exp", b + 1)
                nc.vector.tensor_reduce(qsum[:], qv, AX.X, ALU.add).then_inc(chain_v.handle, 1)
                dve.wait_ge(chain_v.handle, chain_v.at(b * 4 + 4))
                nc.vector.reciprocal(qr[:], qsum[:]).then_inc(lin["q_norm"].handle, 1)
                w(dve, "q_norm", b * 2 + 1)
                nc.vector.tensor_tensor(qv, qv, wide(qr), ALU.mult).then_inc(lin["q_norm"].handle, 1)
                w(dve, "at", b + 1)
                for g in range(4):
                    r = slice(32 * g, 32 * g + 32)
                    last = nc.vector.tensor_copy(at[r, :, r], banks[0][:].rearrange("p (k e) -> p k e", e=P)[r, :, r])
                last.then_inc(lin["at_copy"].handle, 1)

        @block.scalar
        def _(act):
            with act.Fori(0, B) as b:
                for kt in range(KT):
                    w(act, "k_shift", b * KT + (kt + 1))
                    nc.scalar.activation(ks[:, kt], ks[:, kt], ACT.Exp, bias=nmax[:, kt:kt + 1], scale=-1.0,
                                         accum_out=ksum[:, kt:kt + 1]).then_inc(lin["k_exp"].handle, 1)
                w(act, "q_shift", b + 1)
                nc.scalar.activation(q[:], q[:], ACT.Exp).then_inc(lin["q_exp"].handle, 1)
                for t in range(TT):
                    w(act, "k_turn", b * TT + (t + 1))
                    nc.scalar.copy(kn[:, t], banks[t][:]).then_inc(lin["k_copy"].handle, 1)
                for t in range(TT):
                    w(act, "q_turn", b * TT + (t + 1))
                    nc.scalar.copy(qT[:, t % 4, (t // 4) * HALF:(t // 4 + 1) * HALF], banks[t][:]).then_inc(lin["q_copy"].handle, 1)
                for t in range(TT):
                    w(act, "y", b * TT + (t + 1))
                    nc.scalar.copy(y[:, t], banks[t][:]).then_inc(lin["y_copy"].handle, 1)

        @block.tensor
        def _(pe):
            with pe.Fori(0, B) as b:
                w(pe, "k_norm", b + 1)
                for t in range(TT):
                    for kt in range(KT):
                        last = nc.tensor.transpose(banks[t][:, kt * P:(kt + 1) * P], ks[:, kt, t * P:(t + 1) * P], ident[:])
                    last.then_inc(lin["k_turn"].handle, 1)
                w(pe, "q_norm", b * 2 + 2)
                w(pe, "k_copy", b * TT + TT)
                for o in range(8):
                    h, kt = o // 4, o % 4
                    for z in range(4):
                        last = nc.tensor.transpose(banks[o][:, z * P:(z + 1) * P], q[:, h * 4 + z, kt * P:(kt + 1) * P], ident[:])
                    last.then_inc(lin["q_turn"].handle, 1)
                w(pe, "q_copy", b * TT + TT)
                for kt in range(KT):
                    for t in range(TT):
                        last = nc.tensor.matmul(banks[0][:, kt * P:(kt + 1) * P], v[:, t, kt * P:(kt + 1) * P],
                                                kn[:, t, kt * P:(kt + 1) * P], start=(t == 0), stop=(t == TT - 1))
                last.then_inc(lin["at"].handle, 1)
                w(pe, "at_copy", b + 1)
                for t in range(TT):
                    for kt in range(KT):
                        last = nc.tensor.matmul(banks[t][:, kt * P:(kt + 1) * P], qT[:, kt, t * P:(t + 1) * P],
                                                at[:, kt], start=True, stop=True)
                    last.then_inc(lin["y"].handle, 1)

    kv_in.stage_added(64 * B)
    core.input_free[0].stage_added(B)
    chain_v.stage_added(4 * B)


def ssm_inputs(core, cols, eps, io, scr, layer):
    nc = core.nc
    with ExitStack() as ctx:
        sb, psum = allocator(nc, ctx, f"ssmin{layer}")
        two = lambda n, shape: [sb(f"{n}{k}", shape) for k in range(2)]
        xT = two("xT", [P, KT, T])
        Wx, Wz = sb("Wx", [P, KT, DI]), sb("Wz", [P, KT, DI])
        Wp, Wdt = sb("Wp", [P, IB, R + 2 * NS]), sb("Wdt", [R, DI])
        xp, acc = two("xp", [P, KC - 1 + T]), two("acc", [P, T])
        u = sb("u", [P, IB, T])
        xd = sb("xd", [R + 2 * NS, T])
        zs, ea, dt, dtu, uD = (two(n, [P, T]) for n in ("zs", "ea", "dt", "dtu", "uD"))
        zt = [sb(f"zt{k}", [P, HALF]) for k in range(2)]
        ring = [psum(f"ring{k}", [P, HALF]) for k in range(4)]
        X = psum("X", [R + 2 * NS, T])
        DTP = psum("DTP", [P, T])
        c = {n: core.count("ssm_" + n) for n in ("x_evac", "conv", "u", "proj", "proj_copy", "bc_out", "dtp", "z", "relu",
                                                 "log", "dt", "dtu", "uD", "zt", "step")}
        w = lambda eng, n, value: eng.wait_ge(c[n].handle, c[n].at(value))
        col = lambda name, k: cols[:, COL_AT[name + str(layer)] + k:COL_AT[name + str(layer)] + k + 1]
        full, free = core.bank_full, core.bank_free
        dt_out, dtbc_taken, uD_out, z_out = (core.stage_stored[2 * k:2 * k + 2] for k in range(4))
        Z_FIRST = 8
        outs = [("x", m, h) for m in range(IB) for h in range(2)] + [("z", t, f) for t in range(TT) for f in range(2)]
        USES = len(outs) // 4
        block = ctx.enter_context(nc.Block())

        @block.sync
        def _(sp):
            for dst, src in ((Wx, io[f"in_wx{layer}"]), (Wz, io[f"in_wz{layer}"]), (Wp, io[f"x_w{layer}"])):
                sp.dma_start(dst[:], src.rearrange("(k p) f -> p k f", p=P)).then_inc(core.consts_in.handle, 16)
            sp.dma_start(Wdt[:], io[f"dt_w{layer}"]).then_inc(core.consts_in.handle, 16)

            def load(it):
                sp.wait_ge(core.input_free[it % 2].handle, core.input_free[it % 2].at(it // 2))
                sp.dma_start(xT[it % 2][:], scr["xT"][it]).then_inc(core.input_in[it % 2].handle, 16)

            def store_z(it, o):
                _, t, f = outs[o]
                n = o - 2 * IB
                w(sp, "zt", it * 16 + (n + 1))
                sp.dma_start(scr["z"][it, t * P:(t + 1) * P, f * HALF:(f + 1) * HALF], zt[n % 2][:]
                             ).then_inc(z_out[n % 2].handle, 16)

            load(0)
            load(1)
            for it in range(B):
                for m in range(IB):
                    w(sp, "uD", it * IB + (m + 1))
                    sp.dma_start(scr["uD"][it, m], uD[m % 2][:]).then_inc(uD_out[m % 2].handle, 16)
                for n in range(Z_FIRST):
                    store_z(it, 2 * IB + n)
                w(sp, "proj_copy", it + 1)
                sp.dma_start(scr["bc"][it], xd[R:, :]).then_inc(c["bc_out"].handle, 16)
                for m in range(IB):
                    store_z(it, 2 * IB + Z_FIRST + m)
                    w(sp, "dt", it * IB + (m + 1))
                    sp.dma_start(scr["dt"][it, m], dt[m % 2][:]).then_inc(dt_out[m % 2].handle, 16)
                    w(sp, "dtu", it * IB + (m + 1))
                    sp.dma_start(scr["dtu"][it, m], dtu[m % 2][:]).then_inc(dtbc_taken[m % 2].handle, 16)
                if it + 2 < B:
                    load(it + 2)
            for k in range(2):
                for stores, n in ((dt_out, 64), (dtbc_taken, 64), (uD_out, 64), (z_out, 128)):
                    sp.wait_ge(stores[k].handle, stores[k].at(n * B))
            w(sp, "bc_out", 16 * B)

        @block.tensor
        def _(pe):
            pe.wait_ge(core.consts_in.handle, core.consts_in.at(64))
            with pe.Fori(0, B // 2) as i:
                for j in range(2):
                    it = i * 2 + j

                    def product(o):
                        kind, a, h = outs[o]
                        pe.wait_ge(free[o % 4].handle, free[o % 4].at(it * USES + o // 4))
                        for kt in range(KT):
                            if kind == "x":
                                lhs, rhs = Wx[:, kt, a * P:(a + 1) * P], xT[j][:, kt, h * HALF:(h + 1) * HALF]
                            else:
                                lhs, rhs = xT[j][:, kt, a * P:(a + 1) * P], Wz[:, kt, h * HALF:(h + 1) * HALF]
                            last = nc.tensor.matmul(ring[o % 4][:], lhs, rhs, start=(kt == 0), stop=(kt == KT - 1))
                        last.then_inc(full[o % 4].handle, 1)

                    pe.wait_ge(core.input_in[j].handle, core.input_in[j].at(i * 16 + 16))
                    for o in range(2 * IB + Z_FIRST):
                        product(o)
                    for m in range(IB):
                        w(pe, "u", it * IB + (m + 1))
                        for h in range(2):
                            last = nc.tensor.matmul(X[:, h * HALF:(h + 1) * HALF], Wp[:, m, :],
                                                    u[:, m, h * HALF:(h + 1) * HALF], start=(m == 0), stop=(m == IB - 1))
                    last.then_inc(c["proj"].handle, 1)
                    for m in range(IB):
                        product(2 * IB + Z_FIRST + m)
                        if m == 0:
                            w(pe, "proj_copy", it + 1)
                        if m >= 1:
                            w(pe, "z", it * IB + m)
                        for h in range(2):
                            last = nc.tensor.matmul(DTP[:, h * HALF:(h + 1) * HALF], Wdt[:, m * P:(m + 1) * P],
                                                    xd[0:R, h * HALF:(h + 1) * HALF], start=True, stop=True)
                        last.then_inc(c["dtp"].handle, 1)
                    w(pe, "z", it * IB + IB)
                    pe.sem_inc(core.input_free[j].handle, 1)

        @block.scalar
        def _(act):
            step = core.scalar_step
            with act.Fori(0, B // 2) as i:
                for j in range(2):
                    it = i * 2 + j

                    def take_z(n):
                        o = 2 * IB + n
                        act.wait_ge(full[o % 4].handle, full[o % 4].at(it * USES + (o // 4 + 1)))
                        act.wait_ge(z_out[n % 2].handle, z_out[n % 2].at(it * 128 + (n // 2) * 16))
                        nc.scalar.activation(zt[n % 2][:], ring[o % 4][:], ACT.Silu).then_inc(c["zt"].handle, 1)
                        w(act, "zt", it * 16 + (n + 1))
                        act.sem_inc(free[o % 4].handle, 1)

                    def take_x(m):
                        if m >= 2:
                            w(act, "conv", it * IB + (m - 1))
                        for h in range(2):
                            o = 2 * m + h
                            act.wait_ge(full[o % 4].handle, full[o % 4].at(it * USES + (o // 4 + 1)))
                            nc.scalar.copy(xp[m % 2][:, KC - 1 + h * HALF:KC - 1 + (h + 1) * HALF], ring[o % 4][:]
                                           ).then_inc(c["x_evac"].handle, 1)
                            w(act, "x_evac", it * (2 * IB) + (o + 1))
                            act.sem_inc(free[o % 4].handle, 1)

                    def make_u(m):
                        w(act, "conv", it * IB + (m + 1))
                        nc.scalar.activation(u[:, m], acc[m % 2][:], ACT.Silu, bias=col("conv_b", m)).then_inc(c["u"].handle, 1)
                        w(act, "u", it * IB + (m + 1))
                        act.wait_ge(uD_out[m % 2].handle, uD_out[m % 2].at(it * 64 + (m // 2) * 16))
                        nc.scalar.activation(uD[m % 2][:], u[:, m], ACT.Copy, scale=col("D", m)).then_inc(c["uD"].handle, 1)

                    for m in range(IB):
                        take_x(m)
                        if m >= 1:
                            make_u(m - 1)
                    make_u(IB - 1)
                    for n in range(Z_FIRST):
                        take_z(n)
                    w(act, "proj", it + 1)
                    act.wait_ge(core.bc_taken.handle, core.bc_taken.at(it))
                    nc.scalar.copy(xd[:], X[:]).then_inc(c["proj_copy"].handle, 1)
                    for m in range(IB):
                        take_z(Z_FIRST + m)
                        w(act, "dtp", it * IB + (m + 1))
                        if m >= 2:
                            w(act, "dt", it * IB + (m - 1))
                        nc.scalar.activation(zs[m % 2][:], DTP[:], ACT.Identity, bias=col("dt_b", m)).then_inc(c["z"].handle, 1)
                        w(act, "z", it * IB + (m + 1))
                        nc.scalar.activation(ea[m % 2][:], zs[m % 2][:], ACT.Abs).then_inc(step.handle, 1)
                        act.wait_ge(step.handle, step.at(it * (2 * IB) + (2 * m + 1)))
                        nc.scalar.activation(ea[m % 2][:], ea[m % 2][:], ACT.Exp, scale=-1.0).then_inc(step.handle, 1)
                        act.wait_ge(step.handle, step.at(it * (2 * IB) + (2 * m + 2)))
                        nc.scalar.activation(ea[m % 2][:], ea[m % 2][:], ACT.Ln, bias=eps[:, 2:3]).then_inc(c["log"].handle, 1)
                    w(act, "dt", it * IB + IB)
                    w(act, "bc_out", it * 16 + 16)
                    act.sem_inc(core.bc_taken.handle, 1)

        @block.vector
        def _(dve):
            for k in range(2):
                last = nc.vector.memset(xp[k][:, 0:KC - 1], 0.0)
            last.then_inc(core.vector_step.handle, 1)
            dve.wait_ge(core.vector_step.handle, core.vector_step.at(1))
            with dve.Fori(0, B // 2) as i:
                for j in range(2):
                    it = i * 2 + j
                    for m in range(IB):
                        w(dve, "x_evac", it * (2 * IB) + (2 * m + 2))
                        if m >= 2:
                            w(dve, "u", it * IB + (m - 1))
                        a, at = acc[m % 2], COL_AT[f"conv_w{layer}"] + KC * m
                        nc.vector.tensor_scalar(a[:], xp[m % 2][:, 0:T], cols[:, at:at + 1], None, ALU.mult
                                                ).then_inc(c["step"].handle, 1)
                        for k in range(1, KC):
                            w(dve, "step", it * (3 * IB) + (m * 3 + k))
                            ins = nc.vector.scalar_tensor_tensor(out=a[:], in0=xp[m % 2][:, k:k + T],
                                                                 scalar=cols[:, at + k:at + k + 1], in1=a[:],
                                                                 op0=ALU.mult, op1=ALU.add)
                            ins.then_inc(c["step" if k < KC - 1 else "conv"].handle, 1)
                    for m in range(IB):
                        dve.wait_ge(dt_out[m % 2].handle, dt_out[m % 2].at(it * 64 + (m // 2) * 16))
                        dve.wait_ge(dtbc_taken[m % 2].handle, dtbc_taken[m % 2].at(it * 64 + (m // 2) * 16))
                        w(dve, "z", it * IB + (m + 1))
                        nc.vector.tensor_scalar(dt[m % 2][:], zs[m % 2][:], 0.0, None, ALU.max).then_inc(c["relu"].handle, 1)
                        w(dve, "relu", it * IB + (m + 1))
                        w(dve, "log", it * IB + (m + 1))
                        nc.vector.tensor_tensor(dt[m % 2][:], dt[m % 2][:], ea[m % 2][:], ALU.add).then_inc(c["dt"].handle, 1)
                        w(dve, "dt", it * IB + (m + 1))
                        nc.vector.tensor_tensor(dtu[m % 2][:], dt[m % 2][:], u[:, m], ALU.mult).then_inc(c["dtu"].handle, 1)

    core.consts_in.stage_added(64)
    core.vector_step.stage_added(1)
    core.scalar_step.stage_added(2 * IB * B)
    core.bc_taken.stage_added(B)
    for k in range(2):
        core.input_in[k].stage_added(16 * B // 2)
        core.input_free[k].stage_added(B // 2)
        for stores, n in ((dt_out, 64), (dtbc_taken, 64), (uD_out, 64), (z_out, 128)):
            stores[k].stage_added(n * B)
    for k in range(4):
        full[k].stage_added(USES * B)
        free[k].stage_added(USES * B)
    for n, per in (("x_evac", 2 * IB), ("conv", IB), ("u", IB), ("proj", 1), ("proj_copy", 1), ("bc_out", 16), ("dtp", IB),
                   ("z", IB), ("relu", IB), ("log", IB), ("dt", IB), ("dtu", IB), ("uD", IB), ("zt", 2 * TT), ("step", 3 * IB)):
        c[n].stage_added(per * B)


def scan(core, ident, scr, layer):
    nc = core.nc
    with ExitStack() as ctx:
        sb, psum = allocator(nc, ctx, f"scan{layer}")
        Brep = sb("Brep", [P, NS, T])
        Crep = sb("Crep", [P, NS, T])
        two = lambda n, shape: [sb(f"{n}{k}", shape) for k in range(2)]
        dt, dtu, uD, A = two("dt", [P, T]), two("dtu", [P, T]), two("uD", [P, T]), two("A", [P, NS + 1])
        z, g, hC = two("z", [P, TT, P]), two("g", [P, TT, P]), two("hC", [P, T])
        DR = 4
        drive = [sb(f"drive{k}", [P, T]) for k in range(DR)]
        dAh = [psum(f"dAh{k}", [P, T]) for k in range(2)]
        yT = [psum(f"yT{k}", [P, TT, P]) for k in range(2)]
        scanned, scaled, turned, gated = core.scanned, core.scaled, core.unit_turned, core.gated
        decayed, driven = core.count("decayed"), core.count("driven")
        y_full = core.count("scan_y_full")
        in_, in_free = core.input_in, core.input_free
        PAIRS = IB // 2
        IN = 5 * 16
        g_rows = scr["g"].rearrange("b m p k d -> (b m) p k d")
        block = ctx.enter_context(nc.Block())

        @block.sync
        def _(sp):
            def load(b, m, j, use):
                sp.wait_ge(in_free[j].handle, in_free[j].at(use))
                core.apart(sp)
                for dst, src in ((dt[j][:], scr["dt"][b, m]), (dtu[j][:], scr["dtu"][b, m]),
                                 (A[j][:], scr["A"][layer - 2][m]), (uD[j][:], scr["uD"][b, m]),
                                 (z[j][:], scr["z"][b, :, bass.ds(m * P, P)].rearrange("(k p) d -> p k d", p=P))):
                    sp.dma_start(dst, src).then_inc(in_[j].handle, 16)

            with sp.Fori(0, B) as b:
                load(b, 0, 0, b * PAIRS)
                for n in range(NS):
                    sp.wait_ge(scaled.handle, scaled.at(b * (IB * NS) + (n + 1 - NS)))
                    core.apart(sp)
                    sp.dma_start(Brep[:, n, :], scr["bc"][b, n:n + 1, :].broadcast_to([P, T])).then_inc(core.replica_in[n].handle, 16)
                    sp.dma_start(Crep[:, n, :], scr["bc"][b, NS + n:NS + n + 1, :].broadcast_to([P, T])
                                 ).then_inc(core.replica_in[n].handle, 16)
                load(b, 1, 1, b * PAIRS)
                with sp.Fori(1, PAIRS) as i:
                    for j in range(2):
                        load(b, i * 2 + j, j, b * PAIRS + i)

        @block.scalar
        def _(act):
            def store(pair, j):
                act.wait_ge(gated.handle, gated.at(pair * 2 + (j + 1)))
                act.dma_start(g_rows[pair * 2 + j], g[j][:]).then_inc(core.g_stored[j].handle, 16)

            def blocks(pair, first):
                for j in range(2):
                    act.wait_ge(in_[j].handle, in_[j].at(pair * IN + IN))
                    for n in range(NS):
                        k = (pair * 2 + j) * NS + n
                        act.wait_ge(scaled.handle, scaled.at(k - 1))
                        nc.scalar.activation(dAh[n % 2][:], dt[j][:], ACT.Exp, scale=A[j][:, n:n + 1]
                                             ).then_inc(decayed.handle, 1)
                        if n == 6 and not (first and j == 0):
                            store(pair if j == 1 else pair - 1, 1 - j)

            with act.Fori(0, B) as b:
                blocks(b * PAIRS, True)
                with act.Fori(1, PAIRS) as i:
                    blocks(b * PAIRS + i, False)
                store(b * PAIRS + (PAIRS - 1), 1)
            for j in range(2):
                act.wait_ge(core.g_stored[j].handle, core.g_stored[j].at(16 * B * PAIRS))

        @block.gpsimd
        def _(pool):
            with pool.Fori(0, B) as b:
                core.apart(pool)
                with pool.Fori(0, PAIRS) as i:
                    pair = b * PAIRS + i
                    for j in range(2):
                        pool.wait_ge(in_[j].handle, in_[j].at(pair * IN + IN))
                        for n in range(NS):
                            k = (pair * 2 + j) * NS + n
                            pool.wait_ge(core.replica_in[n].handle, core.replica_in[n].at(b * 32 + 32))
                            pool.wait_ge(scanned.handle, scanned.at(k + 1 - DR))
                            nc.gpsimd.tensor_tensor(drive[n % DR][:], dtu[j][:], Brep[:, n, :], ALU.mult
                                                    ).then_inc(driven.handle, 1)

        @block.vector
        def _(dve):
            def gate(pair, j):
                dve.wait_ge(y_full.handle, y_full.at(pair * 2 + (j + 1)))
                dve.wait_ge(core.g_stored[j].handle, core.g_stored[j].at(pair * 16))
                nc.vector.tensor_tensor(g[j][:], yT[j][:], z[j][:], ALU.mult).then_inc(gated.handle, 1)
                dve.wait_ge(gated.handle, gated.at(pair * 2 + (j + 1)))
                dve.sem_inc(in_free[j].handle, 1)

            def blocks(b, pair, first):
                for j in range(2):
                    dve.wait_ge(in_[j].handle, in_[j].at(pair * IN + IN))
                    for n in range(NS):
                        k = (pair * 2 + j) * NS + n
                        dve.wait_ge(core.replica_in[n].handle, core.replica_in[n].at(b * 32 + 32))
                        dve.wait_ge(decayed.handle, decayed.at(k + 1))
                        dve.wait_ge(driven.handle, driven.at(k + 1))
                        nc.vector.tensor_tensor_scan(dAh[n % 2][:], dAh[n % 2][:], drive[n % DR][:], 0.0,
                                                     ALU.mult, ALU.add).then_inc(scanned.handle, 1)
                        dve.wait_ge(scanned.handle, scanned.at(k + 1))
                        dve.wait_ge(turned.handle, turned.at(k - 1))
                        nc.vector.tensor_tensor(hC[n % 2][:], dAh[n % 2][:], Crep[:, n, :], ALU.mult
                                                ).then_inc(scaled.handle, 1)
                        if n == 2 and not (first and j == 0):
                            gate(pair if j == 1 else pair - 1, 1 - j)

            with dve.Fori(0, B) as b:
                blocks(b, b * PAIRS, True)
                core.apart(dve)
                with dve.Fori(1, PAIRS) as i:
                    blocks(b, b * PAIRS + i, False)
                gate(b * PAIRS + (PAIRS - 1), 1)

        @block.tensor
        def _(pe):
            with pe.Fori(0, B * PAIRS) as pair:
                for j in range(2):
                    pe.wait_ge(gated.handle, gated.at(pair * 2 + (j - 1)))
                    pe.wait_ge(in_[j].handle, in_[j].at(pair * IN + IN))
                    for n in range(NS + 1):
                        if n < NS:
                            pe.wait_ge(scaled.handle, scaled.at((pair * 2 + j) * NS + (n + 1)))
                        src = hC[n % 2] if n < NS else uD[j]
                        for t in range(TT):
                            last = nc.tensor.matmul(yT[j][:, t, :], src[:, t * P:(t + 1) * P], ident[:],
                                                    start=(n == 0 and t % 4 == 0), stop=(n == NS), is_transpose=True,
                                                    skip_group_check=True)
                        last.then_inc((turned if n < NS else y_full).handle, 1)

    units = B * IB * NS
    for cc in (scanned, scaled, turned, decayed, driven):
        cc.stage_added(units)
    for cc in (gated, y_full):
        cc.stage_added(B * IB)
    for j in range(2):
        in_[j].stage_added(IN * B * PAIRS)
        in_free[j].stage_added(B * PAIRS)
        core.g_stored[j].stage_added(16 * B * PAIRS)
    for n in range(NS):
        core.replica_in[n].stage_added(32 * B)


def ssm_output(core, ident, io, scr, layer, residual, dst):
    nc = core.nc
    with ExitStack() as ctx:
        sb, psum = allocator(nc, ctx, f"ssmout{layer}")
        Wo = sb("Wo", [P, IB, D])
        gt = sb("gt", [P, D])
        two = lambda n, shape: [sb(f"{n}{k}", shape) for k in range(2)]
        g, gT, x, out = two("g", [P, IB, P]), two("gT", [P, IB, P]), two("x", [P, D]), two("out", [P, D])
        TP = [psum(f"TP{k}", [P, IB, P]) for k in range(2)]
        O = [psum(f"O{k}", [P, D]) for k in range(2)]
        c = {n: core.count("out_" + n) for n in ("gate_in", "turn", "copy", "mm", "step", "done")}
        w = lambda eng, n, value: eng.wait_ge(c[n].handle, c[n].at(value))
        n_in = 16 if residual is None else 32
        PAIRS = TT // 2
        block = ctx.enter_context(nc.Block())

        @block.sync
        def _(sp):
            sp.dma_start(Wo[:], io[f"out_w{layer}"].rearrange("(k p) f -> p k f", p=P)).then_inc(core.consts_in.handle, 16)
            with sp.Fori(0, B) as b:
                for j in range(2):
                    sp.wait_ge(core.input_free[j].handle, core.input_free[j].at(b * PAIRS))
                    core.apart(sp)
                sp.dma_start(gt[:], scr["gate"][layer - 2, bass.ds(b, 1), :].broadcast_to([P, D])).then_inc(c["gate_in"].handle, 16)
                with sp.Fori(0, PAIRS) as i:
                    for j in range(2):
                        sp.wait_ge(core.input_free[j].handle, core.input_free[j].at(b * PAIRS + i))
                        core.apart(sp)
                        sp.dma_start(g[j][:], scr["g"][b, :, :, i * 2 + j, :].rearrange("m p d -> p m d")
                                     ).then_inc(core.input_in[j].handle, 16)
                        if residual is not None:
                            sp.dma_start(x[j][:], residual[b, bass.ds((i * 2 + j) * P, P), :]).then_inc(core.input_in[j].handle, 16)

        @block.tensor
        def _(pe):
            pe.wait_ge(core.consts_in.handle, core.consts_in.at(16))
            with pe.Fori(0, B * PAIRS) as pair:
                for j in range(2):
                    pe.wait_ge(core.input_in[j].handle, core.input_in[j].at(pair * n_in + n_in))
                    pe.wait_ge(core.bank_free[j].handle, core.bank_free[j].at(pair))
                    for m in range(IB):
                        last = nc.tensor.transpose(TP[j][:, m, :], g[j][:, m, :], ident[:])
                    last.then_inc(c["turn"].handle, 1)
                for j in range(2):
                    w(pe, "copy", pair * 2 + (j + 1))
                    pe.wait_ge(core.input_free[j].handle, core.input_free[j].at(pair))
                    for m in range(IB):
                        last = nc.tensor.matmul(O[j][:], gT[j][:, m, :], Wo[:, m, :], start=(m == 0), stop=(m == IB - 1))
                    last.then_inc(c["mm"].handle, 1)

        @block.scalar
        def _(act):
            with act.Fori(0, B * PAIRS) as pair:
                for j in range(2):
                    w(act, "turn", pair * 2 + (j + 1))
                    act.wait_ge(core.input_free[j].handle, core.input_free[j].at(pair))
                    nc.scalar.copy(gT[j][:], TP[j][:]).then_inc(c["copy"].handle, 1)
                    w(act, "copy", pair * 2 + (j + 1))
                    act.sem_inc(core.bank_free[j].handle, 1)
                for j in range(2):
                    w(act, "done", pair * 2 + (j + 1))
                    act.dma_start(dst.rearrange("b t d -> (b t) d")[bass.ds((pair * 2 + j) * P, P), :], out[j][:]
                                  ).then_inc(core.stage_stored[j].handle, 16)
            for j in range(2):
                act.wait_ge(core.stage_stored[j].handle, core.stage_stored[j].at(16 * B * PAIRS))

        @block.vector
        def _(dve):
            with dve.Fori(0, B) as b:
                w(dve, "gate_in", b * 16 + 16)
                core.apart(dve)
                with dve.Fori(0, PAIRS) as i:
                    pair = b * PAIRS + i
                    for j in range(2):
                        w(dve, "mm", pair * 2 + (j + 1))
                        dve.wait_ge(core.stage_stored[j].handle, core.stage_stored[j].at(pair * 16))
                        ins = nc.vector.tensor_tensor(out[j][:], O[j][:], gt[:], ALU.mult)
                        if residual is not None:
                            ins.then_inc(c["step"].handle, 1)
                            w(dve, "step", pair * 2 + (j + 1))
                            ins = nc.vector.tensor_tensor(out[j][:], out[j][:], x[j][:], ALU.add)
                        ins.then_inc(c["done"].handle, 1)
                        w(dve, "done", pair * 2 + (j + 1))
                        dve.sem_inc(core.input_free[j].handle, 1)

    core.consts_in.stage_added(16)
    for j in range(2):
        core.input_in[j].stage_added(n_in * B * PAIRS)
        core.input_free[j].stage_added(B * PAIRS)
        core.bank_free[j].stage_added(B * PAIRS)
        core.bank_full[j].stage_added(0)
        core.stage_stored[j].stage_added(16 * B * PAIRS)
    c["gate_in"].stage_added(16 * B)
    for n in ("turn", "copy", "mm", "done"):
        c[n].stage_added(2 * B * PAIRS)
    if residual is not None:
        c["step"].stage_added(2 * B * PAIRS)


def gather_add(core, io, src, residual, dst):
    nc = core.nc
    with ExitStack() as ctx:
        sb, psum = allocator(nc, ctx, "gather")
        idx = sb("idx", [P, TT], I32)
        idx_b = sb("idx_b", [P, B, TT], I32)
        two = lambda n, shape: [sb(f"{n}{k}", shape) for k in range(2)]
        y, x = two("y", [P, TT, D]), two("x", [P, TT, D])
        idx_done, added = core.count("idx_done"), core.count("gather_added")
        rows_in = [core.count(f"gather_rows_in{k}") for k in range(2)]
        block = ctx.enter_context(nc.Block())

        @block.sync
        def _(sp):
            sp.dma_start(idx[:], io["perm"]).then_inc(core.consts_in.handle, 16)
            for b in range(B):
                sp.wait_ge(core.input_free[b % 2].handle, core.input_free[b % 2].at(b // 2))
                sp.dma_start(x[b % 2][:], residual[b].rearrange("(k p) d -> p k d", p=P)
                             ).then_inc(core.residual_in[b % 2].handle, 16)

        @block.gpsimd
        def _(pool):
            pool.wait_ge(idx_done.handle, idx_done.at(1))
            for b in range(B):
                pool.wait_ge(core.input_free[b % 2].handle, core.input_free[b % 2].at(b // 2))
                for k in range(TT):
                    pool.indirect_dma_start(y[b % 2][:, k, :], None, src.rearrange("b t d -> (b t) d"),
                                            bass.IndirectOffsetOnAxis(ap=idx_b[:, b, k:k + 1], axis=0)
                                            ).then_inc(rows_in[b % 2].handle, 16)

        @block.vector
        def _(dve):
            dve.wait_ge(core.consts_in.handle, core.consts_in.at(16))
            for b in range(B):
                last = nc.vector.tensor_scalar(idx_b[:, b, :], idx[:], float(b * T), None, ALU.add)
            last.then_inc(idx_done.handle, 1)
            for b in range(B):
                dve.wait_ge(rows_in[b % 2].handle, rows_in[b % 2].at((b // 2 + 1) * 16 * TT))
                dve.wait_ge(core.residual_in[b % 2].handle, core.residual_in[b % 2].at((b // 2 + 1) * 16))
                nc.vector.tensor_tensor(x[b % 2][:], x[b % 2][:], y[b % 2][:], ALU.add).then_inc(added.handle, 1)

        @block.scalar
        def _(act):
            for b in range(B):
                act.wait_ge(added.handle, added.at(b + 1))
                act.dma_start(dst[b].rearrange("(k p) d -> p k d", p=P), x[b % 2][:]
                              ).then_inc(core.stage_stored[b % 2].handle, 16)
                act.wait_ge(core.stage_stored[b % 2].handle, core.stage_stored[b % 2].at((b // 2 + 1) * 16))
                act.sem_inc(core.input_free[b % 2].handle, 1)


LAYERS = 4


def program(nc, io, out, kind="Internal"):
    scr = {}
    for name, shape in (("tab", [TABS, B, P, 8]), ("gate", [2, B, D]), ("keep", [2, B, P, TT]), ("A", [2, IB, P, NS + 1]),
                        ("xT", [B, P, KT, T]), ("q_split", [B, 2, D, T]), ("k_split", [B, 2, D, T]),
                        ("v_split", [B, T, 2 * D]), ("kT", [B, P, KT, T]), ("q", [B, T, D]),
                        ("v", [B, T, D]), ("y", [B, T, D]), ("x1", [B, T, D]), ("x2", [B, T, D]), ("x3", [B, T, D]),
                        ("z", [B, T, DI]), ("uD", [B, IB, P, T]), ("dtu", [B, IB, P, T]), ("dt", [B, IB, P, T]),
                        ("bc", [B, 2 * NS, T]), ("g", [B, IB, P, TT, P])):
        scr[name] = nc.dram_tensor(f"scratch_{name}", shape, F32, kind=kind).ap()
    with ExitStack() as ctx:
        core = Core(nc, ctx)
        ident = ctx.enter_context(nc.sbuf_tensor("ident", [P, P], F32))
        eps = ctx.enter_context(nc.sbuf_tensor("eps", [P, 4], F32))
        cols = ctx.enter_context(nc.sbuf_tensor("column_tables", [P, NCOL], F32))
        give_credits(core, ident, eps)
        modulation(core, io, scr, cols)
        tab = scr["tab"]

        normalize(core, "n0", ident, eps, io["x"], tab[0], ACT.Identity, scr["xT"])
        project(core, "p0", io, cols, scr["xT"], [
            dict(kind="T", w=io["q_w"], n=D, col="q_b", dst=scr["q_split"], split=True),
            dict(kind="T", w=io["k_w"], n=D, col="k_b", dst=scr["k_split"], split=True),
            dict(kind="N", w=io["v_w"], n=D, row=0, keep=scr["keep"][0], dst=scr["v_split"], split=True)])
        attention(core, ident, io, scr)
        normalize(core, "n1", ident, eps, scr["y"], tab[1], ACT.Silu, scr["xT"])
        project(core, "p1", io, cols, scr["xT"], [
            dict(kind="N", w=io["out_w"], n=D, row=1, residual=io["x"], dst=scr["x1"])])

        normalize(core, "n2", ident, eps, scr["x1"], tab[2], ACT.Identity, scr["xT"])
        project(core, "p2", io, cols, scr["xT"], [
            dict(kind="T", w=io["Wk"], n=D, col="bk", dst=scr["kT"]),
            dict(kind="N", w=io["Wq"], n=D, row=2, dst=scr["q"]),
            dict(kind="N", w=io["Wv"], n=D, row=3, keep=scr["keep"][1], dst=scr["v"])])
        linear_attention(core, ident, io, scr)
        normalize(core, "n3", ident, eps, scr["y"], tab[3], ACT.Silu, scr["xT"])
        project(core, "p3", io, cols, scr["xT"], [
            dict(kind="N", w=io["film_out_W"], n=D, row=4, residual=scr["x1"], dst=scr["x2"])])

        for layer, x_in in ((2, scr["x2"]), (3, scr["x3"])):
            normalize(core, f"n{layer + 2}", ident, eps, x_in, tab[layer + 2], ACT.Identity, scr["xT"],
                      gather=io["perm"] if layer == 3 else None)
            ssm_inputs(core, cols, eps, io, scr, layer)
            scan(core, ident, scr, layer)
            if layer == 2:
                ssm_output(core, ident, io, scr, layer, scr["x2"], scr["x3"])
            else:
                ssm_output(core, ident, io, scr, layer, None, scr["y"])
        gather_add(core, io, scr["y"], scr["x3"], out)


def kernel(**inputs):
    import concourse.bacc as bacc
    from concourse.bass_utils import run_bass_kernel_spmd as run

    a = {k: np.asarray(v) for k, v in inputs.items()}
    l0 = {k[8:]: v for k, v in a.items() if k.startswith("L0_cond_")}
    l1 = {k[8:]: v for k, v in a.items() if k.startswith("L1_cond_")}
    l2 = {k[8:]: v for k, v in a.items() if k.startswith("L2_cond_")}
    l3 = {k[8:]: v for k, v in a.items() if k.startswith("L3_cond_")}

    def columns(v):
        return v.reshape(-1, P).T

    def tile_columns(v):
        return v.reshape(-1, P, v.shape[-1]).transpose(1, 0, 2).reshape(P, -1)

    col = dict(q_b=l0["q_b"], k_b=l0["k_b"], bk=l1["bk"], norm_w0=l0["norm_w"], norm_b0=l0["norm_b"],
               sb_w=l0["sb_norm_w"], sb_b=l0["sb_norm_b"], emb_b0=l0["emb_b"],
               norm_w1=l1["norm_scale"], norm_b1=l1["norm_bias"], film_w=l1["film_norm_scale"],
               film_b=l1["film_norm_bias"], emb_b1=l1["film_emb_b"],
               ln_g2=l2["ln_g"], ln_b2=l2["ln_b"], ada_b2=l2["ada_b"][:2 * D],
               ln_g3=l3["gamma"], ln_b3=l3["beta"], ada_b3=l3["b_ada"][:2 * D],
               conv_b2=l2["conv_b"], dt_b2=l2["dt_proj_b"], D2=l2["D_param"],
               conv_b3=l3["conv_b"], dt_b3=l3["b_dt"], D3=l3["D_param"])
    col = {k: columns(v) for k, v in col.items()}
    col.update(conv_w2=tile_columns(l2["conv_w"]), A_log2=tile_columns(l2["A_log"]),
               conv_w3=tile_columns(l3["conv_w"].reshape(DI, KC)), A_log3=tile_columns(l3["A_log"]))
    arrays = {
        "x": a["x"],
        "cols": np.concatenate([col[n] for n, _ in COLS], axis=1),
        "rows": np.stack([l0["v_b"], l0["out_b"], l1["bq"], l1["bv"], l1["film_out_b"],
                          l2["ada_b"][2 * D:], l3["b_ada"][2 * D:]]),
        "condT": a["cond_2048"].T,
        "mask0": a["mask_BxS_ff1"], "mask1": a["mask_BxS_ik0"],
        "mask0_cols": a["mask_BxS_ff1"].reshape(B, TT, P).transpose(2, 0, 1),
        "mask1_cols": a["mask_BxS_ik0"].reshape(B, TT, P).transpose(2, 0, 1),
        "perm": a["itok_S_0_1023"].reshape(TT, P).T,
        "emb_w0": l0["emb_w"], "emb_w1": l1["film_emb_W"], "ada_w2": l2["ada_w"].T, "ada_w3": l3["W_ada"],
        "q_w": l0["q_w"], "k_w": l0["k_w"], "v_w": l0["v_w"], "out_w": l0["out_w"],
        "Wq": l1["Wq"], "Wk": l1["Wk"], "Wv": l1["Wv"], "film_out_W": l1["film_out_W"],
        "in_wx2": l2["in_proj_w"][:DI].T, "in_wz2": l2["in_proj_w"][DI:].T,
        "in_wx3": l3["W_in"][:, :DI], "in_wz3": l3["W_in"][:, DI:],
        "x_w2": l2["x_proj_w"].T, "x_w3": l3["W_xp"], "dt_w2": l2["dt_proj_w"].T, "dt_w3": l3["W_dt"],
        "out_w2": l2["out_proj_w"].T, "out_w3": l3["W_out"],
    }
    arrays = {k: np.ascontiguousarray(v) for k, v in arrays.items()}
    nc = bacc.Bacc("TRN2", target_bir_lowering=False, num_devices=1)
    io = {k: nc.dram_tensor(k, v.shape, mybir.dt.from_np(v.dtype), kind="ExternalInput").ap() for k, v in arrays.items()}
    out = nc.dram_tensor("out", (B, T, D), F32, kind="ExternalOutput").ap()
    program(nc, io, out)
    return run(nc, [arrays], core_ids=[0]).results[0]["out"]
```

```python
from contextlib import ExitStack

import numpy as np
import concourse.bass as bass
from concourse import mybir

F32 = mybir.dt.float32
F32R = mybir.dt.float32r
I32 = mybir.dt.int32
ALU = mybir.AluOpType
ACT = mybir.ActivationFunctionType
AX = mybir.AxisListType

P = 128
B, T, D = 4, 1024, 512
E = 1024
H, DH = 16, 32
DI, NS, R, KC = 1024, 16, 64, 4
KT = D // P
TT = T // P
HALF = 512
IB = DI // P
ET = E // P
EPS = 1e-5
HUGE = 3.0e38

COLS = [("q_b", 4), ("k_b", 4), ("bk", 4),
        ("norm_w0", 4), ("norm_b0", 4), ("sb_w", 4), ("sb_b", 4), ("emb_b0", 8),
        ("norm_w1", 4), ("norm_b1", 4), ("film_w", 4), ("film_b", 4), ("emb_b1", 8),
        ("ln_g2", 4), ("ln_b2", 4), ("ada_b2", 8), ("ln_g3", 4), ("ln_b3", 4), ("ada_b3", 8),
        ("conv_b2", 8), ("dt_b2", 8), ("D2", 8), ("conv_w2", 32), ("A_log2", 128),
        ("conv_b3", 8), ("dt_b3", 8), ("D3", 8), ("conv_w3", 32), ("A_log3", 128)]
COL_AT, _n = {}, 0
for _name, _w in COLS:
    COL_AT[_name] = _n
    _n += _w
NCOL = _n
ROWS = ["v_b", "out_b0", "bq", "bv", "out_b1", "gate_b2", "gate_b3"]
TABS = 6


class Count:

    def __init__(self, handle, base):
        self.handle, self.base = handle, base

    def at(self, n):
        return n + self.base

    def stage_added(self, n):
        self.base += n


class Core:

    def __init__(self, nc, ctx):
        self.nc = nc
        sem = lambda name: ctx.enter_context(nc.semaphore(name))
        many = lambda name, n, base: [Count(sem(f"{name}{k}"), base) for k in range(n)]
        self.bank_full = many("bank_full", 8, 2)
        self.bank_free = many("bank_free", 8, 1)
        self.stage_stored = many("stage_stored", 10, 16)
        self.stage_full = many("stage_full", 8, 0)
        self.slot_in = many("slot_in", 8, 0)
        self.input_in = many("input_in", 4, 0)
        self.input_free = many("input_free", 4, 1)
        self.gate_free = many("gate_free", 2, 1)
        self.consts_in = Count(sem("consts_in"), 0)
        self.vector_step = Count(sem("vector_step"), 0)
        self.scalar_step = Count(sem("scalar_step"), 0)
        self.pool_step = Count(sem("pool_step"), 0)
        self.turned_out = many("turned_out", 2, 16)
        self.bc_taken = Count(sem("bc_taken"), 1)
        self.scanned = Count(sem("scanned"), 16)
        self.scaled = Count(sem("scaled"), 16)
        self.unit_turned = Count(sem("unit_turned"), 16)
        self.gated = Count(sem("gated"), 2)
        self.g_stored = many("g_stored", 2, 16)
        self.replica_in = many("replica_in", NS, 0)
        self.scored = Count(sem("scored"), 2 * H)
        self.weighed = Count(sem("weighed"), H)
        self.shifted = Count(sem("shifted"), 1)
        self.passed = Count(sem("passed"), 0)
        self.named = {}
        self._sem = sem

    def apart(self, engine):
        engine.sem_inc(self.passed.handle, 1)

    def count(self, name):
        if name not in self.named:
            self.named[name] = Count(self._sem(name), 0)
        return self.named[name]


class Chain:

    def __init__(self, engine, count, offset=0):
        self.engine, self.count, self.n, self.offset = engine, count, 0, offset

    def __call__(self, instruction):
        self.n += 1
        instruction.then_inc(self.count.handle, 1)
        self.engine.wait_ge(self.count.handle, self.count.at(self.n + self.offset))


def allocator(nc, ctx, stage):
    def sb(name, shape, dt=F32):
        return ctx.enter_context(nc.sbuf_tensor(f"{stage}_{name}", shape, dt))

    def psum(name, shape):
        return ctx.enter_context(nc.psum_tensor(f"{stage}_{name}", shape, F32))

    return sb, psum


def give_credits(core, ident, zero_eps):
    nc = core.nc
    ready = core.count("ident_ready")
    with nc.Block() as block:
        @block.vector
        def _(dve):
            for c in core.bank_full + core.bank_free + core.input_free + core.gate_free:
                dve.sem_inc(c.handle, c.base)
            for c in core.stage_stored:
                dve.sem_inc(c.handle, 16)
            for c in [core.bc_taken, core.scanned, core.scaled, core.unit_turned, core.gated,
                      core.scored, core.weighed, core.shifted] + core.g_stored + core.turned_out:
                dve.sem_inc(c.handle, c.base)
            nc.vector.memset(zero_eps[:, 0:1], EPS)
            nc.vector.memset(zero_eps[:, 1:2], 0.0)
            nc.vector.memset(zero_eps[:, 2:3], 1.0)

        @block.gpsimd
        def _(pool):
            nc.gpsimd.memset(ident[:], 0.0).then_inc(ready.handle, 1)
            pool.wait_ge(ready.handle, 1)
            nc.gpsimd.affine_select(out=ident[:], in_=ident[:], compare_op=ALU.not_equal, fill=1.0,
                                    base=0, pattern=[[-1, P]], channel_multiplier=1)


def modulation(core, ident, io, scr, cols):
    nc = core.nc
    with ExitStack() as ctx:
        sb, psum = allocator(nc, ctx, "mod")
        W = [sb(f"W{k}", [P, ET, width]) for k, width in enumerate((3 * D, 2 * D, 3 * D))]
        condT = sb("condT", [P, ET, B])
        silu_cT = sb("silu_cT", [P, ET, B])
        gate_bias = sb("gate_bias", [B, 2, D])
        gates = sb("gates", [B, 2, D])
        tab = sb("tab", [P, TABS, B, 8])
        e = sb("e", [P, 4, 8, B])
        part = sb("part", [P, 4, KT, B])
        mask0 = sb("mask0", [P, B, TT])
        mask1 = sb("mask1", [P, B, TT], I32)
        keep = sb("keep", [P, 2, B, TT])
        A = sb("A", [P, 2, IB, NS + 1])
        eb = sb("eb", [B, 2, 2 * D])
        pe_rows = [psum(f"rows{k}", [B, 2 * D]) for k in range(2)]
        ps = [psum(f"ps{k}", [P, 8 * B]) for k in range(2)]
        pg = [psum(f"pg{k}", [B, D]) for k in range(2)]
        w_in, w_free = core.input_in, core.input_free
        silu_done, mm_done = core.count("silu_done"), core.count("mod_mm_done")
        dve_done, act_done = core.count("mod_dve_done"), core.count("mod_act_done")
        rows_done, rows_copied = core.count("mod_rows_done"), core.count("mod_rows_copied")
        widths = [2 * D, 2 * D, 3 * D, 3 * D]
        w_src = [io["emb_w0"], io["emb_w1"], io["ada_w2"], io["ada_w3"]]
        block = ctx.enter_context(nc.Block())
        col = lambda name, k, n=1: cols[:, COL_AT[name] + k:COL_AT[name] + k + n]

        @block.sync
        def _(sp):
            ci = core.consts_in.handle
            sp.dma_start(cols[:], io["cols"]).then_inc(ci, 16)
            sp.dma_start(condT[:], io["condT"].rearrange("(k p) b -> p k b", p=P)).then_inc(ci, 16)
            sp.dma_start(gate_bias[:], io["rows"][5:7, :].rearrange("(o r) d -> o r d", o=1)
                         .broadcast_to([B, 2, D])).then_inc(ci, 16)
            sp.dma_start(mask0[:], io["mask0_cols"]).then_inc(ci, 16)
            sp.dma_start(mask1[:], io["mask1_cols"]).then_inc(ci, 16)
            for l in range(4):
                if l == 3:
                    sp.wait_ge(w_free[0].handle, w_free[0].at(1))
                sp.dma_start(W[l % 3][:, :, 0:widths[l]],
                             w_src[l].rearrange("(k p) f -> p k f", p=P)).then_inc(w_in[l % 3].handle, 16)
            out = core.count("tables_out")
            sp.wait_ge(dve_done.handle, dve_done.at(1))
            sp.wait_ge(act_done.handle, act_done.at(1))
            for t in range(TABS):
                sp.dma_start(scr["tab"][t].rearrange("b p e -> p b e"), tab[:, t]).then_inc(out.handle, 16)
            sp.dma_start(scr["gate"].rearrange("l b d -> b l d"), gates[:]).then_inc(out.handle, 16)
            for l in range(2):
                sp.dma_start(scr["keep"][l].rearrange("b p e -> p b e"), keep[:, l]).then_inc(out.handle, 16)
                sp.dma_start(scr["A"][l].rearrange("i p e -> p i e"), A[:, l]).then_inc(out.handle, 16)
            sp.wait_ge(out.handle, out.at(16 * (TABS + 5)))

        @block.scalar
        def _(act):
            act.wait_ge(core.consts_in.handle, core.consts_in.at(80))
            nc.scalar.activation(silu_cT[:], condT[:], ACT.Silu).then_inc(silu_done.handle, 1)
            for l in range(2):
                last = nc.scalar.activation(A[:, l, :, 0:NS],
                                            col(f"A_log{l + 2}", 0, 128).rearrange("p (i n) -> p i n", n=NS), ACT.Exp)
            last.then_inc(core.scalar_step.handle, 1)
            act.wait_ge(core.scalar_step.handle, core.scalar_step.at(1))
            for l in range(2):
                nc.scalar.mul(A[:, l, :, 0:NS], A[:, l, :, 0:NS], -1.0)
                last = nc.scalar.copy(A[:, l, :, NS], col(f"D{l + 2}", 0, 8))
            last.then_inc(act_done.handle, 1)
            for l in range(4):
                act.wait_ge(rows_done.handle, rows_done.at(l + 1))
                if l >= 2:
                    act.wait_ge(mm_done.handle, mm_done.at(l - 1))
                nc.scalar.copy(eb[:, l % 2, :], pe_rows[l % 2][:]).then_inc(rows_copied.handle, 1)

        @block.tensor
        def _(pe):
            pe.wait_ge(silu_done.handle, silu_done.at(1))
            for l in range(4):
                pe.wait_ge(w_in[l % 3].handle, w_in[l % 3].at(16 * (l // 3 + 1)))
                if l >= 2:
                    pe.wait_ge(core.count("mod_read").handle, core.count("mod_read").at(l - 1))
                for h in range(2):
                    for k in range(ET):
                        last = nc.tensor.matmul(pe_rows[l % 2][:, h * D:(h + 1) * D], silu_cT[:, k, :],
                                                W[l % 3][:, k, h * D:(h + 1) * D], start=(k == 0), stop=(k == ET - 1))
                last.then_inc(rows_done.handle, 1)
                if l >= 2:
                    for k in range(ET):
                        last = nc.tensor.matmul(pg[l - 2][:], silu_cT[:, k, :], W[l % 3][:, k, 2 * D:3 * D],
                                                start=(k == 0), stop=(k == ET - 1))
                pe.wait_ge(rows_copied.handle, rows_copied.at(l + 1))
                for f in range(8):
                    last = nc.tensor.transpose(ps[l % 2][:, f * B:(f + 1) * B], eb[:, l % 2, f * P:(f + 1) * P],
                                               ident[0:B, 0:B])
                last.then_inc(mm_done.handle, 1)

        @block.vector
        def _(dve):
            read = core.count("mod_read")
            step = Chain(dve, core.vector_step)
            dve.wait_ge(core.consts_in.handle, core.consts_in.at(80))
            nc.vector.tensor_copy(keep[:, 0], mask0[:])
            nc.vector.tensor_scalar(keep[:, 1], mask1[:], 1.0, None, ALU.not_equal)
            for t, w, b in ((0, "norm_w0", "norm_b0"), (2, "norm_w1", "norm_b1")):
                for bb in range(B):
                    nc.vector.tensor_copy(tab[:, t, bb, 0:4], col(w, 0, 4))
                    nc.vector.tensor_copy(tab[:, t, bb, 4:8], col(b, 0, 4))
            for l in range(4):
                t, w, b, bias = ((1, "sb_w", "sb_b", "emb_b0"), (3, "film_w", "film_b", "emb_b1"),
                                 (4, "ln_g2", "ln_b2", "ada_b2"), (5, "ln_g3", "ln_b3", "ada_b3"))[l]
                scale0, shift0 = (0, 4) if l < 2 else (4, 0)
                dve.wait_ge(mm_done.handle, mm_done.at(l + 1))
                for f in range(8):
                    last = nc.vector.tensor_scalar(e[:, l, f], ps[l % 2][:, f * B:(f + 1) * B], col(bias, f), None, ALU.add)
                if l >= 2:
                    last = nc.vector.tensor_tensor(gates[:, l - 2], pg[l - 2][:], gate_bias[:, l - 2], ALU.add)
                last.then_inc(read.handle, 1)
                dve.wait_ge(read.handle, read.at(l + 1))
                if l == 0:
                    dve.sem_inc(w_free[0].handle, 1)
                for k in range(KT):
                    nc.vector.tensor_scalar(tab[:, t, :, k], e[:, l, scale0 + k], 1.0, col(w, k), ALU.add, ALU.mult)
                    last = nc.vector.tensor_scalar(part[:, l, k], e[:, l, scale0 + k], 1.0, col(b, k), ALU.add, ALU.mult)
                step(last)
                for k in range(KT):
                    last = nc.vector.tensor_tensor(tab[:, t, :, 4 + k], part[:, l, k], e[:, l, shift0 + k], ALU.add)
            last.then_inc(dve_done.handle, 1)

    core.consts_in.stage_added(80)
    for k in range(3):
        w_in[k].stage_added(32 if k == 0 else 16)
    w_free[0].stage_added(1)
    core.vector_step.stage_added(4)
    core.scalar_step.stage_added(1)


def normalize(core, name, ident, eps, src, tab, func, dst, gather=None):
    nc = core.nc
    with ExitStack() as ctx:
        sb, psum = allocator(nc, ctx, name)
        x = [sb(f"x{k}", [P, TT, D]) for k in range(2)]
        tb = [sb(f"tb{k}", [P, 8]) for k in range(2)]
        xh = [sb(f"xh{k}", [P, TT, D]) for k in range(2)]
        xT = [sb(f"xT{k}", [P, KT, T]) for k in range(2)]
        st = sb("st", [P, 2, TT, 6])
        mv = sb("mv", [P, 2, TT, 2])
        lv = sb("lv", [P, 2, TT])
        rstd = sb("rstd", [P, 2, TT])
        banks = [psum(f"bank{k}", [P, HALF]) for k in range(8)]
        stats_done, rstd_done = core.count("stats_done"), core.count("rstd_done")
        xhat_done, turned_out = core.count("xhat_done"), core.turned_out
        evacuated = core.count("turned_in_sbuf")
        xs_in, xs_free = core.input_in, core.input_free
        full, free = core.bank_full, core.bank_free
        if gather is not None:
            idx = sb("idx", [P, TT], I32)
            idx_b = sb("idx_b", [P, B, TT], I32)
            idx_done = core.count("idx_done")
        block = ctx.enter_context(nc.Block())
        table_in = core.slot_in[0:2]
        rows_in = None if gather is None else [core.count(f"{name}_rows_in{k}") for k in range(2)]

        def load_rows(eng, it, j, u):
            eng.wait_ge(xs_free[j].handle, xs_free[j].at(u))
            eng.dma_start(x[j][:], src[it].rearrange("(k p) d -> p k d", p=P)).then_inc(xs_in[j].handle, 16)

        def load_table(eng, it, j, u):
            eng.wait_ge(turned_out[j].handle, turned_out[j].at(u * 16))
            eng.dma_start(tb[j][:], tab[it]).then_inc(table_in[j].handle, 16)

        if gather is None:
            @block.sync
            def _(sp):
                with sp.Fori(0, B // 2) as i:
                    for j in range(2):
                        load_rows(sp, i * 2 + j, j, i)
                    for j in range(2):
                        load_table(sp, i * 2 + j, j, i)
        else:
            @block.sync
            def _(sp):
                sp.dma_start(idx[:], gather).then_inc(core.consts_in.handle, 16)
                for it in range(B):
                    j = it % 2
                    load_table(sp, it, j, it // 2)

            @block.gpsimd
            def _(pool):
                pool.wait_ge(idx_done.handle, idx_done.at(1))
                for it in range(B):
                    j = it % 2
                    pool.wait_ge(xs_free[j].handle, xs_free[j].at(it // 2))
                    for k in range(TT):
                        pool.indirect_dma_start(x[j][:, k, :], None, src.rearrange("b t d -> (b t) d"),
                                                bass.IndirectOffsetOnAxis(ap=idx_b[:, it, k:k + 1], axis=0)
                                                ).then_inc(rows_in[j].handle, 16)

        @block.vector
        def _(dve):
            if gather is not None:
                dve.wait_ge(core.consts_in.handle, core.consts_in.at(16))
                for it in range(B):
                    last = nc.vector.tensor_scalar(idx_b[:, it, :], idx[:], float(it * T), None, ALU.add)
                last.then_inc(idx_done.handle, 1)
            with dve.Fori(0, B // 2) as i:
                for j in range(2):
                    it = i * 2 + j
                    if gather is None:
                        dve.wait_ge(xs_in[j].handle, xs_in[j].at(i * 16 + 16))
                    else:
                        dve.wait_ge(rows_in[j].handle, rows_in[j].at(i * (16 * TT) + 16 * TT))
                    for k in range(TT):
                        last = nc.vector.bn_stats(st[:, j, k, :], x[j][:, k, :])
                    last.then_inc(core.vector_step.handle, 1)
                    dve.wait_ge(core.vector_step.handle, core.vector_step.at(it + 1))
                    core.apart(dve)
                    for k in range(TT):
                        last = nc.vector.bn_aggr(mv[:, j, k, :], st[:, j, k, :])
                    last.then_inc(stats_done.handle, 1)
                for j in range(2):
                    it = i * 2 + j
                    dve.wait_ge(rstd_done.handle, rstd_done.at(i + 1))
                    for o in range(8):
                        dve.wait_ge(full[o].handle, full[o].at(it - 1))
                    for k in range(TT):
                        ins = nc.vector.tensor_scalar(xh[j][:, k, :], x[j][:, k, :], mv[:, j, k, 0:1],
                                                      rstd[:, j, k:k + 1], ALU.subtract, ALU.mult)
                        if k % 4 == 3:
                            ins.then_inc(xhat_done.handle, 1)
                    dve.wait_ge(xhat_done.handle, xhat_done.at(it * 2 + 2))
                    dve.sem_inc(xs_free[j].handle, 1)

        @block.scalar
        def _(act):
            with act.Fori(0, B // 2) as i:
                act.wait_ge(stats_done.handle, stats_done.at(i * 2 + 2))
                nc.scalar.activation(lv[:], mv[:, :, :, 1], ACT.Ln, bias=eps[:, 0:1]).then_inc(core.scalar_step.handle, 1)
                act.wait_ge(core.scalar_step.handle, core.scalar_step.at(i + 1))
                nc.scalar.activation(rstd[:], lv[:], ACT.Exp, scale=-0.5).then_inc(rstd_done.handle, 1)
                for j in range(2):
                    it = i * 2 + j
                    act.wait_ge(table_in[j].handle, table_in[j].at(i * 16 + 16))
                    act.wait_ge(turned_out[j].handle, turned_out[j].at(i * 16))
                    for h in range(2):
                        for kt in range(KT):
                            o = h * KT + kt
                            act.wait_ge(full[o].handle, full[o].at(it + 1))
                            nc.scalar.activation(xT[j][:, kt, h * HALF:(h + 1) * HALF], banks[o][:], func,
                                                 scale=tb[j][:, kt:kt + 1], bias=tb[j][:, 4 + kt:5 + kt]
                                                 ).then_inc(evacuated.handle, 1)
                            act.wait_ge(evacuated.handle, evacuated.at(it * 8 + (o + 1)))
                            act.sem_inc(free[o].handle, 1)
                    act.dma_start(dst[it], xT[j][:]).then_inc(turned_out[j].handle, 16)
            for j in range(2):
                act.wait_ge(turned_out[j].handle, turned_out[j].at(8 * B))

        @block.tensor
        def _(pe):
            with pe.Fori(0, B // 2) as i:
                for j in range(2):
                    it = i * 2 + j
                    for h in range(2):
                        pe.wait_ge(xhat_done.handle, xhat_done.at(it * 2 + (h + 1)))
                        for kt in range(KT):
                            o = h * KT + kt
                            pe.wait_ge(free[o].handle, free[o].at(it))
                            for q in range(4):
                                last = nc.tensor.transpose(banks[o][:, q * P:(q + 1) * P],
                                                           xh[j][:, h * 4 + q, kt * P:(kt + 1) * P], ident[:])
                            last.then_inc(full[o].handle, 1)

    for k in range(2):
        if gather is None:
            xs_in[k].stage_added(16 * B // 2)
        table_in[k].stage_added(16 * B // 2)
        xs_free[k].stage_added(B // 2)
    for o in range(8):
        full[o].stage_added(B)
        free[o].stage_added(B)
    core.vector_step.stage_added(B)
    core.scalar_step.stage_added(B // 2)
    stats_done.stage_added(B)
    rstd_done.stage_added(B // 2)
    xhat_done.stage_added(2 * B)
    evacuated.stage_added(8 * B)
    for j in range(2):
        turned_out[j].stage_added(8 * B)
    if gather is not None:
        core.consts_in.stage_added(16)
        idx_done.stage_added(1)


def project(core, name, io, cols, src, jobs):
    nc = core.nc
    with ExitStack() as ctx:
        sb, psum = allocator(nc, ctx, name)
        xT = [sb(f"xT{k}", [P, KT, T]) for k in range(2)]
        W = [sb(f"W{n}", [P, KT, job["n"]]) for n, job in enumerate(jobs)]
        row = [sb(f"row{n}", [P, D]) if job.get("row") is not None else None for n, job in enumerate(jobs)]
        kp = [sb(f"keep{k}", [P, TT]) for k in range(2)]
        keep = next((job["keep"] for job in jobs if job.get("keep") is not None), None)
        has_res = any(job.get("residual") is not None for job in jobs)
        res = [sb(f"res{k}", [P, D]) for k in range(8)] if has_res else None
        split = jobs[0].get("split", False)
        stage = None if split else [sb(f"stage{k}", [P, HALF]) for k in range(8)]
        parts = [sb(f"parts{k}", [P, 2 * HALF]) for k in range(8)] if split else None
        whole = sb("whole", [P, HALF]) if split else None
        hi_done = core.count("hi_done")

        def part_of(k8, n, s):
            if jobs[n]["kind"] == "T":
                return parts[k8][:, s * HALF:(s + 1) * HALF]
            return parts[k8][:].rearrange("p (h s e) -> p h s e", s=2, e=DH)[:, :, s]

        banks = [psum(f"bank{k}", [P, HALF]) for k in range(8)]
        outs = []
        for n, job in enumerate(jobs):
            if job["kind"] == "T":
                outs += [(n, m, h) for m in range(job["n"] // P) for h in range(2)]
            else:
                outs += [(n, f, t) for t in range(TT) for f in range(job["n"] // D)]
        uses = len(outs) // 8
        full, free = core.bank_full, core.bank_free
        staged, stored = core.stage_full, core.stage_stored
        chained = lambda n: jobs[n].get("keep") is not None or jobs[n].get("residual") is not None
        steps = sum((3 if split else 1) for n, _, _ in outs if chained(n))
        n_T = sum(1 for n, _, _ in outs if jobs[n]["kind"] == "T")
        n_const = 16 * sum(r is not None for r in row)
        weights_in = [core.count(f"weights_in{n}") for n in range(len(jobs))]
        n_in = 16 if keep is None else 32
        block = ctx.enter_context(nc.Block())

        def on_scalar(n):
            return jobs[n]["kind"] == "T"

        @block.tensor
        def _(pe):
            with pe.Fori(0, B // 2) as i:
                for j in range(2):
                    pe.wait_ge(core.input_in[j].handle, core.input_in[j].at(i * n_in + n_in))
                    for o, (n, a, b) in enumerate(outs):
                        if j == 0 and (o == 0 or outs[o - 1][0] != n):
                            pe.wait_ge(weights_in[n].handle, weights_in[n].at(16))
                        k8 = o % 8
                        pe.wait_ge(free[k8].handle, free[k8].at((i * 2 + j) * uses + o // 8))
                        for kt in range(KT):
                            if jobs[n]["kind"] == "T":
                                lhs, rhs = W[n][:, kt, a * P:(a + 1) * P], xT[j][:, kt, b * HALF:(b + 1) * HALF]
                            else:
                                lhs, rhs = xT[j][:, kt, b * P:(b + 1) * P], W[n][:, kt, a * D:(a + 1) * D]
                            last = nc.tensor.matmul(banks[k8][:], lhs, rhs, start=(kt == 0), stop=(kt == KT - 1))
                        last.then_inc(full[k8].handle, 1)
                        if o == len(outs) - 1:
                            pe.wait_ge(full[k8].handle, full[k8].at((i * 2 + j) * uses + uses))
                    if keep is not None:
                        kv = [o for o, (n, _, _) in enumerate(outs) if jobs[n].get("keep") is not None][-1]
                        pe.wait_ge(staged[kv % 8].handle, staged[kv % 8].at((i * 2 + j) * uses + (kv // 8 + 1)))
                    pe.sem_inc(core.input_free[j].handle, 1)

        @block.scalar
        def _(act):
            with act.Fori(0, B // 2) as i:
                for j in range(2):
                    for o, (n, a, b) in enumerate(outs):
                        if not on_scalar(n):
                            continue
                        k8, u = o % 8, (i * 2 + j) * uses + o // 8
                        act.wait_ge(full[k8].handle, full[k8].at(u + 1))
                        act.wait_ge(stored[k8].handle, stored[k8].at(u * 16))
                        at = COL_AT[jobs[n]["col"]] + a
                        result = part_of(k8, n, 0).bitcast(F32R) if split else stage[k8][:]
                        ins = nc.scalar.activation(result, banks[k8][:], ACT.Identity, bias=cols[:, at:at + 1])
                        if split:
                            ins.then_inc(hi_done.handle, 1)
                            continue
                        ins.then_inc(staged[k8].handle, 1)
                        act.wait_ge(staged[k8].handle, staged[k8].at(u + 1))
                        act.sem_inc(free[k8].handle, 1)

        @block.vector
        def _(dve):
            if n_const:
                dve.wait_ge(core.consts_in.handle, core.consts_in.at(n_const))
            with dve.Fori(0, B // 2) as i:
                for j in range(2):
                    done = turned = 0
                    if keep is not None:
                        dve.wait_ge(core.input_in[j].handle, core.input_in[j].at(i * n_in + n_in))
                    for o, (n, a, b) in enumerate(outs):
                        k8, u = o % 8, (i * 2 + j) * uses + o // 8
                        job = jobs[n]
                        if on_scalar(n):
                            if split:
                                turned += 1
                                at = COL_AT[job["col"]] + a
                                dve.wait_ge(hi_done.handle, hi_done.at((i * 2 + j) * n_T + turned))
                                nc.vector.scalar_tensor_tensor(part_of(k8, n, 1).bitcast(F32R), banks[k8][:], cols[:, at:at + 1],
                                                               part_of(k8, n, 0), ALU.add, ALU.subtract
                                                               ).then_inc(staged[k8].handle, 1)
                                dve.wait_ge(staged[k8].handle, staged[k8].at(u + 1))
                                dve.sem_inc(free[k8].handle, 1)
                            continue
                        dve.wait_ge(full[k8].handle, full[k8].at(u + 1))
                        dve.wait_ge(stored[k8].handle, stored[k8].at(u * 16))
                        value = whole if split else stage[k8]
                        ins = nc.vector.tensor_tensor(value[:], banks[k8][:], row[n][:], ALU.add)
                        if job.get("keep") is not None or job.get("residual") is not None:
                            done += 1
                            ins.then_inc(core.vector_step.handle, 1)
                            dve.wait_ge(core.vector_step.handle, core.vector_step.at((i * 2 + j) * steps + done))
                            if job.get("keep") is not None:
                                ins = nc.vector.tensor_scalar(value[:], value[:], kp[j][:, b:b + 1], None, ALU.mult)
                            else:
                                dve.wait_ge(core.slot_in[k8].handle, core.slot_in[k8].at(u * 16 + 16))
                                ins = nc.vector.tensor_tensor(stage[k8][:], stage[k8][:], res[k8][:], ALU.add)
                        if split:
                            step = lambda n_: core.vector_step.at((i * 2 + j) * steps + n_)
                            ins.then_inc(core.vector_step.handle, 1)
                            dve.wait_ge(core.vector_step.handle, step(done + 1))
                            by_head = whole[:].rearrange("p (h e) -> p h e", e=DH)
                            nc.vector.tensor_copy(part_of(k8, n, 0).bitcast(F32R), by_head).then_inc(core.vector_step.handle, 1)
                            dve.wait_ge(core.vector_step.handle, step(done + 2))
                            ins = nc.vector.tensor_tensor(part_of(k8, n, 1).bitcast(F32R), by_head, part_of(k8, n, 0), ALU.subtract)
                            done += 2
                        ins.then_inc(staged[k8].handle, 1)
                        dve.wait_ge(staged[k8].handle, staged[k8].at(u + 1))
                        dve.sem_inc(free[k8].handle, 1)

        @block.sync
        def _(sp):
            def load(it):
                j = it % 2
                sp.wait_ge(core.input_free[j].handle, core.input_free[j].at(it // 2))
                sp.dma_start(xT[j][:], src[it]).then_inc(core.input_in[j].handle, 16)
                if keep is not None:
                    sp.dma_start(kp[j][:], keep[it]).then_inc(core.input_in[j].handle, 16)

            for n, job in enumerate(jobs):
                sp.dma_start(W[n][:], job["w"].rearrange("(k p) f -> p k f", p=P)).then_inc(weights_in[n].handle, 16)
                if n == 0:
                    load(0)
                if row[n] is not None:
                    sp.dma_start(row[n][:], io["rows"][job["row"]:job["row"] + 1, :].broadcast_to([P, D])
                                 ).then_inc(core.consts_in.handle, 16)
            load(1)
            for it in range(B):
                if has_res:
                    for k in range(8):
                        sp.wait_ge(free[k].handle, free[k].at(it * uses))
                        sp.dma_start(res[k][:], jobs[0]["residual"][it, k * P:(k + 1) * P, :]
                                     ).then_inc(core.slot_in[k].handle, 16)
                for o, (n, a, b) in enumerate(outs):
                    k8, u = o % 8, it * uses + o // 8
                    job = jobs[n]
                    sp.wait_ge(staged[k8].handle, staged[k8].at(u + 1))
                    if job["kind"] == "T" and split:
                        tile = parts[k8][:].rearrange("p (s t) -> p s t", s=2)
                        dst = job["dst"][it, :, a * P:(a + 1) * P, b * HALF:(b + 1) * HALF].rearrange("s p t -> p s t")
                    elif job["kind"] == "T":
                        tile, dst = stage[k8][:], job["dst"][it, :, a, b * HALF:(b + 1) * HALF]
                    else:
                        tile = parts[k8][:] if split else stage[k8][:]
                        width = tile.shape[1]
                        dst = job["dst"][it, b * P:(b + 1) * P, a * width:(a + 1) * width]
                    sp.dma_start(dst, tile).then_inc(stored[k8].handle, 16)
                if it + 2 < B:
                    load(it + 2)
            for k in range(8):
                sp.wait_ge(stored[k].handle, stored[k].at(16 * B * uses))

    core.consts_in.stage_added(n_const)
    for c in weights_in:
        c.stage_added(16)
    for k in range(2):
        core.input_in[k].stage_added(n_in * B // 2)
        core.input_free[k].stage_added(B // 2)
    for k in range(8):
        full[k].stage_added(B * uses)
        free[k].stage_added(B * uses)
        staged[k].stage_added(B * uses)
        stored[k].stage_added(16 * B * uses)
        if has_res:
            core.slot_in[k].stage_added(16 * B)
    core.vector_step.stage_added(B * steps)
    if split:
        hi_done.stage_added(B * n_T)


def attention(core, ident, io, scr):
    nc = core.nc
    with ExitStack() as ctx:
        sb, psum = allocator(nc, ctx, "att")
        k = sb("k", [P, H, T])
        v = sb("v", [P, TT, H, 2 * DH])
        mrow = sb("mrow", [P, T])
        mneg = sb("mneg", [P, T])
        fold = sb("fold", [2 * DH, DH])
        q = [sb(f"q{j}", [P, H, P]) for j in range(2)]
        sm = [sb(f"sm{j}", [P, T]) for j in range(2)]
        nmax = [sb(f"nmax{j}", [P, 1]) for j in range(2)]
        pr = [sb(f"pr{j}", [P, T]) for j in range(2)]
        psums = sb("psums", [P, 2 * H])
        pT = [[sb(f"pT{part}{j}", [P, T]) for j in range(2)] for part in ("hi", "lo")]
        rden = sb("rden", [P, 4])
        yts = sb("yts", [2 * DH, 4, P])
        y = [sb(f"y{j}", [P, H, DH]) for j in range(2)]
        S = [psum(f"S{j}", [P, T]) for j in range(2)]
        TP = psum("TP", [P, T])
        YT = psum("YT", [2 * DH, 4, P])
        Y = psum("Y", [P, 4, DH])
        C = H // 4
        k_in, v_in = core.slot_in[0:C], core.slot_in[C:2 * C]
        mask_in, mneg_ready, fold_ready = core.count("mask_in"), core.count("mneg_ready"), core.count("fold_ready")
        q_in = core.input_in
        scored, shifted, weighed = core.scored, core.shifted, core.weighed
        exped, turned = core.count("exped"), core.count("turned")
        hi_copied, lo_taken = core.count("hi_copied"), core.count("lo_taken")
        y_ready, yt_copied, y_turned = core.count("y_ready"), core.count("yt_copied"), core.count("y_turned")
        y_stored = core.stage_stored
        G = 8
        U = 2 * H
        PAIRS = TT // 2
        BU = TT * H
        block = ctx.enter_context(nc.Block())

        @block.sync
        def _(sp):
            def load_k(b, c):
                sp.wait_ge(scored.handle, scored.at(b * BU + (4 * c + 4 - H)))
                for g, part in enumerate((0, 1, 0, 1)):
                    sp.dma_start(k[DH * g:DH * g + DH, 4 * c:4 * c + 4, :],
                                 scr["k_split"][b, part].rearrange("(h e) t -> e h t", e=DH)[:, 4 * c:4 * c + 4, :]
                                 ).then_inc(k_in[c].handle, 16)

            def load_v(b, c):
                sp.wait_ge(weighed.handle, weighed.at(b * BU + (4 * c + 4 - H)))
                sp.dma_start(v[:, :, 4 * c:4 * c + 4, :],
                             scr["v_split"][b].rearrange("(k p) (h e) -> p k h e", p=P, e=2 * DH)[:, :, 4 * c:4 * c + 4, :]
                             ).then_inc(v_in[c].handle, 16)

            def load_q(b, i, j):
                sp.wait_ge(scored.handle, scored.at((b * PAIRS + i) * U + (H * (j + 1) - U)))
                for g, part in enumerate((0, 0, 1, 1)):
                    sp.dma_start(q[j][DH * g:DH * g + DH, :, :],
                                 scr["q_split"][b, part, :, bass.ds((i * 2 + j) * P, P)]
                                 .rearrange("(h e) t -> e h t", e=DH)).then_inc(q_in[j].handle, 16)

            with sp.Fori(0, B) as b:
                sp.wait_ge(mneg_ready.handle, mneg_ready.at(b))
                sp.dma_start(mrow[:], io["mask0"][bass.ds(b, 1), :].broadcast_to([P, T])).then_inc(mask_in.handle, 16)
                load_k(b, 0)
                load_k(b, 1)
                load_v(b, 0)
                load_k(b, 2)
                load_v(b, 1)
                load_k(b, 3)
                load_v(b, 2)
                for j in range(2):
                    load_q(b, 0, j)
                load_v(b, 3)
                core.apart(sp)
                with sp.Fori(1, PAIRS) as i:
                    for j in range(2):
                        load_q(b, i, j)

        @block.gpsimd
        def _(pool):
            with pool.Fori(0, B) as b:
                pool.wait_ge(mask_in.handle, mask_in.at(b * 16 + 16))
                pool.wait_ge(shifted.handle, shifted.at(b * BU))
                core.apart(pool)
                nc.gpsimd.tensor_scalar(mneg[:], mrow[:], 1.0, 1.0e6, ALU.subtract, ALU.mult
                                        ).then_inc(mneg_ready.handle, 1)

        @block.tensor
        def _(pe):
            pe.wait_ge(fold_ready.handle, fold_ready.at(1))
            with pe.Fori(0, B) as b:
                core.apart(pe)
                with pe.Fori(0, PAIRS) as i:
                    pair = b * PAIRS + i
                    base = pair * U

                    def scores(u):
                        j, h = u // H, u % H
                        if h == 0:
                            pe.wait_ge(q_in[j].handle, q_in[j].at(pair * 64 + 64))
                        if u < H and h % 4 == 0:
                            pe.wait_ge(k_in[h // 4].handle, k_in[h // 4].at(b * 64 + 64))
                        if u >= 2:
                            pe.wait_ge(shifted.handle, shifted.at(base + (u - 1)))
                        for c in range(2):
                            last = nc.tensor.matmul(S[u % 2][:, c * HALF:(c + 1) * HALF], q[j][:, h, :].bitcast(F32R),
                                                    k[:, h, c * HALF:(c + 1) * HALF].bitcast(F32R), start=True, stop=True)
                        last.then_inc(scored.handle, 1)

                    def turn(u):
                        pe.wait_ge(exped.handle, exped.at(base + (u + 1)))
                        for half in range(2):
                            if u >= 1:
                                pe.wait_ge(lo_taken.handle, lo_taken.at(base * 2 + (2 * u - 1 + half)))
                            for m in range(4 * half, 4 * half + 4):
                                last = nc.tensor.transpose(TP[:, m * P:(m + 1) * P], pr[u % 2][:, m * P:(m + 1) * P], ident[:])
                            last.then_inc(turned.handle, 1)

                    def weigh(u):
                        g, h = u // 4, u % H
                        pe.wait_ge(lo_taken.handle, lo_taken.at(base * 2 + (2 * u + 2)))
                        if u < H and h % 4 == 0:
                            pe.wait_ge(v_in[h // 4].handle, v_in[h // 4].at(b * 16 + 16))
                        if u % 4 == 0 and g >= 1:
                            pe.wait_ge(yt_copied.handle, yt_copied.at(pair * G + g))
                        for m in range(TT):
                            for part in range(2):
                                last = nc.tensor.matmul(YT[:, h % 4, :], v[:, m, h, :].bitcast(F32R),
                                                        pT[part][u % 2][:, m * P:(m + 1) * P].bitcast(F32R),
                                                        start=(m == 0 and part == 0), stop=(m == TT - 1 and part == 1))
                        last.then_inc(weighed.handle, 1)

                    def turn_back(g):
                        pe.wait_ge(yt_copied.handle, yt_copied.at(pair * G + (g + 1)))
                        if g >= 1:
                            pe.wait_ge(y_ready.handle, y_ready.at(pair * G + g))
                        core.apart(pe)
                        for n in range(4):
                            last = nc.tensor.matmul(Y[:, n, :], yts[:, n, :], fold[:], start=True, stop=True)
                        last.then_inc(y_turned.handle, 1)

                    scores(0)
                    scores(1)
                    for u in range(U):
                        if u + 2 < U:
                            scores(u + 2)
                        turn(u)
                        if u >= 1:
                            weigh(u - 1)
                        if u >= 6 and u % 4 == 2:
                            turn_back((u - 6) // 4)
                    weigh(U - 1)
                    turn_back(G - 1)
                    pe.wait_ge(y_ready.handle, y_ready.at(pair * G + G))

        @block.vector
        def _(dve):
            nc.vector.tensor_tensor(fold[:], ident[0:2 * DH, 0:DH], ident[0:2 * DH, DH:2 * DH], ALU.add
                                    ).then_inc(fold_ready.handle, 1)
            with dve.Fori(0, B) as b:
                dve.wait_ge(mneg_ready.handle, mneg_ready.at(b + 1))
                core.apart(dve)
                with dve.Fori(0, PAIRS) as i:
                    pair = b * PAIRS + i
                    base = pair * U

                    def shift(u):
                        dve.wait_ge(scored.handle, scored.at(base + (u + 1)))
                        if u >= 2:
                            dve.wait_ge(exped.handle, exped.at(base + (u - 1)))
                        core.apart(dve)
                        nc.vector.tensor_tensor_reduce(sm[u % 2][:], S[u % 2][:], mneg[:], -1.0, HUGE,
                                                       ALU.add, ALU.min, nmax[u % 2][:]).then_inc(shifted.handle, 1)

                    def take_lo(u):
                        for half in range(2):
                            cols_ = slice(half * HALF, (half + 1) * HALF)
                            dve.wait_ge(hi_copied.handle, hi_copied.at(base * 2 + (2 * u + half + 1)))
                            nc.vector.tensor_tensor(pT[1][u % 2][:, cols_].bitcast(F32R), TP[:, cols_],
                                                    pT[0][u % 2][:, cols_], ALU.subtract).then_inc(lo_taken.handle, 1)

                    def copy_yt(g):
                        dve.wait_ge(weighed.handle, weighed.at(base + (4 * g + 4)))
                        if g >= 1:
                            dve.wait_ge(y_turned.handle, y_turned.at(pair * G + g))
                        nc.vector.tensor_copy(yts[:], YT[:]).then_inc(yt_copied.handle, 1)

                    def take(g):
                        j, h = g // 4, (g % 4) * 4
                        dve.wait_ge(y_turned.handle, y_turned.at(pair * G + (g + 1)))
                        nc.vector.reciprocal(rden[:], psums[:, 4 * g:4 * g + 4]).then_inc(core.vector_step.handle, 1)
                        dve.wait_ge(core.vector_step.handle, core.vector_step.at(pair * G + (g + 1)))
                        if h == 0:
                            dve.wait_ge(y_stored[j].handle, y_stored[j].at(pair * 16))
                        nc.vector.tensor_tensor(y[j][:, h:h + 4, :], Y[:],
                                                rden[:].unsqueeze(2).broadcast_to([P, 4, DH]), ALU.mult
                                                ).then_inc(y_ready.handle, 1)

                    shift(0)
                    shift(1)
                    for u in range(U):
                        if u >= 1:
                            take_lo(u - 1)
                        if u >= 5 and u % 4 == 1:
                            copy_yt((u - 5) // 4)
                        if u + 2 < U:
                            shift(u + 2)
                        if u >= 8 and u % 4 == 0:
                            take((u - 8) // 4)
                    take_lo(U - 1)
                    for g in range(G - 2, G):
                        if g == G - 1:
                            copy_yt(g)
                        take(g)

        @block.scalar
        def _(act):
            with act.Fori(0, B * PAIRS) as pair:
                base = pair * U

                def copy_hi(u):
                    if u >= 2:
                        act.wait_ge(weighed.handle, weighed.at(base + (u - 1)))
                    for half in range(2):
                        cols_ = slice(half * HALF, (half + 1) * HALF)
                        act.wait_ge(turned.handle, turned.at(base * 2 + (2 * u + half + 1)))
                        nc.scalar.copy(pT[0][u % 2][:, cols_].bitcast(F32R), TP[:, cols_]).then_inc(hi_copied.handle, 1)

                for u in range(U):
                    act.wait_ge(shifted.handle, shifted.at(base + (u + 1)))
                    if u >= 2:
                        act.wait_ge(turned.handle, turned.at(base * 2 + (2 * u - 2)))
                    nc.scalar.activation(pr[u % 2][:], sm[u % 2][:], ACT.Exp, bias=nmax[u % 2][:, 0:1], scale=-1.0,
                                         accum_out=psums[:, u:u + 1]).then_inc(exped.handle, 1)
                    if u >= 1:
                        copy_hi(u - 1)
                    if u == U - 1:
                        copy_hi(u)
                    if u in (H + 8, U - 1):
                        j = 0 if u == H + 8 else 1
                        act.wait_ge(y_ready.handle, y_ready.at(pair * G + (j * 4 + 4)))
                        act.dma_start(scr["y"].rearrange("b t d -> (b t) d")[bass.ds((pair * 2 + j) * P, P), :],
                                      y[j][:].rearrange("p h e -> p (h e)")).then_inc(y_stored[j].handle, 16)
            for j in range(2):
                act.wait_ge(y_stored[j].handle, y_stored[j].at(16 * B * PAIRS))

    n = B * TT * H
    for c in (scored, shifted, exped, weighed):
        c.stage_added(n)
    for j in range(2):
        q_in[j].stage_added(64 * B * PAIRS)
        y_stored[j].stage_added(16 * B * PAIRS)
    for c in range(C):
        k_in[c].stage_added(64 * B)
        v_in[c].stage_added(16 * B)
    core.vector_step.stage_added(4 * B * TT)


def linear_attention(core, ident, io, scr):
    nc = core.nc
    with ExitStack() as ctx:
        sb, psum = allocator(nc, ctx, "lin")
        kT = sb("kT", [P, KT, T])
        q = sb("q", [P, TT, D])
        v = sb("v", [P, TT, D])
        mi = sb("mi", [P, T], I32)
        mneg = sb("mneg", [P, T])
        ks = sb("ks", [P, KT, T])
        nmax = sb("nmax", [P, KT])
        ksum = sb("ksum", [P, KT])
        kr = sb("kr", [P, KT])
        kn = sb("kn", [P, TT, D])
        qmax = sb("qmax", [P, TT * H])
        qsum = sb("qsum", [P, TT * H])
        qr = sb("qr", [P, TT * H])
        qT = sb("qT", [P, KT, T])
        at = sb("at", [P, KT, P])
        y = sb("y", [P, TT, D])
        banks = [psum(f"bank{k}", [P, HALF]) for k in range(8)]
        kv_in = core.count("kv_in")
        chain_v, y_stored = core.vector_step, core.turned_out[0]
        lin = {n: core.count("lin_" + n) for n in ("k_shift", "k_exp", "k_norm", "q_shift", "q_exp", "q_norm",
                                                   "k_turn", "k_copy", "q_turn", "q_copy", "at", "at_copy",
                                                   "y", "y_copy")}
        w = lambda eng, n, value: eng.wait_ge(lin[n].handle, value)
        block = ctx.enter_context(nc.Block())

        @block.sync
        def _(sp):
            rows = lambda name, b: scr[name][b].rearrange("(k p) d -> p k d", p=P)

            def load_k(b):
                sp.dma_start(kT[:], scr["kT"][b]).then_inc(kv_in.handle, 16)
                sp.dma_start(mi[:], io["mask1"][bass.ds(b, 1), :].broadcast_to([P, T])).then_inc(kv_in.handle, 16)

            def load_q(b):
                sp.dma_start(q[:], rows("q", b)).then_inc(kv_in.handle, 16)

            def load_v(b):
                sp.dma_start(v[:], rows("v", b)).then_inc(kv_in.handle, 16)

            def store_y(b):
                w(sp, "y_copy", b * TT + TT)
                sp.dma_start(scr["y"][b].rearrange("(k p) d -> p k d", p=P), y[:]).then_inc(y_stored.handle, 16)

            load_k(0)
            load_q(0)
            load_v(0)
            with sp.Fori(0, B - 1) as b:
                w(sp, "k_shift", b * KT + KT)
                load_k(b + 1)
                w(sp, "q_turn", b * TT + TT)
                load_q(b + 1)
                w(sp, "at", b + 1)
                load_v(b + 1)
                store_y(b)
            store_y(B - 1)
            sp.wait_ge(y_stored.handle, y_stored.at(B * 16))

        @block.vector
        def _(dve):
            nc.vector.memset(at[:], 0.0)
            with dve.Fori(0, B) as b:
                dve.wait_ge(kv_in.handle, kv_in.at(b * 64 + 64))
                nc.vector.tensor_scalar(mneg[:], mi[:], 1.0, -HUGE, ALU.is_equal, ALU.mult).then_inc(chain_v.handle, 1)
                dve.wait_ge(chain_v.handle, chain_v.at(b * 4 + 1))
                core.apart(dve)
                for kt in range(KT):
                    nc.vector.tensor_tensor_reduce(ks[:, kt], kT[:, kt], mneg[:], -1.0, HUGE, ALU.add, ALU.min,
                                                   nmax[:, kt:kt + 1]).then_inc(lin["k_shift"].handle, 1)
                qv = q[:].rearrange("p k (h e) -> p (k h) e", e=DH)
                wide = lambda x: x[:].unsqueeze(2).broadcast_to([P, TT * H, DH])
                nc.vector.tensor_reduce(qmax[:], qv, AX.X, ALU.max).then_inc(chain_v.handle, 1)
                dve.wait_ge(chain_v.handle, chain_v.at(b * 4 + 2))
                nc.vector.tensor_tensor(qv, qv, wide(qmax), ALU.subtract).then_inc(lin["q_shift"].handle, 1)
                w(dve, "k_exp", b * KT + KT)
                nc.vector.reciprocal(kr[:], ksum[:]).then_inc(chain_v.handle, 1)
                dve.wait_ge(chain_v.handle, chain_v.at(b * 4 + 3))
                for kt in range(KT):
                    last = nc.vector.tensor_scalar(ks[:, kt], ks[:, kt], kr[:, kt:kt + 1], None, ALU.mult)
                last.then_inc(lin["k_norm"].handle, 1)
                w(dve, "q_exp", b + 1)
                nc.vector.tensor_reduce(qsum[:], qv, AX.X, ALU.add).then_inc(chain_v.handle, 1)
                dve.wait_ge(chain_v.handle, chain_v.at(b * 4 + 4))
                nc.vector.reciprocal(qr[:], qsum[:]).then_inc(lin["q_norm"].handle, 1)
                w(dve, "q_norm", b * 2 + 1)
                nc.vector.tensor_tensor(qv, qv, wide(qr), ALU.mult).then_inc(lin["q_norm"].handle, 1)
                w(dve, "at", b + 1)
                for g in range(4):
                    r = slice(32 * g, 32 * g + 32)
                    last = nc.vector.tensor_copy(at[r, :, r], banks[0][:].rearrange("p (k e) -> p k e", e=P)[r, :, r])
                last.then_inc(lin["at_copy"].handle, 1)

        @block.scalar
        def _(act):
            with act.Fori(0, B) as b:
                for kt in range(KT):
                    w(act, "k_shift", b * KT + (kt + 1))
                    nc.scalar.activation(ks[:, kt], ks[:, kt], ACT.Exp, bias=nmax[:, kt:kt + 1], scale=-1.0,
                                         accum_out=ksum[:, kt:kt + 1]).then_inc(lin["k_exp"].handle, 1)
                w(act, "q_shift", b + 1)
                nc.scalar.activation(q[:], q[:], ACT.Exp).then_inc(lin["q_exp"].handle, 1)
                for t in range(TT):
                    w(act, "k_turn", b * TT + (t + 1))
                    nc.scalar.copy(kn[:, t], banks[t][:]).then_inc(lin["k_copy"].handle, 1)
                for t in range(TT):
                    w(act, "q_turn", b * TT + (t + 1))
                    nc.scalar.copy(qT[:, t % 4, (t // 4) * HALF:(t // 4 + 1) * HALF], banks[t][:]).then_inc(lin["q_copy"].handle, 1)
                act.wait_ge(y_stored.handle, y_stored.at(b * 16))
                for t in range(TT):
                    w(act, "y", b * TT + (t + 1))
                    nc.scalar.copy(y[:, t], banks[t][:]).then_inc(lin["y_copy"].handle, 1)

        @block.tensor
        def _(pe):
            with pe.Fori(0, B) as b:
                w(pe, "k_norm", b + 1)
                for t in range(TT):
                    for kt in range(KT):
                        last = nc.tensor.transpose(banks[t][:, kt * P:(kt + 1) * P], ks[:, kt, t * P:(t + 1) * P], ident[:])
                    last.then_inc(lin["k_turn"].handle, 1)
                w(pe, "q_norm", b * 2 + 2)
                w(pe, "k_copy", b * TT + TT)
                for o in range(8):
                    h, kt = o // 4, o % 4
                    for z in range(4):
                        last = nc.tensor.transpose(banks[o][:, z * P:(z + 1) * P], q[:, h * 4 + z, kt * P:(kt + 1) * P], ident[:])
                    last.then_inc(lin["q_turn"].handle, 1)
                w(pe, "q_copy", b * TT + TT)
                for kt in range(KT):
                    for t in range(TT):
                        last = nc.tensor.matmul(banks[0][:, kt * P:(kt + 1) * P], v[:, t, kt * P:(kt + 1) * P],
                                                kn[:, t, kt * P:(kt + 1) * P], start=(t == 0), stop=(t == TT - 1))
                last.then_inc(lin["at"].handle, 1)
                w(pe, "at_copy", b + 1)
                for t in range(TT):
                    for kt in range(KT):
                        last = nc.tensor.matmul(banks[t][:, kt * P:(kt + 1) * P], qT[:, kt, t * P:(t + 1) * P],
                                                at[:, kt], start=True, stop=True)
                    last.then_inc(lin["y"].handle, 1)

    kv_in.stage_added(64 * B)
    y_stored.stage_added(16 * B)
    chain_v.stage_added(4 * B)


def ssm_inputs(core, cols, eps, io, scr, layer):
    nc = core.nc
    with ExitStack() as ctx:
        sb, psum = allocator(nc, ctx, f"ssmin{layer}")
        two = lambda n, shape: [sb(f"{n}{k}", shape) for k in range(2)]
        xT = two("xT", [P, KT, T])
        Wx, Wz = sb("Wx", [P, KT, DI]), sb("Wz", [P, KT, DI])
        Wp, Wdt = sb("Wp", [P, IB, R + 2 * NS]), sb("Wdt", [R, DI])
        xp, acc = two("xp", [P, KC - 1 + T]), two("acc", [P, T])
        u = sb("u", [P, IB, T])
        xd = sb("xd", [R + 2 * NS, T])
        dtu, uD = two("dtu", [P, T]), two("uD", [P, T])
        ea, dt = ([sb(f"{n}{k}", [P, T]) for k in range(4)] for n in ("ea", "dt"))
        zt = [sb(f"zt{k}", [P, HALF]) for k in range(2)]
        ring = [psum(f"ring{k}", [P, HALF]) for k in range(4)]
        X = psum("X", [R + 2 * NS, T])
        DTP = psum("DTP", [P, T])
        c = {n: core.count("ssm_" + n) for n in ("x_evac", "conv", "u", "proj", "proj_copy", "bc_out", "dtp", "z", "relu",
                                                 "log", "dt", "dtu", "uD", "zt", "step")}
        w = lambda eng, n, value: eng.wait_ge(c[n].handle, c[n].at(value))
        col = lambda name, k: cols[:, COL_AT[name + str(layer)] + k:COL_AT[name + str(layer)] + k + 1]
        full, free = core.bank_full, core.bank_free
        dtu_out, uD_out, z_out = (core.stage_stored[2 * k:2 * k + 2] for k in range(3))
        dt_out = core.stage_stored[6:10]
        Z_FIRST, Z_MID = 4, range(8, 12)
        z_with = lambda m: Z_FIRST + m if m < 4 else Z_FIRST + len(Z_MID) + m
        outs = [("x", m, h) for m in range(IB) for h in range(2)] + [("z", t, f) for t in range(TT) for f in range(2)]
        USES = len(outs) // 4
        weights_in = [core.count(f"weights_in{n}") for n in range(4)]
        block = ctx.enter_context(nc.Block())

        @block.sync
        def _(sp):
            def load(it):
                sp.wait_ge(core.input_free[it % 2].handle, core.input_free[it % 2].at(it // 2))
                sp.dma_start(xT[it % 2][:], scr["xT"][it]).then_inc(core.input_in[it % 2].handle, 16)

            def store_z(it, o):
                _, t, f = outs[o]
                n = o - 2 * IB
                w(sp, "zt", it * 16 + (n + 1))
                sp.dma_start(scr["z"][it, t * P:(t + 1) * P, f * HALF:(f + 1) * HALF], zt[n % 2][:]
                             ).then_inc(z_out[n % 2].handle, 16)

            def load_weight(n, dst, src):
                sp.dma_start(dst[:], src).then_inc(weights_in[n].handle, 16)

            by_tile = lambda name: io[f"{name}{layer}"].rearrange("(k p) f -> p k f", p=P)
            load_weight(0, Wx, by_tile("in_wx"))
            load(0)
            load_weight(1, Wz, by_tile("in_wz"))
            load_weight(2, Wp, by_tile("x_w"))
            load_weight(3, Wdt, io[f"dt_w{layer}"])
            load(1)
            for it in range(B):
                for m in range(IB):
                    w(sp, "uD", it * IB + (m + 1))
                    sp.dma_start(scr["uD"][it, m], uD[m % 2][:]).then_inc(uD_out[m % 2].handle, 16)
                for n in range(Z_FIRST):
                    store_z(it, 2 * IB + n)
                w(sp, "proj_copy", it + 1)
                sp.dma_start(scr["bc"][it], xd[R:, :]).then_inc(c["bc_out"].handle, 16)
                for m in range(IB):
                    zs = {0: [z_with(k) for k in range(4)], 2: Z_MID, 4: [z_with(k) for k in range(4, 8)]}.get(m, ())
                    for n in zs:
                        store_z(it, 2 * IB + n)
                    w(sp, "dt", it * IB + (m + 1))
                    sp.dma_start(scr["dt"][it, m], dt[m % 4][:]).then_inc(dt_out[m % 4].handle, 16)
                    w(sp, "dtu", it * IB + (m + 1))
                    sp.dma_start(scr["dtu"][it, m], dtu[m % 2][:]).then_inc(dtu_out[m % 2].handle, 16)
                if it + 2 < B:
                    load(it + 2)
            for k in range(2):
                for stores, n in ((dtu_out, 64), (uD_out, 64), (z_out, 128)):
                    sp.wait_ge(stores[k].handle, stores[k].at(n * B))
            for k in range(4):
                sp.wait_ge(dt_out[k].handle, dt_out[k].at(32 * B))
            w(sp, "bc_out", 16 * B)

        @block.tensor
        def _(pe):
            def need(n):
                pe.wait_ge(weights_in[n].handle, weights_in[n].at(16))

            need(0)
            with pe.Fori(0, B // 2) as i:
                for j in range(2):
                    it = i * 2 + j

                    def product(o):
                        kind, a, h = outs[o]
                        pe.wait_ge(free[o % 4].handle, free[o % 4].at(it * USES + o // 4))
                        for kt in range(KT):
                            if kind == "x":
                                lhs, rhs = Wx[:, kt, a * P:(a + 1) * P], xT[j][:, kt, h * HALF:(h + 1) * HALF]
                            else:
                                lhs, rhs = xT[j][:, kt, a * P:(a + 1) * P], Wz[:, kt, h * HALF:(h + 1) * HALF]
                            last = nc.tensor.matmul(ring[o % 4][:], lhs, rhs, start=(kt == 0), stop=(kt == KT - 1))
                        last.then_inc(full[o % 4].handle, 1)

                    pe.wait_ge(core.input_in[j].handle, core.input_in[j].at(i * 16 + 16))
                    for o in range(2 * IB + Z_FIRST):
                        if j == 0 and o == 2 * IB:
                            need(1)
                        product(o)
                    if j == 0:
                        need(2)
                        need(3)
                    for m in range(IB):
                        w(pe, "u", it * IB + (m + 1))
                        for h in range(2):
                            last = nc.tensor.matmul(X[:, h * HALF:(h + 1) * HALF], Wp[:, m, :],
                                                    u[:, m, h * HALF:(h + 1) * HALF], start=(m == 0), stop=(m == IB - 1))
                    last.then_inc(c["proj"].handle, 1)
                    for m in range(IB):
                        if m == 4:
                            for n in Z_MID:
                                product(2 * IB + n)
                        product(2 * IB + z_with(m))
                        if m == 0:
                            w(pe, "proj_copy", it + 1)
                        if m >= 1:
                            w(pe, "z", it * IB + m)
                        for h in range(2):
                            last = nc.tensor.matmul(DTP[:, h * HALF:(h + 1) * HALF], Wdt[:, m * P:(m + 1) * P],
                                                    xd[0:R, h * HALF:(h + 1) * HALF], start=True, stop=True)
                        last.then_inc(c["dtp"].handle, 1)
                    w(pe, "z", it * IB + IB)
                    pe.sem_inc(core.input_free[j].handle, 1)

        @block.scalar
        def _(act):
            step = core.scalar_step
            with act.Fori(0, B // 2) as i:
                for j in range(2):
                    it = i * 2 + j

                    def take_z(n):
                        o = 2 * IB + n
                        act.wait_ge(full[o % 4].handle, full[o % 4].at(it * USES + (o // 4 + 1)))
                        act.wait_ge(z_out[n % 2].handle, z_out[n % 2].at(it * 128 + (n // 2) * 16))
                        nc.scalar.activation(zt[n % 2][:], ring[o % 4][:], ACT.Silu).then_inc(c["zt"].handle, 1)
                        w(act, "zt", it * 16 + (n + 1))
                        act.sem_inc(free[o % 4].handle, 1)

                    def take_x(m):
                        if m >= 2:
                            w(act, "conv", it * IB + (m - 1))
                        for h in range(2):
                            o = 2 * m + h
                            act.wait_ge(full[o % 4].handle, full[o % 4].at(it * USES + (o // 4 + 1)))
                            nc.scalar.copy(xp[m % 2][:, KC - 1 + h * HALF:KC - 1 + (h + 1) * HALF], ring[o % 4][:]
                                           ).then_inc(c["x_evac"].handle, 1)
                            w(act, "x_evac", it * (2 * IB) + (o + 1))
                            act.sem_inc(free[o % 4].handle, 1)

                    def make_u(m):
                        w(act, "conv", it * IB + (m + 1))
                        nc.scalar.activation(u[:, m], acc[m % 2][:], ACT.Silu, bias=col("conv_b", m)).then_inc(c["u"].handle, 1)
                        w(act, "u", it * IB + (m + 1))
                        act.wait_ge(uD_out[m % 2].handle, uD_out[m % 2].at(it * 64 + (m // 2) * 16))
                        nc.scalar.activation(uD[m % 2][:], u[:, m], ACT.Copy, scale=col("D", m)).then_inc(c["uD"].handle, 1)

                    for m in range(IB):
                        take_x(m)
                        if m >= 1:
                            make_u(m - 1)
                    make_u(IB - 1)
                    for n in range(Z_FIRST):
                        take_z(n)
                    w(act, "proj", it + 1)
                    act.wait_ge(core.bc_taken.handle, core.bc_taken.at(it))
                    nc.scalar.copy(xd[:], X[:]).then_inc(c["proj_copy"].handle, 1)
                    for group in (range(0, 4), range(4, 8)):
                        if group[0] == 4:
                            for n in Z_MID:
                                take_z(n)
                        for m in group:
                            take_z(z_with(m))
                            w(act, "relu", it * IB + (m + 1))
                            if m >= 4:
                                w(act, "dt", it * IB + (m - 3))
                            nc.scalar.activation(ea[m % 4][:], DTP[:], ACT.Abs, bias=col("dt_b", m)).then_inc(c["z"].handle, 1)
                        w(act, "z", it * IB + (group[-1] + 1))
                        for m in group:
                            nc.scalar.activation(ea[m % 4][:], ea[m % 4][:], ACT.Exp, scale=-1.0).then_inc(step.handle, 1)
                        act.wait_ge(step.handle, step.at(it * IB + (group[-1] + 1)))
                        for m in group:
                            nc.scalar.activation(ea[m % 4][:], ea[m % 4][:], ACT.Ln, bias=eps[:, 2:3]).then_inc(c["log"].handle, 1)
                    w(act, "dt", it * IB + IB)
                    w(act, "bc_out", it * 16 + 16)
                    act.sem_inc(core.bc_taken.handle, 1)

        @block.vector
        def _(dve):
            for k in range(2):
                last = nc.vector.memset(xp[k][:, 0:KC - 1], 0.0)
            last.then_inc(core.vector_step.handle, 1)
            dve.wait_ge(core.vector_step.handle, core.vector_step.at(1))
            with dve.Fori(0, B // 2) as i:
                for j in range(2):
                    it = i * 2 + j
                    for m in range(IB):
                        w(dve, "x_evac", it * (2 * IB) + (2 * m + 2))
                        if m >= 2:
                            w(dve, "u", it * IB + (m - 1))
                        a, at = acc[m % 2], COL_AT[f"conv_w{layer}"] + KC * m
                        nc.vector.tensor_scalar(a[:], xp[m % 2][:, 0:T], cols[:, at:at + 1], None, ALU.mult
                                                ).then_inc(c["step"].handle, 1)
                        for k in range(1, KC):
                            w(dve, "step", it * (3 * IB) + (m * 3 + k))
                            ins = nc.vector.scalar_tensor_tensor(out=a[:], in0=xp[m % 2][:, k:k + T],
                                                                 scalar=cols[:, at + k:at + k + 1], in1=a[:],
                                                                 op0=ALU.mult, op1=ALU.add)
                            ins.then_inc(c["step" if k < KC - 1 else "conv"].handle, 1)

                    def relu(m):
                        dve.wait_ge(dt_out[m % 4].handle, dt_out[m % 4].at(it * 32 + (m // 4) * 16))
                        w(dve, "dtp", it * IB + (m + 1))
                        nc.vector.tensor_scalar(dt[m % 4][:], DTP[:], col("dt_b", m), 0.0, ALU.add, ALU.max
                                                ).then_inc(c["relu"].handle, 1)

                    def finish_dt(m):
                        w(dve, "relu", it * IB + (m + 1))
                        w(dve, "log", it * IB + (m + 1))
                        nc.vector.tensor_tensor(dt[m % 4][:], dt[m % 4][:], ea[m % 4][:], ALU.add).then_inc(c["dt"].handle, 1)
                        w(dve, "dt", it * IB + (m + 1))
                        dve.wait_ge(dtu_out[m % 2].handle, dtu_out[m % 2].at(it * 64 + (m // 2) * 16))
                        nc.vector.tensor_tensor(dtu[m % 2][:], dt[m % 4][:], u[:, m], ALU.mult).then_inc(c["dtu"].handle, 1)

                    for m in range(4):
                        relu(m)
                    finish_dt(0)
                    finish_dt(1)
                    relu(4)
                    finish_dt(2)
                    finish_dt(3)
                    for m in range(5, 8):
                        relu(m)
                    for m in range(4, 8):
                        finish_dt(m)

    for cc in weights_in:
        cc.stage_added(16)
    core.vector_step.stage_added(1)
    core.scalar_step.stage_added(IB * B)
    core.bc_taken.stage_added(B)
    for k in range(2):
        core.input_in[k].stage_added(16 * B // 2)
        core.input_free[k].stage_added(B // 2)
        for stores, n in ((dtu_out, 64), (uD_out, 64), (z_out, 128)):
            stores[k].stage_added(n * B)
    for k in range(4):
        dt_out[k].stage_added(32 * B)
        full[k].stage_added(USES * B)
        free[k].stage_added(USES * B)
    for n, per in (("x_evac", 2 * IB), ("conv", IB), ("u", IB), ("proj", 1), ("proj_copy", 1), ("bc_out", 16), ("dtp", IB),
                   ("z", IB), ("relu", IB), ("log", IB), ("dt", IB), ("dtu", IB), ("uD", IB), ("zt", 2 * TT), ("step", 3 * IB)):
        c[n].stage_added(per * B)


def scan(core, ident, scr, layer):
    nc = core.nc
    with ExitStack() as ctx:
        sb, psum = allocator(nc, ctx, f"scan{layer}")
        Brep = sb("Brep", [P, NS, T])
        Crep = sb("Crep", [P, NS, T])
        two = lambda n, shape: [sb(f"{n}{k}", shape) for k in range(2)]
        dt, dtu, uD, A = two("dt", [P, T]), two("dtu", [P, T]), two("uD", [P, T]), two("A", [P, NS + 1])
        z, g, hC = two("z", [P, TT, P]), two("g", [P, TT, P]), two("hC", [P, T])
        DR = 4
        drive = [sb(f"drive{k}", [P, T]) for k in range(DR)]
        dAh = [psum(f"dAh{k}", [P, T]) for k in range(2)]
        yT = [psum(f"yT{k}", [P, TT, P]) for k in range(2)]
        scanned, scaled, turned, gated = core.scanned, core.scaled, core.unit_turned, core.gated
        decayed, driven = core.count("decayed"), core.count("driven")
        y_full = core.count("scan_y_full")
        in_, in_free = core.input_in, core.input_free
        PAIRS = IB // 2
        IN = 5 * 16
        g_rows = scr["g"].rearrange("b m p k d -> (b m) p k d")
        block = ctx.enter_context(nc.Block())

        @block.sync
        def _(sp):
            def load(b, m, j, use):
                sp.wait_ge(in_free[j].handle, in_free[j].at(use))
                core.apart(sp)
                for dst, src in ((dt[j][:], scr["dt"][b, m]), (dtu[j][:], scr["dtu"][b, m]),
                                 (A[j][:], scr["A"][layer - 2][m]), (uD[j][:], scr["uD"][b, m]),
                                 (z[j][:], scr["z"][b, :, bass.ds(m * P, P)].rearrange("(k p) d -> p k d", p=P))):
                    sp.dma_start(dst, src).then_inc(in_[j].handle, 16)

            with sp.Fori(0, B) as b:
                load(b, 0, 0, b * PAIRS)
                for n in range(NS):
                    sp.wait_ge(scaled.handle, scaled.at(b * (IB * NS) + (n + 1 - NS)))
                    core.apart(sp)
                    sp.dma_start(Brep[:, n, :], scr["bc"][b, n:n + 1, :].broadcast_to([P, T])).then_inc(core.replica_in[n].handle, 16)
                    sp.dma_start(Crep[:, n, :], scr["bc"][b, NS + n:NS + n + 1, :].broadcast_to([P, T])
                                 ).then_inc(core.replica_in[n].handle, 16)
                load(b, 1, 1, b * PAIRS)
                with sp.Fori(1, PAIRS) as i:
                    for j in range(2):
                        load(b, i * 2 + j, j, b * PAIRS + i)

        @block.scalar
        def _(act):
            def store(pair, j):
                act.wait_ge(gated.handle, gated.at(pair * 2 + (j + 1)))
                act.dma_start(g_rows[pair * 2 + j], g[j][:]).then_inc(core.g_stored[j].handle, 16)

            def blocks(pair, first):
                for j in range(2):
                    act.wait_ge(in_[j].handle, in_[j].at(pair * IN + IN))
                    for n in range(NS):
                        k = (pair * 2 + j) * NS + n
                        act.wait_ge(scaled.handle, scaled.at(k - 1))
                        nc.scalar.activation(dAh[n % 2][:], dt[j][:], ACT.Exp, scale=A[j][:, n:n + 1]
                                             ).then_inc(decayed.handle, 1)
                        if n == 6 and not (first and j == 0):
                            store(pair if j == 1 else pair - 1, 1 - j)

            with act.Fori(0, B) as b:
                blocks(b * PAIRS, True)
                with act.Fori(1, PAIRS) as i:
                    blocks(b * PAIRS + i, False)
                store(b * PAIRS + (PAIRS - 1), 1)
            for j in range(2):
                act.wait_ge(core.g_stored[j].handle, core.g_stored[j].at(16 * B * PAIRS))

        @block.gpsimd
        def _(pool):
            with pool.Fori(0, B) as b:
                core.apart(pool)
                with pool.Fori(0, PAIRS) as i:
                    pair = b * PAIRS + i
                    for j in range(2):
                        pool.wait_ge(in_[j].handle, in_[j].at(pair * IN + IN))
                        for n in range(NS):
                            k = (pair * 2 + j) * NS + n
                            pool.wait_ge(core.replica_in[n].handle, core.replica_in[n].at(b * 32 + 32))
                            pool.wait_ge(scanned.handle, scanned.at(k + 1 - DR))
                            nc.gpsimd.tensor_tensor(drive[n % DR][:], dtu[j][:], Brep[:, n, :], ALU.mult
                                                    ).then_inc(driven.handle, 1)

        @block.vector
        def _(dve):
            def gate(pair, j):
                dve.wait_ge(y_full.handle, y_full.at(pair * 2 + (j + 1)))
                dve.wait_ge(core.g_stored[j].handle, core.g_stored[j].at(pair * 16))
                nc.vector.tensor_tensor(g[j][:], yT[j][:], z[j][:], ALU.mult).then_inc(gated.handle, 1)
                dve.wait_ge(gated.handle, gated.at(pair * 2 + (j + 1)))
                dve.sem_inc(in_free[j].handle, 1)

            def blocks(b, pair, first):
                for j in range(2):
                    dve.wait_ge(in_[j].handle, in_[j].at(pair * IN + IN))
                    for n in range(NS):
                        k = (pair * 2 + j) * NS + n
                        dve.wait_ge(core.replica_in[n].handle, core.replica_in[n].at(b * 32 + 32))
                        dve.wait_ge(decayed.handle, decayed.at(k + 1))
                        dve.wait_ge(driven.handle, driven.at(k + 1))
                        nc.vector.tensor_tensor_scan(dAh[n % 2][:], dAh[n % 2][:], drive[n % DR][:], 0.0,
                                                     ALU.mult, ALU.add).then_inc(scanned.handle, 1)
                        dve.wait_ge(scanned.handle, scanned.at(k + 1))
                        dve.wait_ge(turned.handle, turned.at(k - 1))
                        nc.vector.tensor_tensor(hC[n % 2][:], dAh[n % 2][:], Crep[:, n, :], ALU.mult
                                                ).then_inc(scaled.handle, 1)
                        if n == 2 and not (first and j == 0):
                            gate(pair if j == 1 else pair - 1, 1 - j)

            with dve.Fori(0, B) as b:
                blocks(b, b * PAIRS, True)
                core.apart(dve)
                with dve.Fori(1, PAIRS) as i:
                    blocks(b, b * PAIRS + i, False)
                gate(b * PAIRS + (PAIRS - 1), 1)

        @block.tensor
        def _(pe):
            with pe.Fori(0, B * PAIRS) as pair:
                for j in range(2):
                    pe.wait_ge(gated.handle, gated.at(pair * 2 + (j - 1)))
                    pe.wait_ge(in_[j].handle, in_[j].at(pair * IN + IN))
                    for n in range(NS + 1):
                        if n < NS:
                            pe.wait_ge(scaled.handle, scaled.at((pair * 2 + j) * NS + (n + 1)))
                        src = hC[n % 2] if n < NS else uD[j]
                        for t in range(TT):
                            last = nc.tensor.matmul(yT[j][:, t, :], src[:, t * P:(t + 1) * P], ident[:],
                                                    start=(n == 0 and t % 4 == 0), stop=(n == NS), is_transpose=True,
                                                    skip_group_check=True)
                        last.then_inc((turned if n < NS else y_full).handle, 1)

    units = B * IB * NS
    for cc in (scanned, scaled, turned, decayed, driven):
        cc.stage_added(units)
    for cc in (gated, y_full):
        cc.stage_added(B * IB)
    for j in range(2):
        in_[j].stage_added(IN * B * PAIRS)
        in_free[j].stage_added(B * PAIRS)
        core.g_stored[j].stage_added(16 * B * PAIRS)
    for n in range(NS):
        core.replica_in[n].stage_added(32 * B)


def ssm_output(core, ident, io, scr, layer, residual, dst):
    nc = core.nc
    with ExitStack() as ctx:
        sb, psum = allocator(nc, ctx, f"ssmout{layer}")
        Wo = sb("Wo", [P, IB, D])
        four = lambda n, shape: [sb(f"{n}{k}", shape) for k in range(4)]
        g, gT, x, out = four("g", [P, IB, P]), four("gT", [P, IB, P]), four("x", [P, D]), four("out", [P, D])
        gt = [sb(f"gt{k}", [P, D]) for k in range(2)]
        TP = [psum(f"TP{k}", [P, IB, P]) for k in range(2)]
        O = [psum(f"O{k}", [P, D]) for k in range(4)]
        c = {n: core.count("out_" + n) for n in ("turn", "copy", "mm", "step", "done")}
        gate_in = core.slot_in[0:2]
        w = lambda eng, n, value: eng.wait_ge(c[n].handle, c[n].at(value))
        n_in = 16 if residual is None else 32
        QUADS = B * TT // 4
        block = ctx.enter_context(nc.Block())

        @block.sync
        def _(sp):
            sp.dma_start(Wo[:], io[f"out_w{layer}"].rearrange("(k p) f -> p k f", p=P)).then_inc(core.consts_in.handle, 16)
            with sp.Fori(0, B // 2) as i:
                for jb in range(2):
                    b = i * 2 + jb
                    sp.wait_ge(core.gate_free[jb].handle, core.gate_free[jb].at(i))
                    sp.dma_start(gt[jb][:], scr["gate"][layer - 2, bass.ds(b, 1), :].broadcast_to([P, D])
                                 ).then_inc(gate_in[jb].handle, 16)
                    for t in range(TT):
                        j, quad = t % 4, b * 2 + t // 4
                        sp.wait_ge(core.input_free[j].handle, core.input_free[j].at(quad))
                        core.apart(sp)
                        sp.dma_start(g[j][:], scr["g"][b, :, :, t, :].rearrange("m p d -> p m d")
                                     ).then_inc(core.input_in[j].handle, 16)
                        if residual is not None:
                            sp.dma_start(x[j][:], residual[b, t * P:(t + 1) * P, :]).then_inc(core.input_in[j].handle, 16)

        @block.tensor
        def _(pe):
            pe.wait_ge(core.consts_in.handle, core.consts_in.at(16))
            with pe.Fori(0, QUADS) as quad:
                def turn(j):
                    pe.wait_ge(core.input_in[j].handle, core.input_in[j].at(quad * n_in + n_in))
                    pe.wait_ge(core.bank_free[j % 2].handle, core.bank_free[j % 2].at(quad * 2 + j // 2))
                    for m in range(IB):
                        last = nc.tensor.transpose(TP[j % 2][:, m, :], g[j][:, m, :], ident[:])
                    last.then_inc(c["turn"].handle, 1)

                def product(j):
                    w(pe, "copy", quad * 4 + (j + 1))
                    pe.wait_ge(core.input_free[j].handle, core.input_free[j].at(quad))
                    for m in range(IB):
                        last = nc.tensor.matmul(O[j][:], gT[j][:, m, :], Wo[:, m, :], start=(m == 0), stop=(m == IB - 1))
                    last.then_inc(c["mm"].handle, 1)

                turn(0)
                for j in range(4):
                    if j < 3:
                        turn(j + 1)
                    product(j)

        @block.scalar
        def _(act):
            with act.Fori(0, QUADS) as quad:
                def store(j):
                    w(act, "done", quad * 4 + (j + 1))
                    act.dma_start(dst.rearrange("b t d -> (b t) d")[bass.ds((quad * 4 + j) * P, P), :], out[j][:]
                                  ).then_inc(core.stage_stored[j].handle, 16)

                for j in range(4):
                    w(act, "turn", quad * 4 + (j + 1))
                    act.wait_ge(core.input_free[j].handle, core.input_free[j].at(quad))
                    nc.scalar.copy(gT[j][:], TP[j % 2][:]).then_inc(c["copy"].handle, 1)
                    w(act, "copy", quad * 4 + (j + 1))
                    act.sem_inc(core.bank_free[j % 2].handle, 1)
                    if j >= 2:
                        store(j - 2)
                store(2)
                store(3)
            for j in range(4):
                act.wait_ge(core.stage_stored[j].handle, core.stage_stored[j].at(16 * QUADS))

        @block.vector
        def _(dve):
            with dve.Fori(0, B // 2) as i:
                for jb in range(2):
                    dve.wait_ge(gate_in[jb].handle, gate_in[jb].at(i * 16 + 16))
                    for t in range(TT):
                        j, quad, tile = t % 4, (i * 2 + jb) * 2 + t // 4, (i * 2 + jb) * TT + t
                        w(dve, "mm", tile + 1)
                        dve.wait_ge(core.stage_stored[j].handle, core.stage_stored[j].at(quad * 16))
                        ins = nc.vector.tensor_tensor(out[j][:], O[j][:], gt[jb][:], ALU.mult)
                        if residual is not None:
                            ins.then_inc(c["step"].handle, 1)
                            w(dve, "step", tile + 1)
                            ins = nc.vector.tensor_tensor(out[j][:], out[j][:], x[j][:], ALU.add)
                        ins.then_inc(c["done"].handle, 1)
                        w(dve, "done", tile + 1)
                        dve.sem_inc(core.input_free[j].handle, 1)
                    dve.sem_inc(core.gate_free[jb].handle, 1)

    core.consts_in.stage_added(16)
    for j in range(4):
        core.input_in[j].stage_added(n_in * QUADS)
        core.input_free[j].stage_added(QUADS)
        core.stage_stored[j].stage_added(16 * QUADS)
    for j in range(2):
        core.bank_free[j].stage_added(2 * QUADS)
        core.gate_free[j].stage_added(B // 2)
        gate_in[j].stage_added(16 * B // 2)
    for n in ("turn", "copy", "mm", "done"):
        c[n].stage_added(4 * QUADS)
    if residual is not None:
        c["step"].stage_added(4 * QUADS)


def gather_add(core, io, src, residual, dst):
    nc = core.nc
    with ExitStack() as ctx:
        sb, psum = allocator(nc, ctx, "gather")
        idx = sb("idx", [P, TT], I32)
        idx_b = sb("idx_b", [P, B, TT], I32)
        two = lambda n, shape: [sb(f"{n}{k}", shape) for k in range(2)]
        y, x = two("y", [P, TT, D]), two("x", [P, TT, D])
        idx_done, added = core.count("idx_done"), core.count("gather_added")
        rows_in = [core.count(f"gather_rows_in{k}") for k in range(2)]
        block = ctx.enter_context(nc.Block())

        @block.sync
        def _(sp):
            sp.dma_start(idx[:], io["perm"]).then_inc(core.consts_in.handle, 16)
            for b in range(B):
                sp.wait_ge(core.input_free[b % 2].handle, core.input_free[b % 2].at(b // 2))
                sp.dma_start(x[b % 2][:], residual[b].rearrange("(k p) d -> p k d", p=P)
                             ).then_inc(core.slot_in[b % 2].handle, 16)

        @block.gpsimd
        def _(pool):
            pool.wait_ge(idx_done.handle, idx_done.at(1))
            for b in range(B):
                pool.wait_ge(core.input_free[b % 2].handle, core.input_free[b % 2].at(b // 2))
                for k in range(TT):
                    pool.indirect_dma_start(y[b % 2][:, k, :], None, src.rearrange("b t d -> (b t) d"),
                                            bass.IndirectOffsetOnAxis(ap=idx_b[:, b, k:k + 1], axis=0)
                                            ).then_inc(rows_in[b % 2].handle, 16)

        @block.vector
        def _(dve):
            dve.wait_ge(core.consts_in.handle, core.consts_in.at(16))
            for b in range(B):
                last = nc.vector.tensor_scalar(idx_b[:, b, :], idx[:], float(b * T), None, ALU.add)
            last.then_inc(idx_done.handle, 1)
            for b in range(B):
                dve.wait_ge(rows_in[b % 2].handle, rows_in[b % 2].at((b // 2 + 1) * 16 * TT))
                dve.wait_ge(core.slot_in[b % 2].handle, core.slot_in[b % 2].at((b // 2 + 1) * 16))
                nc.vector.tensor_tensor(x[b % 2][:], x[b % 2][:], y[b % 2][:], ALU.add).then_inc(added.handle, 1)

        @block.scalar
        def _(act):
            for b in range(B):
                act.wait_ge(added.handle, added.at(b + 1))
                act.dma_start(dst[b].rearrange("(k p) d -> p k d", p=P), x[b % 2][:]
                              ).then_inc(core.stage_stored[b % 2].handle, 16)
                act.wait_ge(core.stage_stored[b % 2].handle, core.stage_stored[b % 2].at((b // 2 + 1) * 16))
                act.sem_inc(core.input_free[b % 2].handle, 1)


LAYERS = 4


def program(nc, io, out, kind="Internal"):
    scr = {}
    for name, shape in (("tab", [TABS, B, P, 8]), ("gate", [2, B, D]), ("keep", [2, B, P, TT]), ("A", [2, IB, P, NS + 1]),
                        ("xT", [B, P, KT, T]), ("q_split", [B, 2, D, T]), ("k_split", [B, 2, D, T]),
                        ("v_split", [B, T, 2 * D]), ("kT", [B, P, KT, T]), ("q", [B, T, D]),
                        ("v", [B, T, D]), ("y", [B, T, D]), ("x1", [B, T, D]), ("x2", [B, T, D]), ("x3", [B, T, D]),
                        ("z", [B, T, DI]), ("uD", [B, IB, P, T]), ("dtu", [B, IB, P, T]), ("dt", [B, IB, P, T]),
                        ("bc", [B, 2 * NS, T]), ("g", [B, IB, P, TT, P])):
        scr[name] = nc.dram_tensor(f"scratch_{name}", shape, F32, kind=kind).ap()
    with ExitStack() as ctx:
        core = Core(nc, ctx)
        ident = ctx.enter_context(nc.sbuf_tensor("ident", [P, P], F32))
        eps = ctx.enter_context(nc.sbuf_tensor("eps", [P, 4], F32))
        cols = ctx.enter_context(nc.sbuf_tensor("column_tables", [P, NCOL], F32))
        give_credits(core, ident, eps)
        modulation(core, ident, io, scr, cols)
        tab = scr["tab"]

        normalize(core, "n0", ident, eps, io["x"], tab[0], ACT.Identity, scr["xT"])
        project(core, "p0", io, cols, scr["xT"], [
            dict(kind="T", w=io["q_w"], n=D, col="q_b", dst=scr["q_split"], split=True),
            dict(kind="T", w=io["k_w"], n=D, col="k_b", dst=scr["k_split"], split=True),
            dict(kind="N", w=io["v_w"], n=D, row=0, keep=scr["keep"][0], dst=scr["v_split"], split=True)])
        attention(core, ident, io, scr)
        normalize(core, "n1", ident, eps, scr["y"], tab[1], ACT.Silu, scr["xT"])
        project(core, "p1", io, cols, scr["xT"], [
            dict(kind="N", w=io["out_w"], n=D, row=1, residual=io["x"], dst=scr["x1"])])

        normalize(core, "n2", ident, eps, scr["x1"], tab[2], ACT.Identity, scr["xT"])
        project(core, "p2", io, cols, scr["xT"], [
            dict(kind="T", w=io["Wk"], n=D, col="bk", dst=scr["kT"]),
            dict(kind="N", w=io["Wq"], n=D, row=2, dst=scr["q"]),
            dict(kind="N", w=io["Wv"], n=D, row=3, keep=scr["keep"][1], dst=scr["v"])])
        linear_attention(core, ident, io, scr)
        normalize(core, "n3", ident, eps, scr["y"], tab[3], ACT.Silu, scr["xT"])
        project(core, "p3", io, cols, scr["xT"], [
            dict(kind="N", w=io["film_out_W"], n=D, row=4, residual=scr["x1"], dst=scr["x2"])])

        for layer, x_in in ((2, scr["x2"]), (3, scr["x3"])):
            normalize(core, f"n{layer + 2}", ident, eps, x_in, tab[layer + 2], ACT.Identity, scr["xT"],
                      gather=io["perm"] if layer == 3 else None)
            ssm_inputs(core, cols, eps, io, scr, layer)
            scan(core, ident, scr, layer)
            if layer == 2:
                ssm_output(core, ident, io, scr, layer, scr["x2"], scr["x3"])
            else:
                ssm_output(core, ident, io, scr, layer, None, scr["y"])
        gather_add(core, io, scr["y"], scr["x3"], out)


def kernel(**inputs):
    import concourse.bacc as bacc
    from concourse.bass_utils import run_bass_kernel_spmd as run

    a = {k: np.asarray(v) for k, v in inputs.items()}
    l0 = {k[8:]: v for k, v in a.items() if k.startswith("L0_cond_")}
    l1 = {k[8:]: v for k, v in a.items() if k.startswith("L1_cond_")}
    l2 = {k[8:]: v for k, v in a.items() if k.startswith("L2_cond_")}
    l3 = {k[8:]: v for k, v in a.items() if k.startswith("L3_cond_")}

    def columns(v):
        return v.reshape(-1, P).T

    def tile_columns(v):
        return v.reshape(-1, P, v.shape[-1]).transpose(1, 0, 2).reshape(P, -1)

    col = dict(q_b=l0["q_b"], k_b=l0["k_b"], bk=l1["bk"], norm_w0=l0["norm_w"], norm_b0=l0["norm_b"],
               sb_w=l0["sb_norm_w"], sb_b=l0["sb_norm_b"], emb_b0=l0["emb_b"],
               norm_w1=l1["norm_scale"], norm_b1=l1["norm_bias"], film_w=l1["film_norm_scale"],
               film_b=l1["film_norm_bias"], emb_b1=l1["film_emb_b"],
               ln_g2=l2["ln_g"], ln_b2=l2["ln_b"], ada_b2=l2["ada_b"][:2 * D],
               ln_g3=l3["gamma"], ln_b3=l3["beta"], ada_b3=l3["b_ada"][:2 * D],
               conv_b2=l2["conv_b"], dt_b2=l2["dt_proj_b"], D2=l2["D_param"],
               conv_b3=l3["conv_b"], dt_b3=l3["b_dt"], D3=l3["D_param"])
    col = {k: columns(v) for k, v in col.items()}
    col.update(conv_w2=tile_columns(l2["conv_w"]), A_log2=tile_columns(l2["A_log"]),
               conv_w3=tile_columns(l3["conv_w"].reshape(DI, KC)), A_log3=tile_columns(l3["A_log"]))
    arrays = {
        "x": a["x"],
        "cols": np.concatenate([col[n] for n, _ in COLS], axis=1),
        "rows": np.stack([l0["v_b"], l0["out_b"], l1["bq"], l1["bv"], l1["film_out_b"],
                          l2["ada_b"][2 * D:], l3["b_ada"][2 * D:]]),
        "condT": a["cond_2048"].T,
        "mask0": a["mask_BxS_ff1"], "mask1": a["mask_BxS_ik0"],
        "mask0_cols": a["mask_BxS_ff1"].reshape(B, TT, P).transpose(2, 0, 1),
        "mask1_cols": a["mask_BxS_ik0"].reshape(B, TT, P).transpose(2, 0, 1),
        "perm": a["itok_S_0_1023"].reshape(TT, P).T,
        "emb_w0": l0["emb_w"], "emb_w1": l1["film_emb_W"], "ada_w2": l2["ada_w"].T, "ada_w3": l3["W_ada"],
        "q_w": l0["q_w"], "k_w": l0["k_w"], "v_w": l0["v_w"], "out_w": l0["out_w"],
        "Wq": l1["Wq"], "Wk": l1["Wk"], "Wv": l1["Wv"], "film_out_W": l1["film_out_W"],
        "in_wx2": l2["in_proj_w"][:DI].T, "in_wz2": l2["in_proj_w"][DI:].T,
        "in_wx3": l3["W_in"][:, :DI], "in_wz3": l3["W_in"][:, DI:],
        "x_w2": l2["x_proj_w"].T, "x_w3": l3["W_xp"], "dt_w2": l2["dt_proj_w"].T, "dt_w3": l3["W_dt"],
        "out_w2": l2["out_proj_w"].T, "out_w3": l3["W_out"],
    }
    arrays = {k: np.ascontiguousarray(v) for k, v in arrays.items()}
    nc = bacc.Bacc("TRN2", target_bir_lowering=False, num_devices=1)
    io = {k: nc.dram_tensor(k, v.shape, mybir.dt.from_np(v.dtype), kind="ExternalInput").ap() for k, v in arrays.items()}
    out = nc.dram_tensor("out", (B, T, D), F32, kind="ExternalOutput").ap()
    program(nc, io, out)
    return run(nc, [arrays], core_ids=[0]).results[0]["out"]
```
